# Optimizing a Trainium2 kernel written in Bass

```python
import numpy as np
import jax
import jax.numpy as jnp

def _softmax(x, axis=-1):
    return jax.nn.softmax(x, axis=axis)

def _gelu(x):
    return jax.nn.gelu(x, approximate=True)

def _silu(x):
    return jax.nn.silu(x)

def _sigmoid(x):
    return jax.nn.sigmoid(x)

def _layernorm(x, axis=-1, eps=1e-05):
    m = jnp.mean(x, axis=axis, keepdims=True)
    v = jnp.var(x, axis=axis, keepdims=True)
    return (x - m) / jnp.sqrt(v + eps)

def _scatter_add(tgt, idx, src, axis=0):
    return tgt.at[idx].add(src)

def _segment_sum(src, seg, n):
    return jax.ops.segment_sum(src, seg, n)
kernel_name = 'mk_gnn_resnorm_d4_gnn_r32_8ccc69'

def setup_inputs(seed: int=0):
    np.random.seed(seed)
    _w = jnp.asarray

    def _rec_inputs():
        import jax
        import jax.numpy as jnp
        _gk = jax.random.key(seed)
        x = -0.000125 + 0.9999 * jax.random.normal(jax.random.fold_in(_gk, 1), (2048, 512), jnp.float32)
        src = jax.random.randint(jax.random.fold_in(_gk, 2), (32768,), 0, 2048, jnp.int32)
        dst = jax.random.randint(jax.random.fold_in(_gk, 3), (32768,), 0, 2048, jnp.int32)
        _o = jnp.argsort(dst, stable=True)
        src = src[_o]
        dst = dst[_o]
        edge_attr_4 = 0.00171547 + 0.999346 * jax.random.normal(jax.random.fold_in(_gk, 13), (32768, 4), jnp.float32)
        edge_attr_64 = -5.3897e-05 + 0.999841 * jax.random.normal(jax.random.fold_in(_gk, 14), (32768, 64), jnp.float32)
        edge_attr_8 = 0.000126197 + 0.999763 * jax.random.normal(jax.random.fold_in(_gk, 15), (32768, 8), jnp.float32)
        edge_weight = jax.random.uniform(jax.random.fold_in(_gk, 17), (32768,), jnp.float32, 0.0, 0.999998)
        return (x, src, dst, edge_attr_4, edge_attr_64, edge_attr_8, edge_weight)
    x, src, dst, edge_attr_4, edge_attr_64, edge_attr_8, edge_weight = _rec_inputs()

    def _L0_gnn_setup():
        import jax, jax.numpy as jnp
        import numpy as np
        N_NODES = 2048
        N_EDGES = 16384
        FEAT_DIM = 512
        EMBED_DIM = 512
        key = jax.random.key(seed)
        k1, k2, k3, k4, k5 = jax.random.split(key, 5)
        x = jax.random.normal(k1, (N_NODES, FEAT_DIM), dtype=jnp.float32)
        limit = float(np.sqrt(6.0 / (EMBED_DIM + FEAT_DIM)))
        weight = jax.random.uniform(k2, (EMBED_DIM, FEAT_DIM), dtype=jnp.float32, minval=-limit, maxval=limit)
        row = jax.random.randint(k3, (N_EDGES,), 0, N_NODES, dtype=jnp.int64)
        col = jax.random.randint(k4, (N_EDGES,), 0, N_NODES, dtype=jnp.int64)
        vals = jax.random.uniform(k5, (N_EDGES,), dtype=jnp.float32)
        return {'x': x, 'weight': weight, 'row': row, 'col': col, 'vals': vals}
    _L0_gnn_all = _L0_gnn_setup()
    _L0_gnn_in = {k: v for k, v in _L0_gnn_all.items() if k in ('weight',)}
    del _L0_gnn_all

    def _L1_gnn_setup():
        import jax, jax.numpy as jnp
        import numpy as np
        N, E, H, ED = (50000, 12500, 512, 64)
        BN_EPS = 1e-05

        def _bn(h, g, b):
            mu = jnp.mean(h, axis=0)
            var = jnp.mean(jnp.square(h - mu), axis=0)
            return (h - mu) * jax.lax.rsqrt(var + BN_EPS) * g + b
        key = jax.random.key(seed)
        ks = jax.random.split(key, 8)
        s = lambda d: 1.0 / np.sqrt(d)
        return {'x': jax.random.normal(ks[0], (N, H), jnp.float32), 'edge_attr': jax.random.normal(ks[1], (E, ED), jnp.float32), 'edge_index': jax.random.randint(ks[2], (2, E), 0, N, jnp.int32), 'W_e': jax.random.normal(ks[3], (ED, H), jnp.float32) * s(ED), 'b_e': jnp.zeros((H,), jnp.float32), 'W1': jax.random.normal(ks[4], (H, 2 * H), jnp.float32) * s(H), 'b1': jnp.zeros((2 * H,), jnp.float32), 'g1': jnp.ones((2 * H,), jnp.float32), 'beta1': jnp.zeros((2 * H,), jnp.float32), 'W2': jax.random.normal(ks[5], (2 * H, H), jnp.float32) * s(2 * H), 'b2': jnp.zeros((H,), jnp.float32), 'g2': jnp.ones((H,), jnp.float32), 'beta2': jnp.zeros((H,), jnp.float32), 'eps': jnp.zeros((), jnp.float32)}
    _L1_gnn_all = _L1_gnn_setup()
    _L1_gnn_in = {k: v for k, v in _L1_gnn_all.items() if k in ('W_e', 'b_e', 'W1', 'b1', 'g1', 'beta1', 'W2', 'b2', 'g2', 'beta2', 'eps')}
    del _L1_gnn_all

    def _L2_gnn_setup():
        import jax, jax.numpy as jnp
        import numpy as np
        MUL = 128
        N_NODES = 10000
        N_EDGES = 5000
        R_BASIS = 8
        HIDDEN = 64
        W_NUMEL = 4 * MUL
        SQRT3 = 3.0 ** 0.5
        SILU_2MOM = 1.679177
        AVG_NUM_NEIGHBORS = 10.0

        def _lin_irreps(x0, x1, W0, W1):
            y0 = x0 @ W0 / jnp.sqrt(jnp.float32(W0.shape[0]))
            y1 = jnp.einsum('num,uv->nvm', x1, W1) / jnp.sqrt(jnp.float32(W1.shape[0]))
            return (y0, y1)

        def _forward(node_feats, edge_attrs, edge_feats, edge_index, W_up0, W_up1, W_mlp1, W_mlp2, W_mlp3, W_mlp4, W_out0, W_out1):
            num_nodes = node_feats.shape[0]
            sender, receiver = (edge_index[0], edge_index[1])
            x0 = node_feats[:, :MUL]
            x1 = node_feats[:, MUL:].reshape(num_nodes, MUL, 3)
            x0, x1 = _lin_irreps(x0, x1, W_up0, W_up1)
            h = edge_feats
            for W in (W_mlp1, W_mlp2, W_mlp3):
                h = SILU_2MOM * jax.nn.silu(h @ W / jnp.sqrt(jnp.float32(W.shape[0])))
            tpw = h @ W_mlp4 / jnp.sqrt(jnp.float32(W_mlp4.shape[0]))
            w1, w2, w3, w4 = jnp.split(tpw, 4, axis=-1)
            s0 = x0[sender]
            s1 = x1[sender]
            y0 = edge_attrs[:, 0:1]
            y1 = edge_attrs[:, 1:4]
            p1 = w1 * s0 * y0
            p2 = (w2 * s0)[:, :, None] * y1[:, None, :]
            p3 = w3[:, :, None] * s1 * y0[:, None, :]
            p4 = w4 * jnp.einsum('eum,em->eu', s1, y1) / SQRT3
            m0 = jnp.concatenate([p1, p4], axis=-1)
            m1 = jnp.concatenate([p2, p3], axis=1)
            msg0 = jax.ops.segment_sum(m0, receiver, num_segments=num_nodes)
            msg1 = jax.ops.segment_sum(m1, receiver, num_segments=num_nodes)
            o0, o1 = _lin_irreps(msg0, msg1, W_out0, W_out1)
            out = jnp.concatenate([o0, o1.reshape(num_nodes, 3 * MUL)], axis=-1)
            return out / AVG_NUM_NEIGHBORS
        key = jax.random.key(seed)
        ks = jax.random.split(key, 12)
        rn = lambda k, s: jax.random.normal(k, s, dtype=jnp.float32)
        return {'node_feats': rn(ks[0], (N_NODES, 4 * MUL)), 'edge_attrs': rn(ks[1], (N_EDGES, 4)), 'edge_feats': rn(ks[2], (N_EDGES, R_BASIS)), 'edge_index': jax.random.randint(ks[3], (2, N_EDGES), 0, N_NODES), 'W_up0': rn(ks[4], (MUL, MUL)), 'W_up1': rn(ks[5], (MUL, MUL)), 'W_mlp1': rn(ks[6], (R_BASIS, HIDDEN)), 'W_mlp2': rn(ks[7], (HIDDEN, HIDDEN)), 'W_mlp3': rn(ks[8], (HIDDEN, HIDDEN)), 'W_mlp4': rn(ks[9], (HIDDEN, W_NUMEL)), 'W_out0': rn(ks[10], (2 * MUL, MUL)), 'W_out1': rn(ks[11], (2 * MUL, MUL))}
    _L2_gnn_all = _L2_gnn_setup()
    _L2_gnn_in = {k: v for k, v in _L2_gnn_all.items() if k in ('W_up0', 'W_up1', 'W_mlp1', 'W_mlp2', 'W_mlp3', 'W_mlp4', 'W_out0', 'W_out1')}
    del _L2_gnn_all

    def _L3_gnn_setup():
        import jax, jax.numpy as jnp
        import numpy as np
        N_NODES = 10000
        N_EDGES = 5000
        IN_DIM = 512
        OUT_DIM = 512
        LN_EPS = 1e-05
        key = jax.random.key(seed)
        k_x, k_src, k_ws, k_wn = jax.random.split(key, 4)
        x = jax.random.normal(k_x, (N_NODES, IN_DIM), dtype=jnp.float32)
        edge_src = jax.random.randint(k_src, (N_EDGES,), 0, N_NODES, dtype=jnp.int32)
        edge_dst = jnp.repeat(jnp.arange(N_NODES, dtype=jnp.int32), N_EDGES // N_NODES)
        deg = jnp.full((N_NODES,), float(N_EDGES // N_NODES), dtype=jnp.float32)
        scale = 1.0 / np.sqrt(IN_DIM)
        W_self = jax.random.normal(k_ws, (OUT_DIM, IN_DIM), dtype=jnp.float32) * scale
        W_neigh = jax.random.normal(k_wn, (OUT_DIM, IN_DIM), dtype=jnp.float32) * scale
        bias = jnp.zeros((OUT_DIM,), dtype=jnp.float32)
        gamma = jnp.ones((OUT_DIM,), dtype=jnp.float32)
        beta = jnp.zeros((OUT_DIM,), dtype=jnp.float32)
        return {'x': x, 'edge_src': edge_src, 'edge_dst': edge_dst, 'deg': deg, 'W_self': W_self, 'W_neigh': W_neigh, 'bias': bias, 'gamma': gamma, 'beta': beta}
    _L3_gnn_all = _L3_gnn_setup()
    _L3_gnn_in = {k: v for k, v in _L3_gnn_all.items() if k in ('W_self', 'W_neigh', 'bias', 'gamma', 'beta')}
    del _L3_gnn_all
    return {'x': x, 'src': src, 'dst': dst, 'edge_attr_4': edge_attr_4, 'edge_attr_64': edge_attr_64, 'edge_attr_8': edge_attr_8, 'edge_weight': edge_weight, 'L0_gnn_weight': _L0_gnn_in['weight'], 'L1_gnn_W_e': _L1_gnn_in['W_e'], 'L1_gnn_b_e': _L1_gnn_in['b_e'], 'L1_gnn_W1': _L1_gnn_in['W1'], 'L1_gnn_b1': _L1_gnn_in['b1'], 'L1_gnn_g1': _L1_gnn_in['g1'], 'L1_gnn_beta1': _L1_gnn_in['beta1'], 'L1_gnn_W2': _L1_gnn_in['W2'], 'L1_gnn_b2': _L1_gnn_in['b2'], 'L1_gnn_g2': _L1_gnn_in['g2'], 'L1_gnn_beta2': _L1_gnn_in['beta2'], 'L1_gnn_eps': _L1_gnn_in['eps'], 'L2_gnn_W_up0': _L2_gnn_in['W_up0'], 'L2_gnn_W_up1': _L2_gnn_in['W_up1'], 'L2_gnn_W_mlp1': _L2_gnn_in['W_mlp1'], 'L2_gnn_W_mlp2': _L2_gnn_in['W_mlp2'], 'L2_gnn_W_mlp3': _L2_gnn_in['W_mlp3'], 'L2_gnn_W_mlp4': _L2_gnn_in['W_mlp4'], 'L2_gnn_W_out0': _L2_gnn_in['W_out0'], 'L2_gnn_W_out1': _L2_gnn_in['W_out1'], 'L3_gnn_W_self': _L3_gnn_in['W_self'], 'L3_gnn_W_neigh': _L3_gnn_in['W_neigh'], 'L3_gnn_bias': _L3_gnn_in['bias'], 'L3_gnn_gamma': _L3_gnn_in['gamma'], 'L3_gnn_beta': _L3_gnn_in['beta']}

def reference(x, src, dst, edge_attr_4, edge_attr_64, edge_attr_8, edge_weight, L0_gnn_weight, L1_gnn_W_e, L1_gnn_b_e, L1_gnn_W1, L1_gnn_b1, L1_gnn_g1, L1_gnn_beta1, L1_gnn_W2, L1_gnn_b2, L1_gnn_g2, L1_gnn_beta2, L1_gnn_eps, L2_gnn_W_up0, L2_gnn_W_up1, L2_gnn_W_mlp1, L2_gnn_W_mlp2, L2_gnn_W_mlp3, L2_gnn_W_mlp4, L2_gnn_W_out0, L2_gnn_W_out1, L3_gnn_W_self, L3_gnn_W_neigh, L3_gnn_bias, L3_gnn_gamma, L3_gnn_beta):
    import jax
    import jax.numpy as jnp

    def _L0_gnn_ref(x, weight, row, col, vals):
        import jax, jax.numpy as jnp
        import numpy as np
        N_NODES = 2048
        N_EDGES = 16384
        FEAT_DIM = 512
        EMBED_DIM = 512
        h = jnp.einsum('nf,ef->ne', x, weight)
        msgs = vals[:, None] * h[col]
        out = jax.ops.segment_sum(msgs, row, num_segments=N_NODES)
        return out

    def _L1_gnn_ref(x, edge_attr, edge_index, W_e, b_e, W1, b1, g1, beta1, W2, b2, g2, beta2, eps):
        import jax, jax.numpy as jnp
        import numpy as np
        N, E, H, ED = (50000, 12500, 512, 64)
        BN_EPS = 1e-05

        def _bn(h, g, b):
            mu = jnp.mean(h, axis=0)
            var = jnp.mean(jnp.square(h - mu), axis=0)
            return (h - mu) * jax.lax.rsqrt(var + BN_EPS) * g + b
        src, dst = (edge_index[0], edge_index[1])
        msg = jax.nn.relu(x[src] + edge_attr @ W_e + b_e)
        aggr = jax.ops.segment_sum(msg, dst, num_segments=x.shape[0])
        h = (1.0 + eps) * x + aggr
        h = jax.nn.silu(_bn(h @ W1 + b1, g1, beta1))
        h = h @ W2 + b2
        return jax.nn.silu(_bn(h, g2, beta2))

    def _L2_gnn_ref(node_feats, edge_attrs, edge_feats, edge_index, W_up0, W_up1, W_mlp1, W_mlp2, W_mlp3, W_mlp4, W_out0, W_out1):
        import jax, jax.numpy as jnp
        import numpy as np
        MUL = 128
        N_NODES = 10000
        N_EDGES = 5000
        R_BASIS = 8
        HIDDEN = 64
        W_NUMEL = 4 * MUL
        SQRT3 = 3.0 ** 0.5
        SILU_2MOM = 1.679177
        AVG_NUM_NEIGHBORS = 10.0

        def _lin_irreps(x0, x1, W0, W1):
            y0 = x0 @ W0 / jnp.sqrt(jnp.float32(W0.shape[0]))
            y1 = jnp.einsum('num,uv->nvm', x1, W1) / jnp.sqrt(jnp.float32(W1.shape[0]))
            return (y0, y1)

        def _forward(node_feats, edge_attrs, edge_feats, edge_index, W_up0, W_up1, W_mlp1, W_mlp2, W_mlp3, W_mlp4, W_out0, W_out1):
            num_nodes = node_feats.shape[0]
            sender, receiver = (edge_index[0], edge_index[1])
            x0 = node_feats[:, :MUL]
            x1 = node_feats[:, MUL:].reshape(num_nodes, MUL, 3)
            x0, x1 = _lin_irreps(x0, x1, W_up0, W_up1)
            h = edge_feats
            for W in (W_mlp1, W_mlp2, W_mlp3):
                h = SILU_2MOM * jax.nn.silu(h @ W / jnp.sqrt(jnp.float32(W.shape[0])))
            tpw = h @ W_mlp4 / jnp.sqrt(jnp.float32(W_mlp4.shape[0]))
            w1, w2, w3, w4 = jnp.split(tpw, 4, axis=-1)
            s0 = x0[sender]
            s1 = x1[sender]
            y0 = edge_attrs[:, 0:1]
            y1 = edge_attrs[:, 1:4]
            p1 = w1 * s0 * y0
            p2 = (w2 * s0)[:, :, None] * y1[:, None, :]
            p3 = w3[:, :, None] * s1 * y0[:, None, :]
            p4 = w4 * jnp.einsum('eum,em->eu', s1, y1) / SQRT3
            m0 = jnp.concatenate([p1, p4], axis=-1)
            m1 = jnp.concatenate([p2, p3], axis=1)
            msg0 = jax.ops.segment_sum(m0, receiver, num_segments=num_nodes)
            msg1 = jax.ops.segment_sum(m1, receiver, num_segments=num_nodes)
            o0, o1 = _lin_irreps(msg0, msg1, W_out0, W_out1)
            out = jnp.concatenate([o0, o1.reshape(num_nodes, 3 * MUL)], axis=-1)
            return out / AVG_NUM_NEIGHBORS
        return _forward(node_feats, edge_attrs, edge_feats, edge_index, W_up0, W_up1, W_mlp1, W_mlp2, W_mlp3, W_mlp4, W_out0, W_out1)

    def _L3_gnn_ref(x, edge_src, edge_dst, deg, W_self, W_neigh, bias, gamma, beta):
        import jax, jax.numpy as jnp
        import numpy as np
        N_NODES = 10000
        N_EDGES = 5000
        IN_DIM = 512
        OUT_DIM = 512
        LN_EPS = 1e-05
        n = x.shape[0]
        h_self = jnp.einsum('nd,od->no', x, W_self)
        neigh_sum = jax.ops.segment_sum(x[edge_src], edge_dst, num_segments=n)
        neigh_mean = neigh_sum / jnp.maximum(deg, 1.0)[:, None]
        h_neigh = jnp.einsum('nd,od->no', neigh_mean, W_neigh)
        h = h_self + h_neigh + bias
        mu = jnp.mean(h, axis=-1, keepdims=True)
        var = jnp.mean(jnp.square(h - mu), axis=-1, keepdims=True)
        h = (h - mu) * jax.lax.rsqrt(var + LN_EPS)
        return h * gamma + beta
    edge_index = jnp.stack([src, dst])
    deg = jnp.maximum(jax.ops.segment_sum(jnp.ones(dst.shape, jnp.float32), dst, num_segments=2048), 1.0)
    x = _layernorm(x + _L0_gnn_ref(x, L0_gnn_weight, src, dst, edge_weight), axis=-1)
    x = _layernorm(x + _L1_gnn_ref(x, edge_attr_64, edge_index, L1_gnn_W_e, L1_gnn_b_e, L1_gnn_W1, L1_gnn_b1, L1_gnn_g1, L1_gnn_beta1, L1_gnn_W2, L1_gnn_b2, L1_gnn_g2, L1_gnn_beta2, L1_gnn_eps), axis=-1)
    x = _layernorm(x + _L2_gnn_ref(x, edge_attr_4, edge_attr_8, edge_index, L2_gnn_W_up0, L2_gnn_W_up1, L2_gnn_W_mlp1, L2_gnn_W_mlp2, L2_gnn_W_mlp3, L2_gnn_W_mlp4, L2_gnn_W_out0, L2_gnn_W_out1), axis=-1)
    x = _layernorm(x + _L3_gnn_ref(x, src, dst, deg, L3_gnn_W_self, L3_gnn_W_neigh, L3_gnn_bias, L3_gnn_gamma, L3_gnn_beta), axis=-1)
    return x

_drawn_inputs = setup_inputs


def setup_inputs(seed=0):
    import zlib

    import numpy as np

    out = dict(_drawn_inputs(seed))
    spreads = {'L1_gnn_b_e': (0.0, 0.1),
     'L1_gnn_b1': (0.0, 0.1),
     'L1_gnn_g1': (1.0, 0.2),
     'L1_gnn_beta1': (0.0, 0.1),
     'L1_gnn_b2': (0.0, 0.1),
     'L1_gnn_g2': (1.0, 0.2),
     'L1_gnn_beta2': (0.0, 0.1),
     'L3_gnn_bias': (0.0, 0.1),
     'L3_gnn_gamma': (1.0, 0.2),
     'L3_gnn_beta': (0.0, 0.1)}
    factors = {}
    for name, (base, spread) in spreads.items():
        noise = np.random.default_rng([zlib.crc32(name.encode()), seed]).standard_normal(out[name].shape)
        drawn = base * np.exp(spread * noise) if base else spread * noise
        out[name] = jnp.asarray(drawn.astype(out[name].dtype))
    for name, factor in factors.items():
        out[name] = (out[name] * factor).astype(out[name].dtype)
    return out
```

```python
from contextlib import ExitStack

import concourse.bass as bass
from concourse import mybir

F32 = mybir.dt.float32
I32 = mybir.dt.int32
ALU = mybir.AluOpType
ACT = mybir.ActivationFunctionType
AX = mybir.AxisListType

P = 128
N = 2048
D = 512
E = 32768
NT = N // P
ET = E // P
GROUP = 2 * P
NG = E // GROUP + NT
ST = NG * GROUP // P
U = 16
H8 = 8
TURNS = ST // U
ETURNS = ET // U
G_ALL = 16 * ST // H8
EA, EF, NY = 64, 8, 4
SMALL = 16
C_ONE, C_EF, C_Y, C_SRC, C_LOC = 0, 1, 1 + EF, 1 + EF + NY, 2 + EF + NY
ROW = EA + SMALL
HID = 1024
LN_EPS = 1e-5
SILU_2MOM = 1.679177
SB = D


def wait(eng, sem, value):
    if isinstance(value, int) and value <= 0:
        return
    eng.wait_ge(sem, value)


def turns(eng, n, body):
    body(0)
    with eng.Fori(1, n - 1) as i:
        body(i)
    body(n - 1)


def ahead(turn, k, per, end):
    turn_k = turn + k // per if k // per else turn
    if isinstance(turn_k, int) and turn_k >= end:
        return None
    return turn_k, k % per, turn * per + k


def expand(ap, axis, n):
    shape = list(ap.shape)
    return ap.unsqueeze(axis).broadcast_to(shape[:axis] + [n] + shape[axis:])


class Chain:

    def __init__(self, eng, sem):
        self.eng, self.sem, self.n = eng, sem, 0

    def __call__(self, ins):
        ins.then_inc(self.sem, 1)
        self.n += 1
        self.eng.wait_ge(self.sem, self.n)


def build(nc, a):
    ctx = ExitStack()
    with ctx:
        def sb(name, shape, dt=F32, at=ctx):
            return at.enter_context(nc.sbuf_tensor(name, shape, dt))

        sems = {}

        def sem(name):
            if name not in sems:
                sems[name] = ctx.enter_context(nc.semaphore(name))
            return sems[name]

        def gate(eng, name):
            eng.sem_inc(sem(f"gate_{name}"), 1)

        slots_d = nc.dram_tensor("slots_by_dst", [P * ST, ROW], F32, kind="Internal").ap()
        slots_s = nc.dram_tensor("slots_by_src", [P * ST, 4], F32, kind="Internal").ap()
        table = [nc.dram_tensor(f"nodes_{k}", [N, D], F32, kind="Internal").ap() for k in (1, 2, 3)]
        slots_d_v = slots_d.rearrange("(p t) c -> p t c", p=P)
        slots_s_v = slots_s.rearrange("(p t) c -> p t c", p=P)

        x_res = sb("x_res", [P, NT, D])
        acc = sb("acc", [P, NT * 2 * D])
        small = sb("small", [P, ST, SMALL])
        gath = [sb(f"gath{k}", [P, D]) for k in range(H8)]
        wbuf = sb("wbuf", [P, 8192])
        we = sb("we", [EA + 1, D])
        wup = sb("wup", [P, 2, P])
        ident = sb("ident", [P, P])
        iota = sb("iota", [P, NG])
        bin_s = sb("bin_s", [P, NG], I32)
        bin_d = sb("bin_d", [P, NG], I32)
        idx = sb("idx", [P, 2, H8], I32)
        stats = sb("stats", [P, 2, 6])
        mv = sb("mv", [P, 2, 2])
        std = sb("std", [P, 2])
        rstd = sb("rstd", [P, 2])
        eps_ln = sb("eps_ln", [P, 1])
        rdeg = sb("rdeg", [P, NT])
        ones2 = sb("ones2", [P, 2])
        deg = sb("deg", [P, NT])
        eps1 = sb("eps1", [P, 1])
        bn_in = sb("bn_in", [P, 36])
        bank = [ctx.enter_context(nc.psum_tensor(f"bank{k}", [P, 512], F32)) for k in range(8)]

        edge_small = acc[:, 12288:16384].rearrange("p (t c) -> p t c", c=SMALL)
        is_bin = acc[:, 0:4096].rearrange("p (b t) -> p b t", b=NT)
        count = acc[:, 4096:8192].rearrange("p (b t) -> p b t", b=NT)
        slots0 = acc[:, 8192:8192 + 4 * ST].rearrange("p (t c) -> p t c", c=4)
        acc_n = acc[:, 0:NT * D].rearrange("p (n d) -> p n d", d=D)

        s0 = ExitStack()
        key = [sb(f"key{k}", [P, ET], I32, s0) for k in range(2)]
        hi_i = sb("hi_i", [P, ET], I32, s0)
        lo_i = sb("lo_i", [P, ET], I32, s0)
        hi_f = sb("hi_f", [P, ET], F32, s0)
        rank = sb("rank", [P, ET], F32, s0)
        row = [sb(f"row{k}", [P, ET], I32, s0) for k in range(2)]
        edge_src = sb("edge_src", [P, ET, 4], F32, s0)
        w_in = sb("w_in", [P, ET], F32, s0)
        tri = sb("tri", [P, P], F32, s0)
        ones = sb("ones", [P, P], F32, s0)
        pad_d = sb("pad_d", [P, ROW], F32, s0)
        pad_s = sb("pad_s", [P, 4], F32, s0)
        before = sb("before", [P, NT], F32, s0)
        rcount = sb("rcount", [P, NT], F32, s0)
        tot_i = sb("tot_i", [P, NT], I32, s0)
        grp_i = sb("grp_i", [P, NT], I32, s0)
        grp = sb("grp", [P, NT], F32, s0)
        gend = sb("gend", [P, NT], F32, s0)
        off = sb("off", [P, NT], F32, s0)
        gsum = sb("gsum", [P, NG], F32, s0)
        stage_s = sb("stage_s", [P, 2, H8, 4], F32, s0)
        srow = sb("srow", [P, 2, H8], I32, s0)
        stage_d = sb("stage_d", [P, 2, H8, ROW], F32, s0)
        drow = sb("drow", [P, 2, H8], I32, s0)
        slot0 = sb("slot0", [P, 2, H8, 4], F32, s0)
        oh0 = sb("oh0", [P, H8, P], F32, s0)
        dense0 = sb("dense0", [P, 6, D], F32, s0)
        s0.close()
        ef_in = dense0[:, 0:4, :].rearrange("p a (t c) -> p (a t) c", c=EF)
        y_in = dense0[:, 4:6, :].rearrange("p a (t c) -> p (a t) c", c=NY)
        gcmp = acc[:, 8192:8192 + NG * NT].rearrange("p (g b) -> p g b", b=NT)

        s1 = ExitStack()
        chunk = sb("chunk", [P, 2, H8, ROW], F32, s1)
        rowT = [sb(f"rowT{k}", [ROW, 4 * P], F32, s1) for k in range(4)]
        msg = [sb(f"msg{k}", [P, D], F32, s1) for k in range(4)]
        oh1 = sb("oh1", [P, H8, P], F32, s1)
        s1.close()
        s1d = ExitStack()
        hT = sb("hT", [P, 4, N], F32, s1d)
        bst = sb("bst", [P, 8, 4, 6], F32, s1d)
        bmv = sb("bmv", [P, 8, 2], F32, s1d)
        bstd = sb("bstd", [P, 8], F32, s1d)
        bscale = sb("bscale", [P, 8], F32, s1d)
        bshift = sb("bshift", [P, 8], F32, s1d)
        btmp = sb("btmp", [P, 8], F32, s1d)
        nst = sb("nst", [P, NT, 6], F32, s1d)
        nmv = sb("nmv", [P, NT, 2], F32, s1d)
        nstd = sb("nstd", [P, NT], F32, s1d)
        s1d.close()
        aT = acc[:, :].rearrange("p (f n) -> p f n", f=8)
        s2 = ExitStack()
        slot2 = sb("slot2", [P, 2, H8, SMALL], F32, s2)
        efT = sb("efT", [P, P], F32, s2)
        hid = [sb(f"hid{k}", [P, 4 * P], F32, s2) for k in range(4)]
        prod = [sb(f"prod{k}", [P, 6, P], F32, s2) for k in range(4)]
        dot = [sb(f"dot{k}", [P, P], F32, s2) for k in range(2)]
        oh2 = sb("oh2", [P, 4, 5, P], F32, s2)
        s2.close()
        s2d = ExitStack()
        dn = [sb(f"dn{k}", [P, 8, P], F32, s2d) for k in range(2)]
        dnT = [sb(f"dnT{k}", [P, 8, P], F32, s2d) for k in range(2)]
        dz = [sb(f"dz{k}", [P, D], F32, s2d) for k in range(2)]
        dy = [sb(f"dy{k}", [P, D], F32, s2d) for k in range(2)]
        s2d.close()
        s3 = ExitStack()
        slot3 = sb("slot3", [P, 2, H8, SMALL], F32, s3)
        oh3 = sb("oh3", [P, H8, P], F32, s3)
        s3.close()
        iota_b = iota[:, 0:NT]
        b1, g1, be1 = (bn_in[:, 8 * k:8 * k + 8] for k in range(3))
        b2, g2, be2 = (bn_in[:, 24 + 4 * k:28 + 4 * k] for k in range(3))

        w0 = wbuf[:, 0:2048].rearrange("p (k n) -> p k n", k=4)
        w1 = wbuf[:, 0:4096].rearrange("p (k n) -> p k n", k=4)
        w2 = wbuf[:, 4096:8192].rearrange("p (k n) -> p k n", k=8)
        m1 = wbuf[:, 0:512].rearrange("p (j n) -> p j n", j=4)
        m2 = wbuf[:, 512:640]
        m3 = wbuf[:, 640:768]
        m4 = wbuf[:, 768:1792].rearrange("p (e n) -> p e n", e=2)
        wo = wbuf[:, 1792:2304].rearrange("p (k n) -> p k n", k=4)
        w3 = wbuf[:, 0:4096].rearrange("p (k n) -> p k n", k=8)
        bias3, gamma3, beta3 = (wbuf[:, 4096 + D * k:4096 + D * (k + 1)] for k in range(3))

        acc2 = acc[:, :].rearrange("p (n d) -> p n d", d=2 * D)
        C1, C2 = 1.0 / EF ** 0.5, SILU_2MOM / 8.0
        C_OUT = C2 / (16.0 * 10.0)

        block = ctx.enter_context(nc.Block())

        @block.sync
        def _(sp):
            def load(dst, src, name):
                sp.dma_start(dst, src).then_inc(sem(name), 16)

            for k, name in ((0, "src"), (1, "dst")):
                load(key[k][:, :], a[name].rearrange("(p t) -> p t", p=P), f"s_key{k}")
            load(w_in[:, :], a["edge_weight"].rearrange("(p t) -> p t", p=P), "s_attr")
            load(ef_in, a["edge_attr_8"].rearrange("(p t) c -> p t c", p=P), "s_attr")
            load(y_in, a["edge_attr_4"].rearrange("(p t) c -> p t c", p=P), "s_attr")
            sp.wait_ge(sem("s_pad"), 5)
            sp.dma_start(slots_s_v, expand(pad_s[:, :], 1, ST)).then_inc(sem("s_fill_s"), 16)
            sp.dma_start(slots_d_v, expand(pad_d[:, :], 1, ST)).then_inc(sem("s_fill_d"), 16)
            load(w0, a["w0"].rearrange("(k p) n -> p k n", p=P), "s_w0")
            load(x_res[:, :, :], a["x"].rearrange("(n p) d -> p n d", p=P), "s_x")
            load(we[0:EA, :], a["L1_gnn_W_e"], "s_we")
            load(we[EA:EA + 1, :], a["L1_gnn_b_e"].rearrange("(o n) -> o n", o=1), "s_we")
            load(bn_in[:, :], a["bn"], "s_we")
            load(eps1[:, :], a["eps"], "s_we")
            for k in range(2):
                load(wup[:, k, :], a[f"L2_gnn_W_up{k}"], "s_we")

            sp.wait_ge(sem("s_rows"), 1)

            def stage_src(i):
                for h in range(2):
                    t0 = i * U + h * H8
                    wait(sp, sem(f"s_scat_s{h}"), i * (16 * H8))
                    gate(sp, "sp")
                    sp.dma_start(stage_s[:, h], edge_src[:, bass.ds(t0, H8), :]).then_inc(sem(f"s_stage_s{h}"), 16)
                    sp.dma_start(srow[:, h], row[0][:, bass.ds(t0, H8)]).then_inc(sem(f"s_stage_s{h}"), 16)

            turns(sp, ETURNS, stage_src)

            for h in range(2):
                sp.wait_ge(sem(f"s_scat_s{h}"), 16 * H8 * ETURNS)
            sp.wait_ge(sem("s_binned"), 1)
            load(slots0, slots_s_v, "s_slots0")

            sp.wait_ge(sem("s_rows"), 2)

            def stage_dst(i):
                for h in range(2):
                    t0 = i * U + h * H8
                    wait(sp, sem(f"s_scat_d{h}"), i * (16 * H8))
                    gate(sp, "sp")
                    s = sem(f"s_stage_d{h}")
                    sp.dma_start(stage_d[:, h, :, 0:EA],
                                 a["edge_attr_64"].rearrange("(p t) c -> p t c", p=P)[:, bass.ds(t0, H8), :]).then_inc(s, 16)
                    sp.dma_start(stage_d[:, h, :, EA:ROW], edge_small[:, bass.ds(t0, H8), :]).then_inc(s, 16)
                    sp.dma_start(drow[:, h], row[1][:, bass.ds(t0, H8)]).then_inc(s, 16)

            turns(sp, ETURNS, stage_dst)

            sp.wait_ge(sem("L0_mm"), NT)
            load(w1, a["L1_gnn_W1"].rearrange("(k p) n -> p k n", p=P), "s_w1")
            load(w2, a["L1_gnn_W2"].rearrange("(k p) n -> p k n", p=P), "s_w1")

            for h in range(2):
                sp.wait_ge(sem(f"s_scat_d{h}"), 16 * H8 * ETURNS)

            def chunks(i):
                for h in range(2):
                    H = i * 2 + h
                    wait(sp, sem("L1_tr"), (H - 1) * 2)
                    gate(sp, "sp")
                    wait(sp, sem("L1_idx"), H - 1)
                    gate(sp, "sp")
                    wait(sp, sem("L1_oh"), (H - 1) * H8)
                    gate(sp, "sp")
                    sp.dma_start(chunk[:, h], slots_d_v[:, bass.ds(H * H8, H8), :]).then_inc(sem(f"L1_chunk{h}"), 16)

            turns(sp, TURNS, chunks)

            sp.wait_ge(sem("L1_h2"), 16)
            sp.wait_ge(sem("s_wz"), 1)
            for k in range(H8):
                j, e = divmod(k, 2)
                load(m1[16 * k + C_EF:16 * k + C_EF + EF, j, 64 * e:64 * e + 64], a["L2_gnn_W_mlp1"], "s_w2")
            for e in range(2):
                load(m2[64 * e:64 * e + 64, 64 * e:64 * e + 64], a["L2_gnn_W_mlp2"], "s_w2")
                load(m3[64 * e:64 * e + 64, 64 * e:64 * e + 64], a["L2_gnn_W_mlp3"], "s_w2")
                for q, to in ((1, 0), (0, 1), (2, 2), (3, 3)):
                    load(m4[64 * e:64 * e + 64, e, P * to:P * to + P], a["L2_gnn_W_mlp4"][:, P * q:P * q + P], "s_w2")
            for k in range(2):
                load(wo[:, 2 * k:2 * k + 2, :], a[f"L2_gnn_W_out{k}"].rearrange("(k p) n -> p k n", p=P), "s_w2")

            def up(i):
                for s in range(2):
                    n = i * 2 + s
                    sp.wait_ge(sem("L1_ub"), n + 1)
                    gate(sp, "sp")
                    sp.dma_start(table[1][bass.ds(n * P, P), :], gath[s][:, :]).then_inc(sem(f"L1_st{s}"), 16)

            turns(sp, NT // 2, up)

            def nodes3(i):
                for s in range(2):
                    n = i * 2 + s
                    sp.wait_ge(sem("L2_x"), n + 1)
                    gate(sp, "sp")
                    sp.dma_start(table[2][bass.ds(n * P, P), :], x_res[:, bass.ds(n, 1), :]).then_inc(sem("L2_st"), 16)

            turns(sp, NT // 2, nodes3)
            sp.wait_ge(sem("L2_mm"), NT)
            load(w3, a["w3"].rearrange("(k p) n -> p k n", p=P), "s_w3")
            for k, name in enumerate(("bias", "gamma", "beta")):
                load((bias3, gamma3, beta3)[k], a[name], "s_w3")

            def store(i):
                for s in range(2):
                    n = i * 2 + s
                    sp.wait_ge(sem("L3_y"), n + 1)
                    gate(sp, "sp")
                    sp.dma_start(a["out"][bass.ds(n * P, P), :], dy[s][:, :]).then_inc(sem(f"L3_st{s}"), 16)

            turns(sp, NT // 2, store)
            for s in range(2):
                sp.wait_ge(sem(f"L3_st{s}"), 16 * (NT // 2))

        @block.gpsimd
        def _(pool):
            pool.memset(pad_s[:, :], 0.0).then_inc(sem("s_pad0"), 1)
            pool.memset(pad_d[:, :], 0.0).then_inc(sem("s_pad0"), 1)
            pool.iota(iota[:, :], [[1, NG]], 0, 0, True).then_inc(sem("s_iota"), 1)
            pool.wait_ge(sem("s_pad0"), 2)
            pool.memset(pad_s[:, 1:2], -1.0).then_inc(sem("s_pad"), 1)
            pool.memset(pad_d[:, EA + C_LOC:EA + C_LOC + 1], -1.0).then_inc(sem("s_pad"), 1)
            pool.memset(pad_d[:, EA + C_ONE:EA + C_ONE + 1], 1.0).then_inc(sem("s_pad"), 1)
            pool.memset(edge_small[:, :, :], 0.0).then_inc(sem("s_pad"), 1)
            pool.memset(edge_src[:, :, :], 0.0).then_inc(sem("s_pad"), 1)
            pool.memset(ident[:, :], 0.0).then_inc(sem("s_id"), 1)
            pool.memset(tri[:, :], 0.0).then_inc(sem("s_id"), 1)
            pool.memset(ones[:, :], 1.0).then_inc(sem("s_ones"), 1)
            pool.memset(ones2[:, :], 1.0).then_inc(sem("s_ones"), 1)
            pool.memset(eps_ln[:, :], LN_EPS).then_inc(sem("s_ones"), 1)
            pool.memset(deg[:, :], 0.0).then_inc(sem("s_ones"), 1)
            pool.wait_ge(sem("s_id"), 2)
            pool.affine_select(out=ident[:, :], in_=ident[:, :], compare_op=ALU.not_equal, fill=1.0, base=0,
                               pattern=[[-1, P]], channel_multiplier=1).then_inc(sem("s_id"), 1)
            pool.affine_select(out=tri[:, :], in_=tri[:, :], compare_op=ALU.is_ge, fill=1.0, base=0,
                               pattern=[[-1, P]], channel_multiplier=1).then_inc(sem("s_id"), 1)

            def scatter(tag, stage, at, out, staged):
                def body(i):
                    for h in range(2):
                        pool.wait_ge(sem(f"s_stage_{tag}{h}"), i * (16 * staged) + 16 * staged)
                        gate(pool, "pool")
                        pool.wait_ge(sem(f"s_fill_{tag}"), 16)
                        for k in range(H8):
                            pool.indirect_dma_start(out, bass.IndirectOffsetOnAxis(ap=at[:, h, k:k + 1], axis=0),
                                                    stage[:, h, k, :], None).then_inc(sem(f"s_scat_{tag}{h}"), 16)

                turns(pool, ETURNS, body)

            def gather(L, source, ready, total, free):
                def body(i):
                    for j in range(U):
                        h, k = divmod(j, H8)
                        T = i * U + j
                        pool.wait_ge(sem(f"L{L}_idx"), i * 2 + h + 1)
                        wait(pool, sem(f"L{L}_{free}"), T - H8 + 1)
                        gate(pool, "pool")
                        pool.wait_ge(sem(ready), total)
                        pool.indirect_dma_start(gath[k][:, :], None, source,
                                                bass.IndirectOffsetOnAxis(ap=idx[:, h, k:k + 1], axis=0))\
                            .then_inc(sem(f"gath{k}"), 16)

                turns(pool, TURNS, body)

            scatter("s", stage_s, srow, slots_s, 2)
            gather(0, a["x"], "s_slots0", 16, "seg")
            scatter("d", stage_d, drow, slots_d, 3)
            gather(1, table[0], "L0_st", 16 * NT, "add")
            pool.wait_ge(sem("L1_h2"), 16)
            pool.memset(wbuf[:, 0:2304], 0.0).then_inc(sem("s_wz"), 1)
            pool.memset(acc[:, :], 0.0).then_inc(sem("s_az"), 1)
            pool.wait_ge(sem("L1_st0"), 16 * (NT // 2))
            gather(2, table[1], "L1_st1", 16 * (NT // 2), "prod")
            pool.wait_ge(sem("L2_hs"), NT)
            pool.memset(acc[:, 0:NT * D], 0.0).then_inc(sem("s_az"), 1)
            gather(3, table[2], "L2_st", 16 * NT, "seg")

        @block.scalar
        def _(act):
            act.wait_ge(sem("s_attr"), 48)
            act.wait_ge(sem("s_pad"), 5)
            nc.scalar.activation(edge_small[:, :, C_EF:C_EF + EF], ef_in, ACT.Copy).then_inc(sem("s_small"), 1)
            nc.scalar.activation(edge_small[:, :, C_Y:C_Y + NY], y_in, ACT.Copy).then_inc(sem("s_small"), 1)
            nc.scalar.activation(edge_small[:, :, C_ONE], ef_in[:, :, 0], ACT.Identity, bias=1.0, scale=0.0)\
                .then_inc(sem("s_small"), 1)
            nc.scalar.activation(edge_src[:, :, 2], w_in[:, :], ACT.Copy).then_inc(sem("s_small"), 1)
            act.wait_ge(sem("s_key0"), 16)
            act.wait_ge(sem("s_key1"), 16)
            nc.scalar.activation(edge_src[:, :, 0], key[1][:, :], ACT.Copy).then_inc(sem("s_small"), 1)
            nc.scalar.activation(edge_small[:, :, C_SRC], key[0][:, :], ACT.Copy).then_inc(sem("s_small"), 1)

            act.wait_ge(sem("s_slots0"), 16)

            def idx0(i):
                for h in range(2):
                    H = i * 2 + h
                    wait(act, sem("L0_seg"), (H - 1) * H8)
                    wait(act, sem("L0_oh"), (H - 1) * H8)
                    nc.scalar.activation(slot0[:, h], slots0[:, bass.ds(H * H8, H8), :], ACT.Copy).then_inc(sem("L0_slot"), 1)
                    nc.scalar.activation(idx[:, h], slots0[:, bass.ds(H * H8, H8), 0], ACT.Copy).then_inc(sem("L0_idx"), 1)

            turns(act, TURNS, idx0)

            def copy0(i, ss):
                at_n = ahead(i, ss, 2, NT // 2)
                if at_n is None:
                    return
                _, s, n = at_n
                act.wait_ge(sem("L0_acc"), NG)
                wait(act, sem("L0_tr"), n - 1)
                nc.scalar.activation(dense0[:, s, :], acc_n[:, bass.ds(n, 1), :], ACT.Copy).then_inc(sem("L0_hs"), 1)

            def turned0(i, ss):
                at_n = ahead(i, ss, 2, NT // 2)
                if at_n is None:
                    return
                _, s, n = at_n
                act.wait_ge(sem("L0_tr"), n + 1)
                wait(act, sem("L0_mm"), n - 1)
                nc.scalar.activation(dense0[:, 2 + s, :], bank[2 + s][:, :], ACT.Copy).then_inc(sem("L0_hT"), 1)

            def root(L, n, s):
                act.wait_ge(sem(f"L{L}_mv"), n + 1)
                nc.scalar.activation(std[:, s:s + 1], mv[:, s, 1:2], ACT.Sqrt, bias=eps_ln[:, :]).then_inc(sem(f"L{L}_std"), 1)

            def store0(n):
                act.wait_ge(sem("L0_x"), n + 1)
                act.dma_start(table[0][bass.ds(n * P, P), :], x_res[:, bass.ds(n, 1), :]).then_inc(sem("L0_st"), 16)

            copy0(0, 0)
            copy0(0, 1)
            turned0(0, 0)

            def nodes0(i):
                for s in range(2):
                    n = i * 2 + s
                    copy0(i, s + 2)
                    turned0(i, s + 1)
                    root(0, n, s)
                    store0(n)

            turns(act, NT // 2, nodes0)

            def small1(i, hh):
                at_h = ahead(i, hh, 2, TURNS)
                if at_h is None:
                    return
                turn, h, H = at_h
                act.wait_ge(sem(f"L1_chunk{h}"), turn * 16 + 16)
                wait(act, sem("L1_add"), (H - 1) * H8)
                nc.scalar.activation(small[:, bass.ds(H * H8, H8), :], chunk[:, h, :, EA:ROW], ACT.Copy).then_inc(sem("L1_small"), 1)
                nc.scalar.activation(idx[:, h], chunk[:, h, :, EA + C_SRC], ACT.Copy).then_inc(sem("L1_idx"), 1)

            def turned1(i, qq):
                at_q = ahead(i, qq, 4, TURNS)
                if at_q is None:
                    return
                turn, q, Q = at_q
                act.wait_ge(sem("L1_tr"), Q + 1)
                wait(act, sem("L1_mm"), (Q - 3) * 4)
                nc.scalar.activation(rowT[q][:, :], bank[6 + q % 2][0:ROW, :], ACT.Copy).then_inc(sem("L1_rowT"), 1)

            def relu1(i, jj):
                at_t = ahead(i, jj, U, TURNS)
                if at_t is None:
                    return
                turn, j, T = at_t
                k = j % 4
                act.wait_ge(sem("L1_add"), T + 1)
                nc.scalar.activation(msg[k][:, :], msg[k][:, :], ACT.Relu).then_inc(sem("L1_relu"), 1)

            small1(0, 0)
            turned1(0, 0)
            turned1(0, 1)
            for T in range(3):
                relu1(0, T)

            def edges1(i):
                for j in range(U):
                    if j % H8 == 0:
                        small1(i, j // H8 + 1)
                    if j % 4 == 0:
                        turned1(i, j // 4 + 2)
                    relu1(i, j + 3)

            turns(act, TURNS, edges1)

            def turned1n(i):
                for s in range(2):
                    n = i * 2 + s
                    act.wait_ge(sem("L1_ntr"), n + 1)
                    nc.scalar.activation(hT[:, :, bass.ds(n * P, P)],
                                         bank[s][:, :].rearrange("p (k n) -> p k n", k=4), ACT.Copy).then_inc(sem("L1_hT"), 1)

            turns(act, NT // 2, turned1n)

            def evac1(c):
                for f in range(8):
                    F = c * 8 + f
                    act.wait_ge(sem("L1_h1"), F + 1)
                    nc.scalar.activation(aT[:, f, bass.ds(c * 512, 512)], bank[2 + f % 4][:, :], ACT.Identity,
                                         bias=b1[:, f:f + 1]).then_inc(sem("L1_ev1"), 1)

            turns(act, 4, evac1)

            act.wait_ge(sem("L1_bmv"), 1)
            nc.scalar.activation(bstd[:, :], bmv[:, :, 1], ACT.Sqrt, bias=eps_ln[:, :]).then_inc(sem("L1_bstd"), 1)
            act.wait_ge(sem("L1_bn"), 1)

            def silu1(c):
                if isinstance(c, int) and c >= 4:
                    return
                for f in range(8):
                    at = aT[:, f, bass.ds(c * 512, 512)]
                    nc.scalar.activation(at, at, ACT.Silu, bias=bshift[:, f:f + 1], scale=bscale[:, f:f + 1])\
                        .then_inc(sem("L1_silu"), 1)

            silu1(0)

            def second1(c):
                silu1(c + 1)
                for g in range(4):
                    act.wait_ge(sem("L1_h2"), c * 4 + g + 1)
                    nc.scalar.activation(hT[:, g, bass.ds(c * 512, 512)], bank[2 + g][:, :], ACT.Identity,
                                         bias=b2[:, g:g + 1]).then_inc(sem("L1_ev2"), 1)

            turns(act, 4, second1)

            act.wait_ge(sem("L1_bmv"), 2)
            nc.scalar.activation(bstd[:, 0:4], bmv[:, 0:4, 1], ACT.Sqrt, bias=eps_ln[:, :]).then_inc(sem("L1_bstd"), 1)
            act.wait_ge(sem("L1_bn"), 2)

            def act1(i):
                for s in range(2):
                    n = i * 2 + s
                    wait(act, sem("L1_btr"), n - 1)
                    for g in range(4):
                        ins = nc.scalar.activation(gath[2 + s][:, P * g:P * g + P], hT[:, g, bass.ds(n * P, P)], ACT.Silu,
                                                   bias=bshift[:, g:g + 1], scale=bscale[:, g:g + 1])
                    ins.then_inc(sem("L1_sT"), 1)

            turns(act, NT // 2, act1)

            act.wait_ge(sem("L1_mv"), 1)
            nc.scalar.activation(nstd[:, :], nmv[:, :, 1], ACT.Sqrt, bias=eps_ln[:, :]).then_inc(sem("L1_std"), 1)

            def keep1(i, ss):
                at_n = ahead(i, ss, 2, NT // 2)
                if at_n is None:
                    return
                _, s, n = at_n
                act.wait_ge(sem("L1_xn"), n + 1)
                nc.scalar.activation(x_res[:, bass.ds(n, 1), :], gath[4 + s][:, :], ACT.Copy).then_inc(sem("L1_x"), 1)
                act.wait_ge(sem("L1_utr"), n + 1)
                wait(act, sem("L1_umm"), n - 1)
                nc.scalar.activation(gath[6 + s][:, :], bank[2 + s][:, :], ACT.Copy).then_inc(sem("L1_uT"), 1)

            keep1(0, 0)

            def up1(i):
                for s in range(2):
                    n = i * 2 + s
                    keep1(i, s + 1)
                    act.wait_ge(sem("L1_umm"), n + 1)
                    wait(act, sem(f"L1_st{s}"), i * 16)
                    nc.scalar.activation(gath[s][:, :], bank[4 + s][:, :], ACT.Copy, scale=P ** -0.5).then_inc(sem("L1_ub"), 1)

            turns(act, NT // 2, up1)

            def slots2(i, hh):
                at_h = ahead(i, hh, 2, TURNS)
                if at_h is None:
                    return
                turn, h, H = at_h
                wait(act, sem("L2_prod"), (H - 1) * H8)
                wait(act, sem("L2_tr"), H - 1)
                nc.scalar.activation(slot2[:, h], small[:, bass.ds(H * H8, H8), :], ACT.Copy).then_inc(sem("L2_slot"), 1)
                nc.scalar.activation(idx[:, h], small[:, bass.ds(H * H8, H8), C_SRC], ACT.Copy).then_inc(sem("L2_idx"), 1)

            def turned2(i, hh):
                at_h = ahead(i, hh, 2, TURNS)
                if at_h is None:
                    return
                turn, h, H = at_h
                act.wait_ge(sem("L2_tr"), H + 1)
                wait(act, sem("L2_z"), H * 3 - 2)
                nc.scalar.activation(efT[:, :], bank[7][:, 0:P], ACT.Copy).then_inc(sem("L2_efT"), 1)

            def hidden2(i, hh, k):
                at_h = ahead(i, hh, 2, TURNS)
                if at_h is None:
                    return
                turn, h, H = at_h
                act.wait_ge(sem("L2_z"), H * 3 + k + 1)
                if k == 2:
                    wait(act, sem("L2_w"), (H - 1) * H8)
                nc.scalar.activation(hid[k if k < 2 else 2 + h][:, :], bank[6][:, :], ACT.Silu,
                                     scale=C1 if k == 0 else C2).then_inc(sem("L2_h"), 1)

            def scaled2(i, jj):
                at_t = ahead(i, jj, U, TURNS)
                if at_t is None:
                    return
                turn, j, T = at_t
                h, k = divmod(j, H8)
                y = slot2[:, h, k, C_Y:C_Y + NY]
                act.wait_ge(sem("L2_oh"), T + 1)
                for m in range(4):
                    nc.scalar.activation(oh2[:, j % 4, m, :], oh2[:, j % 4, 4, :], ACT.Copy, scale=y[:, m:m + 1])\
                        .then_inc(sem("L2_ohy"), 1)
                act.wait_ge(sem(f"gath{k}"), 2 * G_ALL + turn * 32 + 16 * h + 16)
                wait(act, sem("L2_prod"), T - 1)
                nc.scalar.activation(dot[j % 2][:, :], gath[k][:, P:2 * P], ACT.Copy, scale=y[:, 1:2]).then_inc(sem("L2_dot"), 1)

            slots2(0, 0)
            turned2(0, 0)
            for k in range(3):
                hidden2(0, 0, k)
            scaled2(0, 0)
            scaled2(0, 1)

            def edges2(i):
                for j in range(U):
                    if j % H8 == 0:
                        slots2(i, j // H8 + 1)
                        turned2(i, j // H8 + 1)
                    if j % H8 in (2, 4, 6):
                        hidden2(i, j // H8 + 1, j % H8 // 2 - 1)
                    scaled2(i, j + 2)

            turns(act, TURNS, edges2)

            def copy2(i, ss):
                at_n = ahead(i, ss, 2, NT // 2)
                if at_n is None:
                    return
                _, s, n = at_n
                act.wait_ge(sem("L2_acc"), NG)
                wait(act, sem("L2_ntr"), n - 1)
                nc.scalar.activation(dn[s][:, :, :], acc2[:, bass.ds(n, 1), :], ACT.Copy).then_inc(sem("L2_hs"), 1)

            def turned2n(L, i, ss):
                at_n = ahead(i, ss, 2, NT // 2)
                if at_n is None:
                    return
                _, s, n = at_n
                act.wait_ge(sem(f"L{L}_ntr"), n + 1)
                wait(act, sem(f"L{L}_mm"), n - 1)
                for b in range(2):
                    nc.scalar.activation(dnT[s][:, 4 * b:4 * b + 4, :], bank[2 * s + b][:, :], ACT.Copy).then_inc(sem(f"L{L}_nT"), 1)

            copy2(0, 0)
            copy2(0, 1)
            turned2n(2, 0, 0)

            def nodes2(i):
                for s in range(2):
                    n = i * 2 + s
                    copy2(i, s + 2)
                    turned2n(2, i, s + 1)
                    root(2, n, s)

            turns(act, NT // 2, nodes2)

            def idx3(i):
                for h in range(2):
                    H = i * 2 + h
                    wait(act, sem("L3_seg"), (H - 1) * H8)
                    wait(act, sem("L3_oh"), (H - 1) * H8)
                    nc.scalar.activation(slot3[:, h], small[:, bass.ds(H * H8, H8), :], ACT.Copy).then_inc(sem("L3_slot"), 1)
                    nc.scalar.activation(idx[:, h], small[:, bass.ds(H * H8, H8), C_SRC], ACT.Copy).then_inc(sem("L3_idx"), 1)

            turns(act, TURNS, idx3)

            def copy3(i, ss):
                at_n = ahead(i, ss, 2, NT // 2)
                if at_n is None:
                    return
                _, s, n = at_n
                act.wait_ge(sem("L3_acc"), NG)
                wait(act, sem("L3_ntr"), n - 1)
                nc.scalar.activation(dn[s][:, 0:4, :], x_res[:, bass.ds(n, 1), :], ACT.Copy).then_inc(sem("L3_xs"), 1)

            copy3(0, 0)
            copy3(0, 1)
            turned2n(3, 0, 0)

            def nodes3(i):
                for s in range(2):
                    n = i * 2 + s
                    copy3(i, s + 2)
                    turned2n(3, i, s + 1)
                    for k in range(2):
                        act.wait_ge(sem("L3_mv"), n * 2 + k + 1)
                        nc.scalar.activation(std[:, k:k + 1], mv[:, k, 1:2], ACT.Sqrt, bias=eps_ln[:, :]).then_inc(sem("L3_std"), 1)

            turns(act, NT // 2, nodes3)

        @block.tensor
        def _(pe):
            pe.wait_ge(sem("s_id"), 4)
            pe.wait_ge(sem("s_ones"), 4)
            for k in range(2):
                pe.wait_ge(sem("s_rcount"), k + 1)
                nc.tensor.matmul(bank[0][:, 0:NT], tri[:, :], rcount[:, :], start=True, stop=True)
                nc.tensor.matmul(bank[1][:, 0:NT], ones[:, :], rcount[:, :], start=True, stop=True).then_inc(sem("s_counts"), 1)

            def sums(L, oh, lead):
                def body(i):
                    for j in range(U):
                        h, k = divmod(j, H8)
                        T = i * U + j
                        pe.wait_ge(sem(f"L{L}_oh"), T + 1)
                        pe.wait_ge(sem(f"gath{k}"), L * G_ALL + i * 32 + 16 * h + 16)
                        if j % 2 == 0:
                            wait(pe, sem(f"L{L}_acc"), i * 8 + j // 2 - 1)
                        b = j // 2 % 2
                        if L == 3:
                            nc.tensor.matmul(bank[2 + b][:, 0:2], oh[:, k, :], ones2[:, :], start=j % 2 == 0, stop=j % 2 == 1)
                        nc.tensor.matmul(bank[b][:, :], oh[:, k, :], gath[k][:, :], start=j % 2 == 0, stop=j % 2 == 1)\
                            .then_inc(sem(f"L{L}_seg"), 1)

                turns(pe, TURNS, body)

            sums(0, oh0, None)

            def turn0(i, ss):
                at_n = ahead(i, ss, 2, NT // 2)
                if at_n is None:
                    return
                _, s, n = at_n
                pe.wait_ge(sem("L0_hs"), n + 1)
                wait(pe, sem("L0_hT"), n - 1)
                for k in range(4):
                    ins = nc.tensor.transpose(bank[2 + s][:, P * k:P * k + P], dense0[:, s, P * k:P * k + P], ident[:, :])
                ins.then_inc(sem("L0_tr"), 1)

            pe.wait_ge(sem("s_w0"), 16)
            turn0(0, 0)

            def nodes0(i):
                for s in range(2):
                    n = i * 2 + s
                    turn0(i, s + 1)
                    pe.wait_ge(sem("L0_hT"), n + 1)
                    wait(pe, sem("L0_z"), n - 1)
                    for k in range(4):
                        ins = nc.tensor.matmul(bank[4 + s][:, :], dense0[:, 2 + s, P * k:P * k + P], w0[:, k, :],
                                               start=k == 0, stop=k == 3)
                    ins.then_inc(sem("L0_mm"), 1)

            turns(pe, NT // 2, nodes0)

            pe.wait_ge(sem("L0_z"), NT)
            pe.wait_ge(sem("s_we"), 16 * 6)

            def turn1(i, qq):
                at_q = ahead(i, qq, 4, TURNS)
                if at_q is None:
                    return
                turn, q, Q = at_q
                h = q // 2
                pe.wait_ge(sem(f"L1_chunk{h}"), turn * 16 + 16)
                wait(pe, sem("L1_rowT"), Q - 1)
                for k in range(4):
                    ins = nc.tensor.transpose(bank[6 + q % 2][0:ROW, P * k:P * k + P], chunk[:, h, 4 * (q % 2) + k, :], ident[:, :])
                ins.then_inc(sem("L1_tr"), 1)

            def mm1(i, jj):
                at_t = ahead(i, jj, U, TURNS)
                if at_t is None:
                    return
                turn, j, T = at_t
                q, k = divmod(j, 4)
                pe.wait_ge(sem("L1_rowT"), turn * 4 + q + 1)
                wait(pe, sem("L1_add"), T - 3)
                nc.tensor.matmul(bank[j % 4][:, :], rowT[q][0:EA + 1, P * k:P * k + P], we[:, :], start=True, stop=True)\
                    .then_inc(sem("L1_mm"), 1)

            turn1(0, 0)
            turn1(0, 1)
            for T in range(5):
                mm1(0, T)

            def edges1(i):
                for j in range(U):
                    T = i * U + j
                    if j % 4 == 0:
                        turn1(i, j // 4 + 2)
                    mm1(i, j + 5)
                    pe.wait_ge(sem("L1_oh"), T + 1)
                    pe.wait_ge(sem("L1_relu"), T + 1)
                    if j % 2 == 0:
                        wait(pe, sem("L1_acc"), i * 8 + j // 2 - 1)
                    nc.tensor.matmul(bank[4 + j // 2 % 2][:, :], oh1[:, j % H8, :], msg[j % 4][:, :],
                                     start=j % 2 == 0, stop=j % 2 == 1).then_inc(sem("L1_seg"), 1)

            turns(pe, TURNS, edges1)

            def turn1n(i):
                for s in range(2):
                    n = i * 2 + s
                    pe.wait_ge(sem("L1_hs"), n + 1)
                    wait(pe, sem("L1_hT"), n - 1)
                    for k in range(4):
                        ins = nc.tensor.transpose(bank[s][:, P * k:P * k + P], gath[s][:, P * k:P * k + P], ident[:, :])
                    ins.then_inc(sem("L1_ntr"), 1)

            turns(pe, NT // 2, turn1n)
            pe.wait_ge(sem("s_w1"), 32)
            pe.wait_ge(sem("L1_hT"), NT)
            pe.wait_ge(sem("L1_acc"), NG)

            def first1(c):
                for f in range(8):
                    wait(pe, sem("L1_ev1"), c * 8 + f - 3)
                    for k in range(4):
                        ins = nc.tensor.matmul(bank[2 + f % 4][:, :], w1[:, k, P * f:P * f + P], hT[:, k, bass.ds(c * 512, 512)],
                                               start=k == 0, stop=k == 3)
                    ins.then_inc(sem("L1_h1"), 1)

            turns(pe, 4, first1)
            pe.wait_ge(sem("L1_ev1"), 32)

            def second1(c):
                pe.wait_ge(sem("L1_silu"), c * 8 + 8)
                for g in range(4):
                    wait(pe, sem("L1_ev2"), c * 4 + g - 3)
                    for f in range(8):
                        ins = nc.tensor.matmul(bank[2 + g][:, :], w2[:, f, P * g:P * g + P], aT[:, f, bass.ds(c * 512, 512)],
                                               start=f == 0, stop=f == 7)
                    ins.then_inc(sem("L1_h2"), 1)

            turns(pe, 4, second1)

            def back1(i):
                for s in range(2):
                    n = i * 2 + s
                    pe.wait_ge(sem("L1_sT"), n + 1)
                    wait(pe, sem("L1_z"), n - 1)
                    for g in range(4):
                        ins = nc.tensor.transpose(bank[s][:, P * g:P * g + P], gath[2 + s][:, P * g:P * g + P], ident[:, :])
                    ins.then_inc(sem("L1_btr"), 1)

            turns(pe, NT // 2, back1)

            def uturn(i, ss):
                at_n = ahead(i, ss, 2, NT // 2)
                if at_n is None:
                    return
                _, s, n = at_n
                pe.wait_ge(sem("L1_xn"), n + 1)
                wait(pe, sem("L1_uT"), n - 1)
                nc.tensor.transpose(bank[2 + s][:, 0:P], gath[4 + s][:, 0:P], ident[:, :])
                for m in range(3):
                    ins = nc.tensor.transpose(bank[2 + s][:, P * m + P:P * m + 2 * P],
                                              gath[4 + s][:, P:D].rearrange("p (u m) -> p m u", m=3)[:, m, :], ident[:, :])
                ins.then_inc(sem("L1_utr"), 1)

            pe.wait_ge(sem("L1_ev2"), 16)
            uturn(0, 0)

            def up1(i):
                for s in range(2):
                    n = i * 2 + s
                    uturn(i, s + 1)
                    pe.wait_ge(sem("L1_uT"), n + 1)
                    wait(pe, sem("L1_ub"), n - 1)
                    for m in range(4):
                        ins = nc.tensor.matmul(bank[4 + s][:, P * m:P * m + P], gath[6 + s][:, P * m:P * m + P],
                                               wup[:, min(m, 1), :], start=True, stop=True)
                    ins.then_inc(sem("L1_umm"), 1)

            turns(pe, NT // 2, up1)

            pe.wait_ge(sem("s_w2"), 16 * (8 + 12 + 2))
            pe.wait_ge(sem("L1_ub"), NT)

            def turn2(i, hh):
                at_h = ahead(i, hh, 2, TURNS)
                if at_h is None:
                    return
                turn, h, H = at_h
                pe.wait_ge(sem("L2_slot"), H + 1)
                wait(pe, sem("L2_efT"), H)
                nc.tensor.transpose(bank[7][:, 0:P], slot2[:, h].rearrange("p t c -> p (t c)"), ident[:, :]).then_inc(sem("L2_tr"), 1)

            def layer2(i, hh, k):
                at_h = ahead(i, hh, 2, TURNS)
                if at_h is None:
                    return
                turn, h, H = at_h
                wait(pe, sem("L2_h"), H * 3 + k)
                if k == 0:
                    pe.wait_ge(sem("L2_efT"), H + 1)
                    for j in range(4):
                        ins = nc.tensor.matmul(bank[6][:, P * j:P * j + P], m1[:, j, :], efT[:, :], start=True, stop=True)
                else:
                    ins = nc.tensor.matmul(bank[6][:, :], (m2, m3)[k - 1], hid[k - 1][:, :], start=True, stop=True)
                ins.then_inc(sem("L2_z"), 1)

            def weights2(i, jj):
                at_t = ahead(i, jj, U, TURNS)
                if at_t is None:
                    return
                turn, j, T = at_t
                h, k = divmod(j, H8)
                pe.wait_ge(sem("L2_h"), (turn * 2 + h + 1) * 3)
                wait(pe, sem("L2_prod"), T - 1)
                nc.tensor.matmul(bank[4 + j % 2][:, :], hid[2 + h][:, P * (k // 2):P * (k // 2) + P], m4[:, k % 2, :],
                                 start=True, stop=True).then_inc(sem("L2_w"), 1)

            turn2(0, 0)
            for k in range(3):
                layer2(0, 0, k)
            weights2(0, 0)
            weights2(0, 1)

            def edges2(i):
                for j in range(U):
                    T = i * U + j
                    if j % H8 == 0:
                        turn2(i, j // H8 + 1)
                    if j % H8 in (1, 3, 5):
                        layer2(i, j // H8 + 1, j % H8 // 2)
                    pe.wait_ge(sem("L2_ohy"), T * 4 + 4)
                    pe.wait_ge(sem("L2_prod"), T + 1)
                    if j % 2 == 0:
                        wait(pe, sem("L2_acc"), i * 8 + j // 2 - 1)
                    first, last, b = j % 2 == 0, j % 2 == 1, j // 2 % 2
                    q, o = prod[j % 4], oh2[:, j % 4]
                    nc.tensor.matmul(bank[b][:, :], o[:, 0, :], q[:, 1:5, :], start=first, stop=last)
                    for m in range(3):
                        nc.tensor.matmul(bank[2 + b][:, P * m:P * m + P], o[:, 1 + m, :], q[:, 0, :],
                                         start=first and m == 0, stop=False, skip_group_check=True)
                    nc.tensor.matmul(bank[2 + b][:, 3 * P:4 * P], o[:, 4, :], q[:, 5, :], start=False, stop=last,
                                     skip_group_check=True).then_inc(sem("L2_seg"), 1)
                    weights2(i, j + 2)

            turns(pe, TURNS, edges2)

            def turn2n(L, i, ss):
                at_n = ahead(i, ss, 2, NT // 2)
                if at_n is None:
                    return
                _, s, n = at_n
                for name in (("L2_hs",) if L == 2 else ("L3_xs", "L3_hs")):
                    pe.wait_ge(sem(name), n + 1)
                wait(pe, sem(f"L{L}_nT"), (n - 1) * 2)
                for k in range(8):
                    ins = nc.tensor.transpose(bank[2 * s + k // 4][:, P * (k % 4):P * (k % 4) + P], dn[s][:, k, :], ident[:, :])
                ins.then_inc(sem(f"L{L}_ntr"), 1)

            pe.wait_ge(sem("L2_acc"), NG)
            turn2n(2, 0, 0)

            def nodes2(i):
                for s in range(2):
                    n = i * 2 + s
                    turn2n(2, i, s + 1)
                    pe.wait_ge(sem("L2_nT"), n * 2 + 2)
                    wait(pe, sem("L2_nz"), n - 1)
                    for m, (k0, k1) in enumerate(((0, 7), (4, 1), (5, 2), (6, 3))):
                        for r, k in enumerate((k0, k1)):
                            ins = nc.tensor.matmul(bank[4 + s][:, P * m:P * m + P], dnT[s][:, k, :], wo[:, 2 * min(m, 1) + r, :],
                                                   start=r == 0, stop=r == 1)
                    ins.then_inc(sem("L2_mm"), 1)

            turns(pe, NT // 2, nodes2)

            pe.wait_ge(sem("L2_nz"), NT)
            sums(3, oh3, None)
            pe.wait_ge(sem("s_w3"), 64)
            pe.wait_ge(sem("L3_acc"), NG)
            turn2n(3, 0, 0)

            def nodes3(i):
                for s in range(2):
                    n = i * 2 + s
                    turn2n(3, i, s + 1)
                    pe.wait_ge(sem("L3_nT"), n * 2 + 2)
                    wait(pe, sem("L3_z"), n - 1)
                    for k in range(8):
                        ins = nc.tensor.matmul(bank[4 + s][:, :], dnT[s][:, k, :], w3[:, k, :], start=k == 0, stop=k == 7)
                    ins.then_inc(sem("L3_mm"), 1)

            turns(pe, NT // 2, nodes3)

        @block.vector
        def _(dve):
            v = nc.vector
            step = Chain(dve, sem("s_step"))

            def bins(k, loc, bin_of, grouped):
                dve.wait_ge(sem(f"s_key{k}"), 16)
                step(v.tensor_scalar(hi_i[:, :], key[k][:, :], 7, None, ALU.arith_shift_right))
                step(v.tensor_scalar(lo_i[:, :], key[k][:, :], P - 1, None, ALU.bitwise_and))
                step(v.tensor_copy(hi_f[:, :], hi_i[:, :]))
                dve.wait_ge(sem("s_pad"), 5)
                step(v.tensor_copy(loc, lo_i[:, :]))
                dve.wait_ge(sem("s_iota"), 1)
                step(v.tensor_tensor(is_bin, expand(hi_f[:, :], 1, NT), expand(iota_b, 2, ET), ALU.is_equal))
                step(v.tensor_tensor_scan(count.rearrange("p b t -> p (b t)"), is_bin.rearrange("p b t -> p (b t)"), is_bin.rearrange("p b t -> p (b t)"), 0.0, ALU.add, ALU.bypass))
                step(v.memset(before[:, :], 0.0))
                step(v.tensor_copy(before[:, 1:NT], count[:, 0:NT - 1, ET - 1]))
                v.tensor_tensor(rcount[:, :], count[:, :, ET - 1], before[:, :], ALU.subtract).then_inc(sem("s_rcount"), 1)
                dve.wait_ge(sem("s_counts"), k + 1)
                step(v.tensor_scalar(tot_i[:, :], bank[1][:, 0:NT], float(GROUP - 1), None, ALU.add))
                step(v.tensor_scalar(grp_i[:, :], tot_i[:, :], 8, None, ALU.arith_shift_right))
                step(v.tensor_copy(grp[:, :], grp_i[:, :]))
                step(v.tensor_tensor_scan(gend[:, :], grp[:, :], grp[:, :], 0.0, ALU.add, ALU.bypass))
                step(v.tensor_tensor(off[:, :], gend[:, :], grp[:, :], ALU.subtract))
                step(v.scalar_tensor_tensor(off[:, :], off[:, :], float(GROUP), bank[0][:, 0:NT], ALU.mult, ALU.add))
                step(v.scalar_tensor_tensor(off[:, :], off[:, :], -1.0, before[:, :], ALU.add, ALU.subtract))
                step(v.tensor_tensor(count, count, expand(off[:, :], 2, ET), ALU.add))
                step(v.tensor_tensor(is_bin, count, is_bin, ALU.mult))
                step(v.tensor_reduce(rank[:, :], is_bin.rearrange("p b t -> p t b"), AX.X, ALU.add))
                step(v.tensor_copy(hi_i[:, :], rank[:, :]))
                step(v.tensor_scalar(lo_i[:, :], hi_i[:, :], P - 1, None, ALU.bitwise_and))
                step(v.tensor_scalar(hi_i[:, :], hi_i[:, :], 7, None, ALU.arith_shift_right))
                v.scalar_tensor_tensor(row[k][:, :], lo_i[:, :], float(ST), hi_i[:, :], ALU.mult, ALU.add).then_inc(sem("s_row"), 1)
                step(v.tensor_tensor(gcmp, expand(gend[:, :], 1, NG), expand(iota[:, :], 2, NT), ALU.is_le))
                step(v.tensor_reduce(gsum[:, :], gcmp, AX.X, ALU.add))
                step(v.tensor_scalar(bin_of[:, :], gsum[:, :], float(NT - 1), None, ALU.min))
                dve.wait_ge(sem("s_small"), 6)
                dve.wait_ge(sem("s_row"), k + 1)
                v.memset(before[:, :], 0.0).then_inc(sem("s_rows"), 1)

            bins(0, edge_src[:, :, 1], bin_s, 0)
            bins(1, edge_small[:, :, C_LOC], bin_d, 1)
            dve.wait_ge(sem("s_rows"), 2)
            step(v.memset(acc[:, 0:NT * D], 0.0))
            v.memset(before[:, :], 0.0).then_inc(sem("s_binned"), 1)

            def bin_registers(table_of, i):
                _, r = nc.values_load_multi_w_load_instructions(
                    table_of[0:1, bass.ds(i * 8, 8)], engines=[mybir.EngineType.DVE], min_val=0, max_val=NT - 1)
                return r

            def sums(L, oh, slot, col, table_of):
                def onehot(i, jj):
                    at_t = ahead(i, jj, U, TURNS)
                    if at_t is None:
                        return
                    turn, j, T = at_t
                    h, k = divmod(j, H8)
                    dve.wait_ge(sem(f"L{L}_slot"), turn * 2 + h + 1)
                    wait(dve, sem(f"L{L}_seg"), T - H8 + 1)
                    if L == 0:
                        ins = v.tensor_scalar(oh[:, k, :], iota[:, 0:P], slot[:, h, k, 1:2], slot[:, h, k, 2:3],
                                              ALU.is_equal, ALU.mult)
                    else:
                        ins = v.tensor_scalar(oh[:, k, :], iota[:, 0:P], slot[:, h, k, col:col + 1], None, ALU.is_equal)
                    ins.then_inc(sem(f"L{L}_oh"), 1)

                for T in range(4):
                    onehot(0, T)

                def body(i):
                    regs = bin_registers(table_of, i)
                    for j in range(U):
                        T = i * U + j
                        onehot(i, j + 4)
                        if j % 2:
                            dve.wait_ge(sem(f"L{L}_seg"), T + 1)
                            G = i * 8 + j // 2
                            b = j // 2 % 2
                            wait(dve, sem(f"L{L}_acc"), G)
                            at = acc_n[:, bass.ds(regs[j // 2], 1), :]
                            if L == 3:
                                d = deg[:, bass.ds(regs[j // 2], 1)]
                                v.tensor_tensor(d, d, bank[2 + b][:, 0:1], ALU.add)
                            v.tensor_tensor(at, at, bank[b][:, :], ALU.add).then_inc(sem(f"L{L}_acc"), 1)

                turns(dve, TURNS, body)

            sums(0, oh0, slot0, 1, bin_s)

            def norm(L, n, s, z, out):
                v.bn_stats(stats[:, s, :], z).then_inc(sem(f"L{L}_bs"), 1)
                dve.wait_ge(sem(f"L{L}_bs"), n + 1)
                gate(dve, "dve")
                v.bn_aggr(mv[:, s, :], stats[:, s, :]).then_inc(sem(f"L{L}_mv"), 1)
                dve.wait_ge(sem(f"L{L}_std"), n + 1)
                v.reciprocal(rstd[:, s:s + 1], std[:, s:s + 1]).then_inc(sem(f"L{L}_rs"), 1)
                dve.wait_ge(sem(f"L{L}_rs"), n + 1)
                dve.wait_ge(sem(f"L{L}_mv"), n + 1)
                return v.tensor_scalar(out, z, mv[:, s, 0:1], rstd[:, s:s + 1], ALU.subtract, ALU.mult)

            dve.wait_ge(sem("s_x"), 16)

            def nodes0(i):
                for s in range(2):
                    n = i * 2 + s
                    z = dense0[:, 4 + s, :]
                    dve.wait_ge(sem("L0_mm"), n + 1)
                    v.tensor_tensor(z, bank[4 + s][:, :], x_res[:, bass.ds(n, 1), :], ALU.add).then_inc(sem("L0_z"), 1)
                    dve.wait_ge(sem("L0_z"), n + 1)
                    norm(0, n, s, z, x_res[:, bass.ds(n, 1), :]).then_inc(sem("L0_x"), 1)

            turns(dve, NT // 2, nodes0)

            step(v.memset(acc[:, 0:NT * D], 0.0))
            dve.wait_ge(sem("s_we"), 16 * 6)
            step(v.tensor_scalar(eps1[:, :], eps1[:, :], 1.0, None, ALU.add))

            def add1(i, jj):
                at_t = ahead(i, jj, U, TURNS)
                if at_t is None:
                    return
                turn, j, T = at_t
                h, k = divmod(j, H8)
                dve.wait_ge(sem(f"L1_chunk{h}"), turn * 16 + 16)
                wait(dve, sem("L1_seg"), T - H8 + 1)
                v.tensor_scalar(oh1[:, k, :], iota[:, 0:P], chunk[:, h, k, EA + C_LOC:EA + C_LOC + 1], None, ALU.is_equal)\
                    .then_inc(sem("L1_oh"), 1)
                dve.wait_ge(sem("L1_mm"), T + 1)
                dve.wait_ge(sem(f"gath{k}"), G_ALL + turn * 32 + 16 * h + 16)
                wait(dve, sem("L1_seg"), T - 3)
                v.tensor_tensor(msg[j % 4][:, :], bank[j % 4][:, :], gath[k][:, :], ALU.add).then_inc(sem("L1_add"), 1)

            for T in range(3):
                add1(0, T)

            def edges1(i):
                regs = bin_registers(bin_d, i)
                for j in range(U):
                    T = i * U + j
                    add1(i, j + 3)
                    if j % 2:
                        dve.wait_ge(sem("L1_seg"), T + 1)
                        wait(dve, sem("L1_acc"), i * 8 + j // 2)
                        at = acc_n[:, bass.ds(regs[j // 2], 1), :]
                        v.tensor_tensor(at, at, bank[4 + j // 2 % 2][:, :], ALU.add).then_inc(sem("L1_acc"), 1)

            turns(dve, TURNS, edges1)

            dve.wait_ge(sem("L1_acc"), NG)

            def own1(i):
                for s in range(2):
                    n = i * 2 + s
                    wait(dve, sem("L1_ntr"), n - 1)
                    v.scalar_tensor_tensor(gath[s][:, :], x_res[:, bass.ds(n, 1), :], eps1[:, 0:1], acc_n[:, bass.ds(n, 1), :],
                                           ALU.mult, ALU.add).then_inc(sem("L1_hs"), 1)

            turns(dve, NT // 2, own1)

            def batch(count_of, src, nf, evs):
                def body(c):
                    for f in range(nf):
                        dve.wait_ge(sem(evs), c * nf + f + 1)
                        v.bn_stats(bst[:, f, bass.ds(c, 1), :], src[:, f, bass.ds(c * 512, 512)]).then_inc(sem(f"L1_bst{nf}"), 1)

                turns(dve, 4, body)
                dve.wait_ge(sem(f"L1_bst{nf}"), 4 * nf)
                for f in range(nf):
                    ins = v.bn_aggr(bmv[:, f, :], bst[:, f, :, :].rearrange("p c s -> p (c s)"))
                ins.then_inc(sem("L1_bmv"), 1)
                dve.wait_ge(sem("L1_bstd"), count_of)
                g, be = (g1, be1) if nf == 8 else (g2, be2)
                sc, sh, tm = bscale[:, 0:nf], bshift[:, 0:nf], btmp[:, 0:nf]
                step(v.reciprocal(tm, bstd[:, 0:nf]))
                step(v.tensor_tensor(sc, tm, g, ALU.mult))
                step(v.tensor_tensor(tm, bmv[:, 0:nf, 0], sc, ALU.mult))
                v.tensor_tensor(sh, be, tm, ALU.subtract).then_inc(sem("L1_bn"), 1)

            batch(1, aT, 8, "L1_ev1")
            batch(2, hT, 4, "L1_ev2")

            def back1(i):
                for s in range(2):
                    n = i * 2 + s
                    at = x_res[:, bass.ds(n, 1), :]
                    dve.wait_ge(sem("L1_btr"), n + 1)
                    v.tensor_tensor(at, at, bank[s][:, :], ALU.add).then_inc(sem("L1_z"), 1)
                    dve.wait_ge(sem("L1_z"), n + 1)
                    v.bn_stats(nst[:, bass.ds(n, 1), :], x_res[:, bass.ds(n, 1), :]).then_inc(sem("L1_nst"), 1)

            turns(dve, NT // 2, back1)
            dve.wait_ge(sem("L1_nst"), NT)
            for n in range(NT):
                ins = v.bn_aggr(nmv[:, n, :], nst[:, n, :])
            ins.then_inc(sem("L1_mv"), 1)
            dve.wait_ge(sem("L1_std"), 1)
            step(v.reciprocal(nstd[:, :], nstd[:, :]))

            def norm1(i):
                for s in range(2):
                    n = i * 2 + s
                    wait(dve, sem("L1_utr"), n - 1)
                    wait(dve, sem("L1_x"), n - 1)
                    v.tensor_scalar(gath[4 + s][:, :], x_res[:, bass.ds(n, 1), :], nmv[:, bass.ds(n, 1), 0:1],
                                    nstd[:, bass.ds(n, 1)], ALU.subtract, ALU.mult).then_inc(sem("L1_xn"), 1)

            turns(dve, NT // 2, norm1)

            dve.wait_ge(sem("s_az"), 1)
            dve.wait_ge(sem("L1_x"), NT)

            def onehot2(i, jj):
                at_t = ahead(i, jj, U, TURNS)
                if at_t is None:
                    return
                turn, j, T = at_t
                h, k = divmod(j, H8)
                dve.wait_ge(sem("L2_slot"), turn * 2 + h + 1)
                wait(dve, sem("L2_seg"), T - 3)
                v.tensor_scalar(oh2[:, j % 4, 4, :], iota[:, 0:P], slot2[:, h, k, C_LOC:C_LOC + 1], None, ALU.is_equal)\
                    .then_inc(sem("L2_oh"), 1)

            def products2(i, jj):
                at_t = ahead(i, jj, U, TURNS)
                if at_t is None:
                    return
                turn, j, T = at_t
                h, k = divmod(j, H8)
                w, s, q, t, y = bank[4 + j % 2], gath[k], prod[j % 4], dot[j % 2], slot2[:, h, k, :]
                dve.wait_ge(sem("L2_dot"), T + 1)
                wait(dve, sem("L2_seg"), T - 3)
                v.scalar_tensor_tensor(t[:, :], s[:, 2 * P:3 * P], y[:, C_Y + 2:C_Y + 3], t[:, :], ALU.mult, ALU.add)\
                    .then_inc(sem("L2_t"), 1)
                dve.wait_ge(sem("L2_w"), T + 1)
                v.tensor_tensor(q[:, 0:2, :], w[:, 0:2 * P].rearrange("p (a c) -> p a c", a=2), expand(s[:, 0:P], 1, 2), ALU.mult)
                dve.wait_ge(sem("L2_t"), T * 2 + 1)
                v.scalar_tensor_tensor(t[:, :], s[:, 3 * P:4 * P], y[:, C_Y + 3:C_Y + 4], t[:, :], ALU.mult, ALU.add)\
                    .then_inc(sem("L2_t"), 1)
                v.tensor_tensor(q[:, 2:5, :], expand(w[:, 2 * P:3 * P], 1, 3),
                                s[:, P:4 * P].rearrange("p (m c) -> p m c", m=3), ALU.mult)
                dve.wait_ge(sem("L2_t"), T * 2 + 2)
                v.scalar_tensor_tensor(q[:, 5, :], t[:, :], 3.0 ** -0.5, w[:, 3 * P:4 * P], ALU.mult, ALU.mult)\
                    .then_inc(sem("L2_prod"), 1)

            for T in range(3):
                onehot2(0, T)
            products2(0, 0)

            def edges2(i):
                regs = bin_registers(bin_d, i)
                for j in range(U):
                    T = i * U + j
                    products2(i, j + 1)
                    if j % 2:
                        b = j // 2 % 2
                        dve.wait_ge(sem("L2_seg"), T + 1)
                        wait(dve, sem("L2_acc"), i * 8 + j // 2)
                        for part in range(2):
                            at = acc2[:, bass.ds(regs[j // 2], 1), D * part:D * part + D]
                            ins = v.tensor_tensor(at, at, bank[2 * part + b][:, :], ALU.add)
                        ins.then_inc(sem("L2_acc"), 1)
                    onehot2(i, j + 3)

            turns(dve, TURNS, edges2)

            def nodes2(i):
                for s in range(2):
                    n = i * 2 + s
                    z, x = dz[s], x_res[:, bass.ds(n, 1), :].rearrange("p o d -> p (o d)")
                    dve.wait_ge(sem("L2_mm"), n + 1)
                    v.scalar_tensor_tensor(z[:, 0:P], bank[4 + s][:, 0:P], C_OUT, x[:, 0:P], ALU.mult, ALU.add)
                    v.scalar_tensor_tensor(z[:, P:D].rearrange("p (u m) -> p u m", m=3),
                                           bank[4 + s][:, P:D].rearrange("p (m u) -> p u m", m=3), C_OUT,
                                           x[:, P:D].rearrange("p (u m) -> p u m", m=3), ALU.mult, ALU.add).then_inc(sem("L2_nz"), 1)
                    dve.wait_ge(sem("L2_nz"), n + 1)
                    norm(2, n, s, z[:, :], x_res[:, bass.ds(n, 1), :]).then_inc(sem("L2_x"), 1)

            turns(dve, NT // 2, nodes2)

            dve.wait_ge(sem("s_az"), 2)
            dve.wait_ge(sem("s_ones"), 4)
            sums(3, oh3, slot3, C_LOC, bin_d)
            dve.wait_ge(sem("L3_acc"), NG)
            step(v.tensor_scalar(deg[:, :], deg[:, :], 1.0, None, ALU.max))
            step(v.reciprocal(rdeg[:, :], deg[:, :]))

            def mean3(i, ss):
                at_n = ahead(i, ss, 2, NT // 2)
                if at_n is None:
                    return
                _, s, n = at_n
                wait(dve, sem("L3_ntr"), n - 1)
                v.tensor_scalar(dn[s][:, 4:8, :], acc_n[:, bass.ds(n, 1), :].rearrange("p o (k c) -> p (o k) c", k=4),
                                rdeg[:, bass.ds(n, 1)], None, ALU.mult).then_inc(sem("L3_hs"), 1)

            mean3(0, 0)
            mean3(0, 1)
            dve.wait_ge(sem("s_w3"), 64)

            def nodes3(i):
                for s in range(2):
                    n = i * 2 + s
                    z, y = dz[s][:, :], dy[s][:, :]
                    mean3(i, s + 2)
                    dve.wait_ge(sem("L3_mm"), n + 1)
                    v.tensor_tensor(z, bank[4 + s][:, :], bias3, ALU.add).then_inc(sem("L3_z"), 1)
                    dve.wait_ge(sem("L3_z"), n + 1)
                    norm(3, n * 2, 0, z, z).then_inc(sem("L3_n"), 1)
                    dve.wait_ge(sem("L3_n"), n * 4 + 1)
                    v.tensor_tensor(z, z, gamma3, ALU.mult).then_inc(sem("L3_n"), 1)
                    dve.wait_ge(sem("L3_n"), n * 4 + 2)
                    v.tensor_tensor(z, z, beta3, ALU.add).then_inc(sem("L3_n"), 1)
                    dve.wait_ge(sem("L3_n"), n * 4 + 3)
                    v.tensor_tensor(z, z, x_res[:, bass.ds(n, 1), :], ALU.add).then_inc(sem("L3_n"), 1)
                    dve.wait_ge(sem("L3_n"), n * 4 + 4)
                    wait(dve, sem(f"L3_st{s}"), i * 16)
                    norm(3, n * 2 + 1, 1, z, y).then_inc(sem("L3_y"), 1)

            turns(dve, NT // 2, nodes3)


_INS = ["src", "dst", "x", "edge_attr_4", "edge_attr_64", "edge_attr_8", "edge_weight", "L1_gnn_W_e", "L1_gnn_b_e",
        "L1_gnn_W1", "L1_gnn_W2", "L2_gnn_W_up0", "L2_gnn_W_up1", "L2_gnn_W_mlp1", "L2_gnn_W_mlp2", "L2_gnn_W_mlp3",
        "L2_gnn_W_mlp4", "L2_gnn_W_out0", "L2_gnn_W_out1"]


def kernel(**inputs):
    import numpy as np
    import concourse.bacc as bacc
    from concourse.bass_utils import run_bass_kernel_spmd

    arrays = {name: np.ascontiguousarray(inputs[name]) for name in _INS}
    arrays["w0"] = np.ascontiguousarray(np.asarray(inputs["L0_gnn_weight"]).T)
    arrays["w3"] = np.ascontiguousarray(np.concatenate(
        [np.asarray(inputs["L3_gnn_W_self"]).T, np.asarray(inputs["L3_gnn_W_neigh"]).T]))
    columns = [np.asarray(inputs[f"L1_gnn_{k}"]).reshape(-1, P).T for k in ("b1", "g1", "beta1", "b2", "g2", "beta2")]
    arrays["bn"] = np.ascontiguousarray(np.concatenate(columns, axis=1))
    arrays["eps"] = np.ascontiguousarray(np.broadcast_to(np.asarray(inputs["L1_gnn_eps"]), (P, 1)))
    for k in ("bias", "gamma", "beta"):
        arrays[k] = np.ascontiguousarray(np.broadcast_to(np.asarray(inputs[f"L3_gnn_{k}"]), (P, D)))

    nc = bacc.Bacc("TRN2", target_bir_lowering=False, num_devices=1)
    aps = {name: nc.dram_tensor(f"in_{name}", v.shape, mybir.dt.from_np(v.dtype), kind="ExternalInput").ap()
           for name, v in arrays.items()}
    aps["out"] = nc.dram_tensor("out", (N, D), F32, kind="ExternalOutput").ap()
    build(nc, aps)
    r = run_bass_kernel_spmd(nc, [{f"in_{name}": v for name, v in arrays.items()}], core_ids=[0])
    return r.results[0]["out"]
```

```python
from contextlib import ExitStack

import concourse.bass as bass
from concourse import mybir

F32 = mybir.dt.float32
I32 = mybir.dt.int32
F32R = mybir.dt.float32r
ALU = mybir.AluOpType
ACT = mybir.ActivationFunctionType
AX = mybir.AxisListType

P = 128
N = 2048
D = 512
E = 32768
NT = N // P
ET = E // P
GROUP = 2 * P
NG = E // GROUP + NT
ST = NG * GROUP // P
U = 16
H8 = 8
PADS = ST - ET
TURNS = ST // U
ETURNS = ET // U
G_ALL = 16 * ST // H8
EA, EF, NY = 64, 8, 4
SMALL = 16
C_EF, C_Y, C_SRC, C_LOC = 0, EF, EF + NY, EF + NY + 1
ROW = EA + SMALL
HID = 1024
LN_EPS = 1e-5
SILU_2MOM = 1.679177
SB = D


def wait(eng, sem, value):
    if isinstance(value, int) and value <= 0:
        return
    eng.wait_ge(sem, value)


def turns(eng, n, body):
    body(0)
    with eng.Fori(1, n - 1) as i:
        body(i)
    body(n - 1)


def ahead(turn, k, per, end):
    turn_k = turn + k // per if k // per else turn
    if isinstance(turn_k, int) and turn_k >= end:
        return None
    return turn_k, k % per, turn * per + k


def expand(ap, axis, n):
    shape = list(ap.shape)
    return ap.unsqueeze(axis).broadcast_to(shape[:axis] + [n] + shape[axis:])


class Chain:

    def __init__(self, eng, sem):
        self.eng, self.sem, self.n = eng, sem, 0

    def __call__(self, ins):
        ins.then_inc(self.sem, 1)
        self.n += 1
        self.eng.wait_ge(self.sem, self.n)


def build(nc, a):
    ctx = ExitStack()
    with ctx:
        def sb(name, shape, dt=F32, at=ctx):
            return at.enter_context(nc.sbuf_tensor(name, shape, dt))

        sems = {}

        def sem(name):
            if name not in sems:
                sems[name] = ctx.enter_context(nc.semaphore(name))
            return sems[name]

        def gate(eng, name):
            eng.sem_inc(sem(f"gate_{name}"), 1)

        slots_d = nc.dram_tensor("slots_by_dst", [P * ST, ROW], F32, kind="Internal").ap()
        table = [nc.dram_tensor(f"nodes_{k}", [N, D], F32, kind="Internal").ap() for k in (1, 2, 3)]
        proj0 = nc.dram_tensor("projected_0", [N, D], F32, kind="Internal").ap()
        slots_d_v = slots_d.rearrange("(p t) c -> p t c", p=P)

        x_res = sb("x_res", [P, NT, D])
        acc = sb("acc", [P, NT * 2 * D])
        small = sb("small", [P, ST, SMALL])
        gath = [sb(f"gath{k}", [P, D]) for k in range(H8)]
        wbuf = sb("wbuf", [P, 8192])
        we_hi = sb("we_hi", [P, D], F32R)
        we_lo = sb("we_lo", [P, D], F32R)
        be = sb("be", [P, D])
        wup = sb("wup", [P, 2, P])
        ident = sb("ident", [P, P])
        iota = sb("iota", [P, ST])
        bin_s = sb("bin_s", [P, NG], I32)
        bin_d = sb("bin_d", [P, NG], I32)
        idx = sb("idx", [P, 2, H8], I32)
        stats = sb("stats", [P, 2, 6])
        mv = sb("mv", [P, 2, 2])
        std = sb("std", [P, 2])
        rstd = sb("rstd", [P, 2])
        eps_ln = sb("eps_ln", [P, 1])
        rdeg = sb("rdeg", [P, NT])
        ones2 = sb("ones2", [P, 2])
        deg = sb("deg", [P, NT])
        eps1 = sb("eps1", [P, 1])
        bn_in = sb("bn_in", [P, 36])
        bank = [ctx.enter_context(nc.psum_tensor(f"bank{k}", [P, 512], F32)) for k in range(8)]

        edge_small = acc[:, 12288:16384].rearrange("p (t c) -> p t c", c=SMALL)
        is_bin = acc[:, 0:4096].rearrange("p (b t) -> p b t", b=NT)
        count = acc[:, 4096:8192].rearrange("p (b t) -> p b t", b=NT)
        slots0 = acc[:, 8192:8192 + 4 * ST].rearrange("p (t c) -> p t c", c=4)
        pad_in = acc[:, 11264:11264 + PADS * NT].rearrange("p (t b) -> p t b", b=NT)
        acc_n = acc[:, 0:NT * D].rearrange("p (n d) -> p n d", d=D)

        s0 = ExitStack()
        key = [sb(f"key{k}", [P, ET], I32, s0) for k in range(2)]
        hi_i = sb("hi_i", [P, ET], I32, s0)
        lo_i = sb("lo_i", [P, ET], I32, s0)
        hi_f = sb("hi_f", [P, ET], F32, s0)
        rank = sb("rank", [P, ET], F32, s0)
        row = sb("row", [P, ET], I32, s0)
        w_in = sb("w_in", [P, ET], F32, s0)
        tile_f = sb("tile_f", [P, ET], F32, s0)
        lane_f = sb("lane_f", [P, ET], F32, s0)
        dst_f = sb("dst_f", [P, ET], F32, s0)
        loc_f = sb("loc_f", [P, ET], F32, s0)
        w_hi = sb("w_hi", [P, ET], F32R, s0)
        w_lo = sb("w_lo", [P, ET], F32, s0)
        tri = sb("tri", [P, P], F32, s0)
        ones = sb("ones", [P, P], F32, s0)
        pad_d = sb("pad_d", [P, ROW], F32, s0)
        pad_n = sb("pad_n", [P, PADS], F32, s0)
        pad_row = sb("pad_row", [P, PADS], I32, s0)
        pad_f = sb("pad_f", [P, PADS], F32, s0)
        pad_lane = sb("pad_lane", [P, PADS], I32, s0)
        held = sb("held", [P, NT], F32, s0)
        pads_from = sb("pads_from", [P, NT], F32, s0)
        before = sb("before", [P, NT], F32, s0)
        rcount = sb("rcount", [P, NT], F32, s0)
        tot_i = sb("tot_i", [P, NT], I32, s0)
        grp_i = sb("grp_i", [P, NT], I32, s0)
        grp = sb("grp", [P, NT], F32, s0)
        gend = sb("gend", [P, NT], F32, s0)
        off = sb("off", [P, NT], F32, s0)
        gsum = sb("gsum", [P, NG], F32, s0)
        stage_d = sb("stage_d", [P, 2, H8, ROW], F32, s0)
        drow = sb("drow", [P, 2, H8], I32, s0)
        slot0 = sb("slot0", [P, 2, H8, 4], F32, s0)
        of_tile = [sb(f"of_tile{k}", [P, ST], F32R, s0) for k in range(4)]
        of_lane = [sb(f"of_lane{k}", [P, 4, P], F32R, s0) for k in range(4)]
        s0.close()
        small_flat = small[:, :, :].rearrange("p t c -> p (t c)")
        dense0 = small_flat[:, 0:6 * D].rearrange("p (b d) -> p b d", b=6)
        oh0 = small_flat[:, 6 * D:6 * D + H8 * P].rearrange("p (k n) -> p k n", k=H8)
        in_lane = small_flat[:, 6 * D + H8 * P:6 * D + H8 * P + 4 * P].rearrange("p (k n) -> p k n", k=4)
        ef_in = dense0[:, 0:4, :].rearrange("p a (t c) -> p (a t) c", c=EF)
        y_in = dense0[:, 4:6, :].rearrange("p a (t c) -> p (a t) c", c=NY)
        gcmp = acc[:, 8192:8192 + NG * NT].rearrange("p (g b) -> p g b", b=NT)

        s1 = ExitStack()
        chunk = sb("chunk", [P, 2, H8, ROW], F32, s1)
        parts = [sb(f"parts{k}", [P, H8, 2 * EA], F32R, s1) for k in range(2)]
        rowT = [sb(f"rowT{k}", [P, 4 * P], F32R, s1) for k in range(4)]
        msg = [sb(f"msg{k}", [P, D], F32, s1) for k in range(4)]
        oh1 = sb("oh1", [P, H8, P], F32, s1)
        s1.close()
        s1d = ExitStack()
        hT = sb("hT", [P, 4, N], F32, s1d)
        bst = sb("bst", [P, 8, 4, 6], F32, s1d)
        bmv = sb("bmv", [P, 8, 2], F32, s1d)
        bstd = sb("bstd", [P, 8], F32, s1d)
        bscale = sb("bscale", [P, 8], F32, s1d)
        bshift = sb("bshift", [P, 8], F32, s1d)
        btmp = sb("btmp", [P, 8], F32, s1d)
        nst = sb("nst", [P, NT, 6], F32, s1d)
        nmv = sb("nmv", [P, NT, 2], F32, s1d)
        nstd = sb("nstd", [P, NT], F32, s1d)
        s1d.close()
        aT = acc[:, :].rearrange("p (f n) -> p f n", f=8)
        s2 = ExitStack()
        slot2 = sb("slot2", [P, 2, H8, SMALL], F32, s2)
        efT = sb("efT", [P, P], F32, s2)
        hid = [sb(f"hid{k}", [P, 4 * P], F32, s2) for k in range(4)]
        prod = [sb(f"prod{k}", [P, 6, P], F32, s2) for k in range(4)]
        dot = [sb(f"dot{k}", [P, P], F32, s2) for k in range(2)]
        oh2 = sb("oh2", [P, 4, 5, P], F32, s2)
        s2.close()
        s2d = ExitStack()
        dn = [sb(f"dn{k}", [P, 8, P], F32, s2d) for k in range(2)]
        dnT = [sb(f"dnT{k}", [P, 8, P], F32, s2d) for k in range(2)]
        dz = [sb(f"dz{k}", [P, D], F32, s2d) for k in range(2)]
        dy = [sb(f"dy{k}", [P, D], F32, s2d) for k in range(2)]
        s2d.close()
        s3 = ExitStack()
        slot3 = sb("slot3", [P, 2, H8, SMALL], F32, s3)
        oh3 = sb("oh3", [P, H8, P], F32, s3)
        s3.close()
        iota_b = iota[:, 0:NT]
        b1, g1, be1 = (bn_in[:, 8 * k:8 * k + 8] for k in range(3))
        b2, g2, be2 = (bn_in[:, 24 + 4 * k:28 + 4 * k] for k in range(3))

        w0 = wbuf[:, 0:2048].rearrange("p (k n) -> p k n", k=4)
        w1 = wbuf[:, 0:4096].rearrange("p (k n) -> p k n", k=4)
        w2 = wbuf[:, 4096:8192].rearrange("p (k n) -> p k n", k=8)
        we_f = wbuf[:, 2048:2560]
        m1 = wbuf[:, 0:512].rearrange("p (j n) -> p j n", j=4)
        m2 = wbuf[:, 512:640]
        m3 = wbuf[:, 640:768]
        m4 = wbuf[:, 768:1792].rearrange("p (e n) -> p e n", e=2)
        wo = wbuf[:, 1792:2304].rearrange("p (k n) -> p k n", k=4)
        w3 = wbuf[:, 0:4096].rearrange("p (k n) -> p k n", k=8)
        bias3, gamma3, beta3 = (wbuf[:, 4096 + D * k:4096 + D * (k + 1)] for k in range(3))

        acc2 = acc[:, :].rearrange("p (n d) -> p n d", d=2 * D)
        C1, C2 = 1.0 / EF ** 0.5, SILU_2MOM / 8.0
        C_OUT = C2 / (16.0 * 10.0)

        block = ctx.enter_context(nc.Block())

        @block.sync
        def _(sp):
            def load(dst, src, name):
                sp.dma_start(dst, src).then_inc(sem(name), 16)

            for k, name in ((0, "src"), (1, "dst")):
                load(key[k][:, :], a[name].rearrange("(p t) -> p t", p=P), f"s_key{k}")
            load(ef_in, a["edge_attr_8"].rearrange("(p t) c -> p t c", p=P), "s_attr")
            load(y_in, a["edge_attr_4"].rearrange("(p t) c -> p t c", p=P), "s_attr")
            load(w_in[:, :], a["edge_weight"].rearrange("(p t) -> p t", p=P), "s_w")
            load(x_res[:, :, :], a["x"].rearrange("(n p) d -> p n d", p=P), "s_x")
            load(w0, a["w0"].rearrange("(k p) n -> p k n", p=P), "s_w0")
            for k in range(2):
                load(we_f[EA * k:EA * k + EA, :], a["L1_gnn_W_e"], "s_we")
            load(be[:, :], a["be"], "s_we")
            load(bn_in[:, :], a["bn"], "s_we")
            load(eps1[:, :], a["eps"], "s_we")
            for k in range(2):
                load(wup[:, k, :], a[f"L2_gnn_W_up{k}"], "s_wup")

            sp.wait_ge(sem("s_rows"), 1)

            def stage_dst(i):
                for h in range(2):
                    t0 = i * U + h * H8
                    wait(sp, sem(f"s_scat_d{h}"), i * (16 * H8))
                    gate(sp, "sp")
                    s = sem(f"s_stage_d{h}")
                    sp.dma_start(stage_d[:, h, :, 0:EA],
                                 a["edge_attr_64"].rearrange("(p t) c -> p t c", p=P)[:, bass.ds(t0, H8), :]).then_inc(s, 16)
                    sp.dma_start(stage_d[:, h, :, EA:ROW], edge_small[:, bass.ds(t0, H8), :]).then_inc(s, 16)
                    sp.dma_start(drow[:, h], row[:, bass.ds(t0, H8)]).then_inc(s, 16)

            turns(sp, ETURNS, stage_dst)

            sp.wait_ge(sem("L0_mm"), NT)
            sp.wait_ge(sem("s_wsplit"), 2)
            load(w1, a["L1_gnn_W1"].rearrange("(k p) n -> p k n", p=P), "s_w1")
            load(w2, a["L1_gnn_W2"].rearrange("(k p) n -> p k n", p=P), "s_w1")

            sp.wait_ge(sem("s_pads"), 16 * PADS)
            for h in range(2):
                sp.wait_ge(sem(f"s_scat_d{h}"), 16 * H8 * ETURNS)

            def chunks(i):
                for h in range(2):
                    H = i * 2 + h
                    wait(sp, sem("L1_part"), (H - 1) * 2)
                    gate(sp, "sp")
                    wait(sp, sem("L1_idx"), H - 1)
                    gate(sp, "sp")
                    sp.dma_start(chunk[:, h], slots_d_v[:, bass.ds(H * H8, H8), :]).then_inc(sem(f"L1_chunk{h}"), 16)

            turns(sp, TURNS, chunks)

            sp.wait_ge(sem("L1_h2"), 16)
            sp.wait_ge(sem("s_wz"), 1)
            for k in range(H8):
                j, e = divmod(k, 2)
                load(m1[16 * k + C_EF:16 * k + C_EF + EF, j, 64 * e:64 * e + 64], a["L2_gnn_W_mlp1"], "s_w2")
            for e in range(2):
                load(m2[64 * e:64 * e + 64, 64 * e:64 * e + 64], a["L2_gnn_W_mlp2"], "s_w2")
                load(m3[64 * e:64 * e + 64, 64 * e:64 * e + 64], a["L2_gnn_W_mlp3"], "s_w2")
                for q, to in ((1, 0), (0, 1), (2, 2), (3, 3)):
                    load(m4[64 * e:64 * e + 64, e, P * to:P * to + P], a["L2_gnn_W_mlp4"][:, P * q:P * q + P], "s_w2")
            for k in range(2):
                load(wo[:, 2 * k:2 * k + 2, :], a[f"L2_gnn_W_out{k}"].rearrange("(k p) n -> p k n", p=P), "s_w2")

            def up(i):
                for s in range(2):
                    n = i * 2 + s
                    sp.wait_ge(sem("L1_ub"), n + 1)
                    gate(sp, "sp")
                    sp.dma_start(table[1][bass.ds(n * P, P), :], gath[s][:, :]).then_inc(sem(f"L1_st{s}"), 16)

            turns(sp, NT // 2, up)

            def nodes3(i):
                for s in range(2):
                    n = i * 2 + s
                    sp.wait_ge(sem("L2_x"), n + 1)
                    gate(sp, "sp")
                    sp.dma_start(table[2][bass.ds(n * P, P), :], x_res[:, bass.ds(n, 1), :]).then_inc(sem("L2_st"), 16)

            turns(sp, NT // 2, nodes3)
            sp.wait_ge(sem("L2_mm"), NT)
            load(w3, a["w3"].rearrange("(k p) n -> p k n", p=P), "s_w3")
            for k, name in enumerate(("bias", "gamma", "beta")):
                load((bias3, gamma3, beta3)[k], a[name], "s_w3")

            def store(i):
                for s in range(2):
                    n = i * 2 + s
                    sp.wait_ge(sem("L3_y"), n + 1)
                    gate(sp, "sp")
                    sp.dma_start(a["out"][bass.ds(n * P, P), :], dy[s][:, :]).then_inc(sem(f"L3_st{s}"), 16)

            turns(sp, NT // 2, store)
            for s in range(2):
                sp.wait_ge(sem(f"L3_st{s}"), 16 * (NT // 2))

        @block.gpsimd
        def _(pool):
            pool.memset(pad_d[:, :], 0.0).then_inc(sem("s_pad0"), 1)
            pool.iota(iota[:, :], [[1, ST]], 0, 0, True).then_inc(sem("s_iota"), 1)
            pool.iota(pad_n[:, :], [[1, PADS]], 0, PADS, True).then_inc(sem("s_iota"), 1)
            pool.wait_ge(sem("s_pad0"), 1)
            pool.memset(pad_d[:, EA + C_LOC:EA + C_LOC + 1], -1.0).then_inc(sem("s_pad"), 1)
            pool.memset(edge_small[:, :, :], 0.0).then_inc(sem("s_pad"), 1)
            pool.memset(ident[:, :], 0.0).then_inc(sem("s_id"), 1)
            pool.memset(tri[:, :], 0.0).then_inc(sem("s_id"), 1)
            pool.memset(ones[:, :], 1.0).then_inc(sem("s_ones"), 1)
            pool.memset(ones2[:, :], 1.0).then_inc(sem("s_ones"), 1)
            pool.memset(eps_ln[:, :], LN_EPS).then_inc(sem("s_ones"), 1)
            pool.memset(deg[:, :], 0.0).then_inc(sem("s_ones"), 1)
            pool.wait_ge(sem("s_id"), 2)
            pool.affine_select(out=ident[:, :], in_=ident[:, :], compare_op=ALU.not_equal, fill=1.0, base=0,
                               pattern=[[-1, P]], channel_multiplier=1).then_inc(sem("s_id"), 1)
            pool.affine_select(out=tri[:, :], in_=tri[:, :], compare_op=ALU.is_ge, fill=1.0, base=0,
                               pattern=[[-1, P]], channel_multiplier=1).then_inc(sem("s_id"), 1)

            def scatter(i):
                for h in range(2):
                    pool.wait_ge(sem(f"s_stage_d{h}"), i * 48 + 48)
                    gate(pool, "pool")
                    for k in range(H8):
                        pool.indirect_dma_start(slots_d, bass.IndirectOffsetOnAxis(ap=drow[:, h, k:k + 1], axis=0),
                                                stage_d[:, h, k, :], None).then_inc(sem(f"s_scat_d{h}"), 16)

            def gather(L, source, ready, total, free):
                def body(i):
                    for j in range(U):
                        h, k = divmod(j, H8)
                        T = i * U + j
                        pool.wait_ge(sem(f"L{L}_idx"), i * 2 + h + 1)
                        wait(pool, sem(f"L{L}_{free}"), T - H8 + 1)
                        gate(pool, "pool")
                        pool.wait_ge(sem(ready), total)
                        pool.indirect_dma_start(gath[k][:, :], None, source,
                                                bass.IndirectOffsetOnAxis(ap=idx[:, h, k:k + 1], axis=0))\
                            .then_inc(sem(f"gath{k}"), 16)

                turns(pool, TURNS, body)

            pool.wait_ge(sem("s_pad"), 2)
            for k in range(PADS):
                pool.wait_ge(sem("s_rows"), 1)
                pool.indirect_dma_start(slots_d, bass.IndirectOffsetOnAxis(ap=pad_row[:, k:k + 1], axis=0),
                                        pad_d[:, :], None).then_inc(sem("s_pads"), 16)
            turns(pool, ETURNS, scatter)
            pool.wait_ge(sem("L0_pst0"), 16 * (NT // 2))
            gather(0, proj0, "L0_pst1", 16 * (NT // 2), "seg")
            pool.wait_ge(sem("L0_st0"), 16 * (NT // 2))
            gather(1, table[0], "L0_st1", 16 * (NT // 2), "add")
            pool.wait_ge(sem("L1_h2"), 16)
            pool.memset(wbuf[:, 0:2304], 0.0).then_inc(sem("s_wz"), 1)
            pool.memset(acc[:, :], 0.0).then_inc(sem("s_az"), 1)
            pool.wait_ge(sem("L1_st0"), 16 * (NT // 2))
            gather(2, table[1], "L1_st1", 16 * (NT // 2), "prod")
            pool.wait_ge(sem("L2_hs"), NT)
            pool.memset(acc[:, 0:NT * D], 0.0).then_inc(sem("s_az"), 1)
            gather(3, table[2], "L2_st", 16 * NT, "seg")

        @block.scalar
        def _(act):
            act.wait_ge(sem("s_attr"), 32)
            act.wait_ge(sem("s_pad"), 2)
            nc.scalar.activation(edge_small[:, :, C_EF:C_EF + EF], ef_in, ACT.Copy).then_inc(sem("s_small"), 1)
            nc.scalar.activation(edge_small[:, :, C_Y:C_Y + NY], y_in, ACT.Copy).then_inc(sem("s_small"), 1)
            act.wait_ge(sem("s_key0"), 16)
            nc.scalar.activation(edge_small[:, :, C_SRC], key[0][:, :], ACT.Copy).then_inc(sem("s_small"), 1)
            act.wait_ge(sem("s_key1"), 16)
            nc.scalar.activation(dst_f[:, :], key[1][:, :], ACT.Copy).then_inc(sem("s_vals"), 1)
            act.wait_ge(sem("s_w"), 16)
            nc.scalar.activation(w_hi[:, :], w_in[:, :], ACT.Copy).then_inc(sem("s_vals"), 1)

            act.wait_ge(sem("s_small"), 3)
            act.wait_ge(sem("s_x"), 16)

            def copy0(i, ss):
                at_n = ahead(i, ss, 2, NT // 2)
                if at_n is None:
                    return
                _, s, n = at_n
                wait(act, sem("L0_tr"), n - 1)
                nc.scalar.activation(dense0[:, s, :], x_res[:, bass.ds(n, 1), :], ACT.Copy).then_inc(sem("L0_hs"), 1)

            def turned0(i, ss):
                at_n = ahead(i, ss, 2, NT // 2)
                if at_n is None:
                    return
                _, s, n = at_n
                act.wait_ge(sem("L0_tr"), n + 1)
                wait(act, sem("L0_mm"), n - 1)
                nc.scalar.activation(dense0[:, 2 + s, :], bank[6 + s][:, :], ACT.Copy).then_inc(sem("L0_hT"), 1)

            copy0(0, 0)
            copy0(0, 1)
            turned0(0, 0)

            def project0(i):
                for s in range(2):
                    n = i * 2 + s
                    copy0(i, s + 2)
                    turned0(i, s + 1)
                    act.wait_ge(sem("L0_mm"), n + 1)
                    wait(act, sem(f"L0_pst{s}"), i * 16)
                    nc.scalar.activation(dense0[:, 4 + s, :], bank[4 + s][:, :], ACT.Copy).then_inc(sem("L0_pr"), 1)
                    act.wait_ge(sem("L0_pr"), n + 1)
                    act.dma_start(proj0[bass.ds(n * P, P), :], dense0[:, 4 + s, :]).then_inc(sem(f"L0_pst{s}"), 16)

            turns(act, NT // 2, project0)

            act.wait_ge(sem("s_loc1"), 1)

            def scale0(i):
                for j in range(U):
                    t = i * U + j
                    act.wait_ge(sem("s_in_lane"), t + 1)
                    wait(act, sem("s_placed"), t - 3)
                    for value, of in enumerate((dst_f, loc_f, w_hi)[:3 - j % 2]):
                        ins = nc.scalar.activation(of_lane[j % 4][:, value, :], in_lane[:, j % 4, :], ACT.Copy,
                                                   scale=of[:, bass.ds(t, 1)].bitcast(F32))
                    ins.then_inc(sem("s_scaled"), 1)

            turns(act, ETURNS, scale0)

            act.wait_ge(sem("s_slots0"), 3)

            def idx0(i):
                for h in range(2):
                    H = i * 2 + h
                    wait(act, sem("L0_seg"), (H - 1) * H8)
                    wait(act, sem("L0_oh"), (H - 1) * H8)
                    nc.scalar.activation(slot0[:, h], slots0[:, bass.ds(H * H8, H8), :], ACT.Copy).then_inc(sem("L0_slot"), 1)
                    nc.scalar.activation(idx[:, h], slots0[:, bass.ds(H * H8, H8), 0], ACT.Copy).then_inc(sem("L0_idx"), 1)

            turns(act, TURNS, idx0)

            def root(L, n, s):
                act.wait_ge(sem(f"L{L}_mv"), n + 1)
                nc.scalar.activation(std[:, s:s + 1], mv[:, s, 1:2], ACT.Sqrt, bias=eps_ln[:, :]).then_inc(sem(f"L{L}_std"), 1)

            def nodes0(i):
                for s in range(2):
                    n = i * 2 + s
                    root(0, n, s)
                    act.wait_ge(sem("L0_y"), n + 1)
                    act.dma_start(table[0][bass.ds(n * P, P), :], dense0[:, 2 + s, :]).then_inc(sem(f"L0_st{s}"), 16)

            turns(act, NT // 2, nodes0)

            def small1(i, hh):
                at_h = ahead(i, hh, 2, TURNS)
                if at_h is None:
                    return
                turn, h, H = at_h
                act.wait_ge(sem(f"L1_chunk{h}"), turn * 16 + 16)
                wait(act, sem("L1_add"), (H - 1) * H8)
                nc.scalar.activation(small[:, bass.ds(H * H8, H8), :], chunk[:, h, :, EA:ROW], ACT.Copy).then_inc(sem("L1_small"), 1)
                nc.scalar.activation(idx[:, h], chunk[:, h, :, EA + C_SRC], ACT.Copy).then_inc(sem("L1_idx"), 1)

            def turned1(i, qq):
                at_q = ahead(i, qq, 4, TURNS)
                if at_q is None:
                    return
                turn, q, Q = at_q
                act.wait_ge(sem("L1_tr"), Q + 1)
                wait(act, sem("L1_mm"), (Q - 3) * 4)
                nc.scalar.activation(rowT[q][:, :], bank[6 + q % 2][:, :], ACT.Copy).then_inc(sem("L1_rowT"), 1)

            def relu1(i, jj):
                at_t = ahead(i, jj, U, TURNS)
                if at_t is None:
                    return
                turn, j, T = at_t
                k = j % 4
                act.wait_ge(sem("L1_add"), T + 1)
                nc.scalar.activation(msg[k][:, :], msg[k][:, :], ACT.Relu).then_inc(sem("L1_relu"), 1)

            def high1(i, hh):
                at_h = ahead(i, hh, 2, TURNS)
                if at_h is None:
                    return
                turn, h, H = at_h
                act.wait_ge(sem(f"L1_chunk{h}"), turn * 16 + 16)
                wait(act, sem("L1_tr"), (H - 1) * 2)
                nc.scalar.activation(parts[h][:, :, 0:EA], chunk[:, h, :, 0:EA], ACT.Copy).then_inc(sem("L1_high"), 1)

            for s in range(2):
                act.wait_ge(sem(f"L0_st{s}"), 16 * (NT // 2))
            high1(0, 0)
            small1(0, 0)
            high1(0, 1)
            turned1(0, 0)
            turned1(0, 1)
            for T in range(3):
                relu1(0, T)

            def edges1(i):
                for j in range(U):
                    if j % H8 == 0:
                        small1(i, j // H8 + 1)
                    if j % H8 == 4:
                        high1(i, j // H8 + 2)
                    if j % 4 == 0:
                        turned1(i, j // 4 + 2)
                    relu1(i, j + 3)

            turns(act, TURNS, edges1)

            def turned1n(i):
                for s in range(2):
                    n = i * 2 + s
                    act.wait_ge(sem("L1_ntr"), n + 1)
                    nc.scalar.activation(hT[:, :, bass.ds(n * P, P)],
                                         bank[s][:, :].rearrange("p (k n) -> p k n", k=4), ACT.Copy).then_inc(sem("L1_hT"), 1)

            turns(act, NT // 2, turned1n)

            def evac1(c):
                for f in range(8):
                    F = c * 8 + f
                    act.wait_ge(sem("L1_h1"), F + 1)
                    nc.scalar.activation(aT[:, f, bass.ds(c * 512, 512)], bank[2 + f % 4][:, :], ACT.Identity,
                                         bias=b1[:, f:f + 1]).then_inc(sem("L1_ev1"), 1)

            turns(act, 4, evac1)

            act.wait_ge(sem("L1_bmv"), 1)
            nc.scalar.activation(bstd[:, :], bmv[:, :, 1], ACT.Sqrt, bias=eps_ln[:, :]).then_inc(sem("L1_bstd"), 1)
            act.wait_ge(sem("L1_bn"), 1)

            def silu1(c):
                if isinstance(c, int) and c >= 4:
                    return
                for f in range(8):
                    at = aT[:, f, bass.ds(c * 512, 512)]
                    nc.scalar.activation(at, at, ACT.Silu, bias=bshift[:, f:f + 1], scale=bscale[:, f:f + 1])\
                        .then_inc(sem("L1_silu"), 1)

            silu1(0)

            def second1(c):
                silu1(c + 1)
                for g in range(4):
                    act.wait_ge(sem("L1_h2"), c * 4 + g + 1)
                    nc.scalar.activation(hT[:, g, bass.ds(c * 512, 512)], bank[2 + g][:, :], ACT.Identity,
                                         bias=b2[:, g:g + 1]).then_inc(sem("L1_ev2"), 1)

            turns(act, 4, second1)

            act.wait_ge(sem("L1_bmv"), 2)
            nc.scalar.activation(bstd[:, 0:4], bmv[:, 0:4, 1], ACT.Sqrt, bias=eps_ln[:, :]).then_inc(sem("L1_bstd"), 1)
            act.wait_ge(sem("L1_bn"), 2)

            def act1(i):
                for s in range(2):
                    n = i * 2 + s
                    wait(act, sem("L1_btr"), n - 1)
                    for g in range(4):
                        ins = nc.scalar.activation(gath[2 + s][:, P * g:P * g + P], hT[:, g, bass.ds(n * P, P)], ACT.Silu,
                                                   bias=bshift[:, g:g + 1], scale=bscale[:, g:g + 1])
                    ins.then_inc(sem("L1_sT"), 1)

            turns(act, NT // 2, act1)

            act.wait_ge(sem("L1_mv"), 1)
            nc.scalar.activation(nstd[:, :], nmv[:, :, 1], ACT.Sqrt, bias=eps_ln[:, :]).then_inc(sem("L1_std"), 1)

            def keep1(i, ss):
                at_n = ahead(i, ss, 2, NT // 2)
                if at_n is None:
                    return
                _, s, n = at_n
                act.wait_ge(sem("L1_xn"), n + 1)
                nc.scalar.activation(x_res[:, bass.ds(n, 1), :], gath[4 + s][:, :], ACT.Copy).then_inc(sem("L1_x"), 1)
                act.wait_ge(sem("L1_utr"), n + 1)
                wait(act, sem("L1_umm"), n - 1)
                nc.scalar.activation(gath[6 + s][:, :], bank[2 + s][:, :], ACT.Copy).then_inc(sem("L1_uT"), 1)

            keep1(0, 0)

            def up1(i):
                for s in range(2):
                    n = i * 2 + s
                    keep1(i, s + 1)
                    act.wait_ge(sem("L1_umm"), n + 1)
                    wait(act, sem(f"L1_st{s}"), i * 16)
                    nc.scalar.activation(gath[s][:, :], bank[4 + s][:, :], ACT.Copy, scale=P ** -0.5).then_inc(sem("L1_ub"), 1)

            turns(act, NT // 2, up1)

            def slots2(i, hh):
                at_h = ahead(i, hh, 2, TURNS)
                if at_h is None:
                    return
                turn, h, H = at_h
                wait(act, sem("L2_prod"), (H - 1) * H8)
                wait(act, sem("L2_tr"), H - 1)
                nc.scalar.activation(slot2[:, h], small[:, bass.ds(H * H8, H8), :], ACT.Copy).then_inc(sem("L2_slot"), 1)
                nc.scalar.activation(idx[:, h], small[:, bass.ds(H * H8, H8), C_SRC], ACT.Copy).then_inc(sem("L2_idx"), 1)

            def turned2(i, hh):
                at_h = ahead(i, hh, 2, TURNS)
                if at_h is None:
                    return
                turn, h, H = at_h
                act.wait_ge(sem("L2_tr"), H + 1)
                wait(act, sem("L2_z"), H * 3 - 2)
                nc.scalar.activation(efT[:, :], bank[7][:, 0:P], ACT.Copy).then_inc(sem("L2_efT"), 1)

            def hidden2(i, hh, k):
                at_h = ahead(i, hh, 2, TURNS)
                if at_h is None:
                    return
                turn, h, H = at_h
                act.wait_ge(sem("L2_z"), H * 3 + k + 1)
                if k == 2:
                    wait(act, sem("L2_w"), (H - 1) * H8)
                nc.scalar.activation(hid[k if k < 2 else 2 + h][:, :], bank[6][:, :], ACT.Silu,
                                     scale=C1 if k == 0 else C2).then_inc(sem("L2_h"), 1)

            def scaled2(i, jj):
                at_t = ahead(i, jj, U, TURNS)
                if at_t is None:
                    return
                turn, j, T = at_t
                h, k = divmod(j, H8)
                y = slot2[:, h, k, C_Y:C_Y + NY]
                act.wait_ge(sem("L2_oh"), T + 1)
                for m in range(4):
                    nc.scalar.activation(oh2[:, j % 4, m, :], oh2[:, j % 4, 4, :], ACT.Copy, scale=y[:, m:m + 1])\
                        .then_inc(sem("L2_ohy"), 1)
                act.wait_ge(sem(f"gath{k}"), 2 * G_ALL + turn * 32 + 16 * h + 16)
                wait(act, sem("L2_prod"), T - 1)
                nc.scalar.activation(dot[j % 2][:, :], gath[k][:, P:2 * P], ACT.Copy, scale=y[:, 1:2]).then_inc(sem("L2_dot"), 1)

            slots2(0, 0)
            turned2(0, 0)
            for k in range(3):
                hidden2(0, 0, k)
            scaled2(0, 0)
            scaled2(0, 1)

            def edges2(i):
                for j in range(U):
                    if j % H8 == 0:
                        slots2(i, j // H8 + 1)
                        turned2(i, j // H8 + 1)
                    if j % H8 in (2, 4, 6):
                        hidden2(i, j // H8 + 1, j % H8 // 2 - 1)
                    scaled2(i, j + 2)

            turns(act, TURNS, edges2)

            def copy2(i, ss):
                at_n = ahead(i, ss, 2, NT // 2)
                if at_n is None:
                    return
                _, s, n = at_n
                act.wait_ge(sem("L2_acc"), NG)
                wait(act, sem("L2_ntr"), n - 1)
                nc.scalar.activation(dn[s][:, :, :], acc2[:, bass.ds(n, 1), :], ACT.Copy).then_inc(sem("L2_hs"), 1)

            def turned2n(L, i, ss):
                at_n = ahead(i, ss, 2, NT // 2)
                if at_n is None:
                    return
                _, s, n = at_n
                act.wait_ge(sem(f"L{L}_ntr"), n + 1)
                wait(act, sem(f"L{L}_mm"), n - 1)
                for b in range(2):
                    nc.scalar.activation(dnT[s][:, 4 * b:4 * b + 4, :], bank[2 * s + b][:, :], ACT.Copy).then_inc(sem(f"L{L}_nT"), 1)

            copy2(0, 0)
            copy2(0, 1)
            turned2n(2, 0, 0)

            def nodes2(i):
                for s in range(2):
                    n = i * 2 + s
                    copy2(i, s + 2)
                    turned2n(2, i, s + 1)
                    root(2, n, s)

            turns(act, NT // 2, nodes2)

            def idx3(i):
                for h in range(2):
                    H = i * 2 + h
                    wait(act, sem("L3_seg"), (H - 1) * H8)
                    wait(act, sem("L3_oh"), (H - 1) * H8)
                    nc.scalar.activation(slot3[:, h], small[:, bass.ds(H * H8, H8), :], ACT.Copy).then_inc(sem("L3_slot"), 1)
                    nc.scalar.activation(idx[:, h], small[:, bass.ds(H * H8, H8), C_SRC], ACT.Copy).then_inc(sem("L3_idx"), 1)

            turns(act, TURNS, idx3)

            def copy3(i, ss):
                at_n = ahead(i, ss, 2, NT // 2)
                if at_n is None:
                    return
                _, s, n = at_n
                act.wait_ge(sem("L3_acc"), NG)
                wait(act, sem("L3_ntr"), n - 1)
                nc.scalar.activation(dn[s][:, 0:4, :], x_res[:, bass.ds(n, 1), :], ACT.Copy).then_inc(sem("L3_xs"), 1)

            copy3(0, 0)
            copy3(0, 1)
            turned2n(3, 0, 0)

            def nodes3(i):
                for s in range(2):
                    n = i * 2 + s
                    copy3(i, s + 2)
                    turned2n(3, i, s + 1)
                    for k in range(2):
                        act.wait_ge(sem("L3_mv"), n * 2 + k + 1)
                        nc.scalar.activation(std[:, k:k + 1], mv[:, k, 1:2], ACT.Sqrt, bias=eps_ln[:, :]).then_inc(sem("L3_std"), 1)

            turns(act, NT // 2, nodes3)

        @block.tensor
        def _(pe):
            pe.wait_ge(sem("s_id"), 4)
            pe.wait_ge(sem("s_ones"), 4)
            def counts(k):
                pe.wait_ge(sem("s_rcount"), k + 1)
                nc.tensor.matmul(bank[0][:, 0:NT], tri[:, :], rcount[:, :], start=True, stop=True)
                nc.tensor.matmul(bank[1][:, 0:NT], ones[:, :], rcount[:, :], start=True, stop=True).then_inc(sem("s_counts"), 1)

            counts(0)

            def turn0(i, ss):
                at_n = ahead(i, ss, 2, NT // 2)
                if at_n is None:
                    return
                _, s, n = at_n
                pe.wait_ge(sem("L0_hs"), n + 1)
                wait(pe, sem("L0_hT"), n - 1)
                for k in range(4):
                    ins = nc.tensor.transpose(bank[6 + s][:, P * k:P * k + P], dense0[:, s, P * k:P * k + P], ident[:, :])
                ins.then_inc(sem("L0_tr"), 1)

            pe.wait_ge(sem("s_w0"), 16)
            turn0(0, 0)

            def nodes0(i):
                for s in range(2):
                    n = i * 2 + s
                    turn0(i, s + 1)
                    pe.wait_ge(sem("L0_hT"), n + 1)
                    wait(pe, sem("L0_pr"), n - 1)
                    for k in range(4):
                        ins = nc.tensor.matmul(bank[4 + s][:, :], dense0[:, 2 + s, P * k:P * k + P], w0[:, k, :],
                                               start=k == 0, stop=k == 3)
                    ins.then_inc(sem("L0_mm"), 1)

            nodes0(0)
            with pe.Fori(1, NT // 4) as i:
                nodes0(i)
            counts(1)
            with pe.Fori(NT // 4, NT // 2 - 1) as i:
                nodes0(i)
            nodes0(NT // 2 - 1)

            def place0(i):
                for j in range(U):
                    t = i * U + j
                    pe.wait_ge(sem("s_onehots"), t + 1)
                    pe.wait_ge(sem("s_scaled"), t + 1)
                    for value in range(4):
                        ins = nc.tensor.matmul(bank[value][:, 0:ST], of_lane[j % 4][:, value, :], of_tile[j % 4][:, :],
                                               start=isinstance(i, int) and i == 0 and j == 0,
                                               stop=isinstance(i, int) and i == ETURNS - 1 and j == U - 1)
                    ins.then_inc(sem("s_placed"), 1)

            turns(pe, ETURNS, place0)
            pe.wait_ge(sem("s_slots0"), 3)

            def sums(L, oh, lead):
                def body(i):
                    for j in range(U):
                        h, k = divmod(j, H8)
                        T = i * U + j
                        pe.wait_ge(sem(f"L{L}_oh"), T + 1)
                        pe.wait_ge(sem(f"gath{k}"), L * G_ALL + i * 32 + 16 * h + 16)
                        if j % 2 == 0:
                            wait(pe, sem(f"L{L}_acc"), i * 8 + j // 2 - 1)
                        b = j // 2 % 2
                        if L == 3:
                            nc.tensor.matmul(bank[2 + b][:, 0:2], oh[:, k, :], ones2[:, :], start=j % 2 == 0, stop=j % 2 == 1)
                        nc.tensor.matmul(bank[b][:, :], oh[:, k, :], gath[k][:, :], start=j % 2 == 0, stop=j % 2 == 1)\
                            .then_inc(sem(f"L{L}_seg"), 1)

                turns(pe, TURNS, body)

            sums(0, oh0, None)

            pe.wait_ge(sem("s_wsplit"), 2)

            def turn1(i, qq):
                at_q = ahead(i, qq, 4, TURNS)
                if at_q is None:
                    return
                turn, q, Q = at_q
                h = q // 2
                pe.wait_ge(sem("L1_part"), (turn * 2 + h) * 2 + 2)
                wait(pe, sem("L1_rowT"), Q - 1)
                for k in range(4):
                    ins = nc.tensor.transpose(bank[6 + q % 2][:, P * k:P * k + P],
                                              parts[h][:, 4 * (q % 2) + k, :].bitcast(F32), ident[:, :])
                ins.then_inc(sem("L1_tr"), 1)

            def mm1(i, jj):
                at_t = ahead(i, jj, U, TURNS)
                if at_t is None:
                    return
                turn, j, T = at_t
                q, k = divmod(j, 4)
                pe.wait_ge(sem("L1_rowT"), turn * 4 + q + 1)
                wait(pe, sem("L1_add"), T - 3)
                rows = rowT[q][:, P * k:P * k + P]
                nc.tensor.matmul(bank[j % 4][:, :], rows, we_hi[:, :], start=True, stop=False)
                nc.tensor.matmul(bank[j % 4][:, :], rows, we_lo[:, :], start=False, stop=True)\
                    .then_inc(sem("L1_mm"), 1)

            turn1(0, 0)
            turn1(0, 1)
            for T in range(5):
                mm1(0, T)

            def edges1(i):
                for j in range(U):
                    T = i * U + j
                    if j % 4 == 0:
                        turn1(i, j // 4 + 2)
                    mm1(i, j + 5)
                    pe.wait_ge(sem("L1_oh"), T + 1)
                    pe.wait_ge(sem("L1_relu"), T + 1)
                    if j % 2 == 0:
                        wait(pe, sem("L1_acc"), i * 8 + j // 2 - 1)
                    nc.tensor.matmul(bank[4 + j // 2 % 2][:, :], oh1[:, j % H8, :], msg[j % 4][:, :],
                                     start=j % 2 == 0, stop=j % 2 == 1).then_inc(sem("L1_seg"), 1)

            turns(pe, TURNS, edges1)

            def turn1n(i):
                for s in range(2):
                    n = i * 2 + s
                    pe.wait_ge(sem("L1_hs"), n + 1)
                    wait(pe, sem("L1_hT"), n - 1)
                    for k in range(4):
                        ins = nc.tensor.transpose(bank[s][:, P * k:P * k + P], gath[s][:, P * k:P * k + P], ident[:, :])
                    ins.then_inc(sem("L1_ntr"), 1)

            turns(pe, NT // 2, turn1n)
            pe.wait_ge(sem("s_w1"), 32)
            pe.wait_ge(sem("L1_hT"), NT)
            pe.wait_ge(sem("L1_acc"), NG)

            def first1(c):
                for f in range(8):
                    wait(pe, sem("L1_ev1"), c * 8 + f - 3)
                    for k in range(4):
                        ins = nc.tensor.matmul(bank[2 + f % 4][:, :], w1[:, k, P * f:P * f + P], hT[:, k, bass.ds(c * 512, 512)],
                                               start=k == 0, stop=k == 3)
                    ins.then_inc(sem("L1_h1"), 1)

            turns(pe, 4, first1)
            pe.wait_ge(sem("L1_ev1"), 32)

            def second1(c):
                pe.wait_ge(sem("L1_silu"), c * 8 + 8)
                for g in range(4):
                    wait(pe, sem("L1_ev2"), c * 4 + g - 3)
                    for f in range(8):
                        ins = nc.tensor.matmul(bank[2 + g][:, :], w2[:, f, P * g:P * g + P], aT[:, f, bass.ds(c * 512, 512)],
                                               start=f == 0, stop=f == 7)
                    ins.then_inc(sem("L1_h2"), 1)

            turns(pe, 4, second1)

            def back1(i):
                for s in range(2):
                    n = i * 2 + s
                    pe.wait_ge(sem("L1_sT"), n + 1)
                    wait(pe, sem("L1_z"), n - 1)
                    for g in range(4):
                        ins = nc.tensor.transpose(bank[s][:, P * g:P * g + P], gath[2 + s][:, P * g:P * g + P], ident[:, :])
                    ins.then_inc(sem("L1_btr"), 1)

            turns(pe, NT // 2, back1)

            def uturn(i, ss):
                at_n = ahead(i, ss, 2, NT // 2)
                if at_n is None:
                    return
                _, s, n = at_n
                pe.wait_ge(sem("L1_xn"), n + 1)
                wait(pe, sem("L1_uT"), n - 1)
                nc.tensor.transpose(bank[2 + s][:, 0:P], gath[4 + s][:, 0:P], ident[:, :])
                for m in range(3):
                    ins = nc.tensor.transpose(bank[2 + s][:, P * m + P:P * m + 2 * P],
                                              gath[4 + s][:, P:D].rearrange("p (u m) -> p m u", m=3)[:, m, :], ident[:, :])
                ins.then_inc(sem("L1_utr"), 1)

            pe.wait_ge(sem("L1_ev2"), 16)
            uturn(0, 0)

            def up1(i):
                for s in range(2):
                    n = i * 2 + s
                    uturn(i, s + 1)
                    pe.wait_ge(sem("L1_uT"), n + 1)
                    wait(pe, sem("L1_ub"), n - 1)
                    for m in range(4):
                        ins = nc.tensor.matmul(bank[4 + s][:, P * m:P * m + P], gath[6 + s][:, P * m:P * m + P],
                                               wup[:, min(m, 1), :], start=True, stop=True)
                    ins.then_inc(sem("L1_umm"), 1)

            turns(pe, NT // 2, up1)

            pe.wait_ge(sem("s_w2"), 16 * (8 + 12 + 2))
            pe.wait_ge(sem("L1_ub"), NT)

            def turn2(i, hh):
                at_h = ahead(i, hh, 2, TURNS)
                if at_h is None:
                    return
                turn, h, H = at_h
                pe.wait_ge(sem("L2_slot"), H + 1)
                wait(pe, sem("L2_efT"), H)
                nc.tensor.transpose(bank[7][:, 0:P], slot2[:, h].rearrange("p t c -> p (t c)"), ident[:, :]).then_inc(sem("L2_tr"), 1)

            def layer2(i, hh, k):
                at_h = ahead(i, hh, 2, TURNS)
                if at_h is None:
                    return
                turn, h, H = at_h
                wait(pe, sem("L2_h"), H * 3 + k)
                if k == 0:
                    pe.wait_ge(sem("L2_efT"), H + 1)
                    for j in range(4):
                        ins = nc.tensor.matmul(bank[6][:, P * j:P * j + P], m1[:, j, :], efT[:, :], start=True, stop=True)
                else:
                    ins = nc.tensor.matmul(bank[6][:, :], (m2, m3)[k - 1], hid[k - 1][:, :], start=True, stop=True)
                ins.then_inc(sem("L2_z"), 1)

            def weights2(i, jj):
                at_t = ahead(i, jj, U, TURNS)
                if at_t is None:
                    return
                turn, j, T = at_t
                h, k = divmod(j, H8)
                pe.wait_ge(sem("L2_h"), (turn * 2 + h + 1) * 3)
                wait(pe, sem("L2_prod"), T - 1)
                nc.tensor.matmul(bank[4 + j % 2][:, :], hid[2 + h][:, P * (k // 2):P * (k // 2) + P], m4[:, k % 2, :],
                                 start=True, stop=True).then_inc(sem("L2_w"), 1)

            turn2(0, 0)
            for k in range(3):
                layer2(0, 0, k)
            weights2(0, 0)
            weights2(0, 1)

            def edges2(i):
                for j in range(U):
                    T = i * U + j
                    if j % H8 == 0:
                        turn2(i, j // H8 + 1)
                    if j % H8 in (1, 3, 5):
                        layer2(i, j // H8 + 1, j % H8 // 2)
                    pe.wait_ge(sem("L2_ohy"), T * 4 + 4)
                    pe.wait_ge(sem("L2_prod"), T + 1)
                    if j % 2 == 0:
                        wait(pe, sem("L2_acc"), i * 8 + j // 2 - 1)
                    first, last, b = j % 2 == 0, j % 2 == 1, j // 2 % 2
                    q, o = prod[j % 4], oh2[:, j % 4]
                    nc.tensor.matmul(bank[b][:, :], o[:, 0, :], q[:, 1:5, :], start=first, stop=last)
                    for m in range(3):
                        nc.tensor.matmul(bank[2 + b][:, P * m:P * m + P], o[:, 1 + m, :], q[:, 0, :],
                                         start=first and m == 0, stop=False, skip_group_check=True)
                    nc.tensor.matmul(bank[2 + b][:, 3 * P:4 * P], o[:, 4, :], q[:, 5, :], start=False, stop=last,
                                     skip_group_check=True).then_inc(sem("L2_seg"), 1)
                    weights2(i, j + 2)

            turns(pe, TURNS, edges2)

            def turn2n(L, i, ss):
                at_n = ahead(i, ss, 2, NT // 2)
                if at_n is None:
                    return
                _, s, n = at_n
                for name in (("L2_hs",) if L == 2 else ("L3_xs", "L3_hs")):
                    pe.wait_ge(sem(name), n + 1)
                wait(pe, sem(f"L{L}_nT"), (n - 1) * 2)
                for k in range(8):
                    ins = nc.tensor.transpose(bank[2 * s + k // 4][:, P * (k % 4):P * (k % 4) + P], dn[s][:, k, :], ident[:, :])
                ins.then_inc(sem(f"L{L}_ntr"), 1)

            pe.wait_ge(sem("L2_acc"), NG)
            turn2n(2, 0, 0)

            def nodes2(i):
                for s in range(2):
                    n = i * 2 + s
                    turn2n(2, i, s + 1)
                    pe.wait_ge(sem("L2_nT"), n * 2 + 2)
                    wait(pe, sem("L2_nz"), n - 1)
                    for m, (k0, k1) in enumerate(((0, 7), (4, 1), (5, 2), (6, 3))):
                        for r, k in enumerate((k0, k1)):
                            ins = nc.tensor.matmul(bank[4 + s][:, P * m:P * m + P], dnT[s][:, k, :], wo[:, 2 * min(m, 1) + r, :],
                                                   start=r == 0, stop=r == 1)
                    ins.then_inc(sem("L2_mm"), 1)

            turns(pe, NT // 2, nodes2)

            pe.wait_ge(sem("L2_nz"), NT)
            sums(3, oh3, None)
            pe.wait_ge(sem("s_w3"), 64)
            pe.wait_ge(sem("L3_acc"), NG)
            turn2n(3, 0, 0)

            def nodes3(i):
                for s in range(2):
                    n = i * 2 + s
                    turn2n(3, i, s + 1)
                    pe.wait_ge(sem("L3_nT"), n * 2 + 2)
                    wait(pe, sem("L3_z"), n - 1)
                    for k in range(8):
                        ins = nc.tensor.matmul(bank[4 + s][:, :], dnT[s][:, k, :], w3[:, k, :], start=k == 0, stop=k == 7)
                    ins.then_inc(sem("L3_mm"), 1)

            turns(pe, NT // 2, nodes3)

        @block.vector
        def _(dve):
            v = nc.vector
            step = Chain(dve, sem("s_step"))

            def bins(turn, k, loc, bin_of):
                dve.wait_ge(sem(f"s_key{k}"), 16)
                step(v.tensor_scalar(hi_i[:, :], key[k][:, :], 7, None, ALU.arith_shift_right))
                step(v.tensor_scalar(lo_i[:, :], key[k][:, :], P - 1, None, ALU.bitwise_and))
                step(v.tensor_copy(hi_f[:, :], hi_i[:, :]))
                dve.wait_ge(sem("s_pad"), 2)
                step(v.tensor_copy(loc, lo_i[:, :]))
                dve.wait_ge(sem("s_iota"), 1)
                step(v.tensor_tensor(is_bin, expand(hi_f[:, :], 1, NT), expand(iota_b, 2, ET), ALU.is_equal))
                step(v.tensor_tensor_scan(count.rearrange("p b t -> p (b t)"), is_bin.rearrange("p b t -> p (b t)"), is_bin.rearrange("p b t -> p (b t)"), 0.0, ALU.add, ALU.bypass))
                step(v.memset(before[:, :], 0.0))
                step(v.tensor_copy(before[:, 1:NT], count[:, 0:NT - 1, ET - 1]))
                v.tensor_tensor(rcount[:, :], count[:, :, ET - 1], before[:, :], ALU.subtract).then_inc(sem("s_rcount"), 1)
                dve.wait_ge(sem("s_counts"), turn + 1)
                step(v.tensor_scalar(tot_i[:, :], bank[1][:, 0:NT], float(GROUP - 1), None, ALU.add))
                step(v.tensor_scalar(grp_i[:, :], tot_i[:, :], 8, None, ALU.arith_shift_right))
                step(v.tensor_copy(grp[:, :], grp_i[:, :]))
                step(v.tensor_tensor_scan(gend[:, :], grp[:, :], grp[:, :], 0.0, ALU.add, ALU.bypass))
                step(v.tensor_tensor(off[:, :], gend[:, :], grp[:, :], ALU.subtract))
                step(v.scalar_tensor_tensor(off[:, :], off[:, :], float(GROUP), bank[0][:, 0:NT], ALU.mult, ALU.add))
                step(v.scalar_tensor_tensor(off[:, :], off[:, :], -1.0, before[:, :], ALU.add, ALU.subtract))
                step(v.tensor_tensor(count, count, expand(off[:, :], 2, ET), ALU.add))
                step(v.tensor_tensor(is_bin, count, is_bin, ALU.mult))
                step(v.tensor_reduce(rank[:, :], is_bin.rearrange("p b t -> p t b"), AX.X, ALU.add))
                step(v.tensor_copy(hi_i[:, :], rank[:, :]))
                step(v.tensor_scalar(lo_i[:, :], hi_i[:, :], P - 1, None, ALU.bitwise_and))
                step(v.tensor_scalar(hi_i[:, :], hi_i[:, :], 7, None, ALU.arith_shift_right))
                if turn == 0:
                    step(v.scalar_tensor_tensor(row[:, :], lo_i[:, :], float(ST), hi_i[:, :], ALU.mult, ALU.add))
                    step(v.tensor_copy(held[:, :], bank[1][:, 0:NT]))
                    step(v.tensor_tensor_scan(pads_from[:, :], held[:, :], held[:, :], 0.0, ALU.add, ALU.bypass))
                    step(v.tensor_tensor(pads_from[:, :], held[:, :], pads_from[:, :], ALU.subtract))
                    step(v.tensor_tensor(off[:, :], gend[:, :], grp[:, :], ALU.subtract))
                    step(v.scalar_tensor_tensor(pads_from[:, :], off[:, :], float(GROUP), pads_from[:, :], ALU.mult, ALU.add))
                    dve.wait_ge(sem("s_iota"), 2)
                    step(v.tensor_tensor(pad_in[:, :, :], expand(pad_n[:, :], 2, NT), expand(pads_from[:, :], 1, PADS), ALU.is_ge))
                    step(v.tensor_tensor(pad_in[:, :, :], pad_in[:, :, :], expand(held[:, :], 1, PADS), ALU.mult))
                    step(v.tensor_reduce(pad_f[:, :], pad_in[:, :, :], AX.X, ALU.add))
                    step(v.tensor_tensor(pad_row[:, :], pad_f[:, :], pad_n[:, :], ALU.add))
                    step(v.tensor_scalar(pad_lane[:, :], pad_row[:, :], P - 1, None, ALU.bitwise_and))
                    step(v.tensor_scalar(pad_row[:, :], pad_row[:, :], 7, None, ALU.arith_shift_right))
                    step(v.scalar_tensor_tensor(pad_row[:, :], pad_lane[:, :], float(ST), pad_row[:, :], ALU.mult, ALU.add))
                    dve.wait_ge(sem("s_small"), 3)
                    v.memset(before[:, :], 0.0).then_inc(sem("s_rows"), 1)
                else:
                    step(v.tensor_copy(tile_f[:, :], hi_i[:, :]))
                    step(v.tensor_copy(lane_f[:, :], lo_i[:, :]))
                step(v.tensor_tensor(gcmp, expand(gend[:, :], 1, NG), expand(iota[:, 0:NG], 2, NT), ALU.is_le))
                step(v.tensor_reduce(gsum[:, :], gcmp, AX.X, ALU.add))
                step(v.tensor_scalar(bin_of[:, :], gsum[:, :], float(NT - 1), None, ALU.min))

            bins(0, 1, edge_small[:, :, C_LOC], bin_d)
            dve.wait_ge(sem("s_rows"), 1)
            bins(1, 0, loc_f[:, :], bin_s)

            dve.wait_ge(sem("s_vals"), 2)
            v.tensor_scalar(loc_f[:, :], loc_f[:, :], 1.0, None, ALU.add).then_inc(sem("s_loc1"), 1)
            step(v.tensor_tensor(w_lo[:, :], w_in[:, :], w_hi[:, :], ALU.subtract))

            def onehots0(i):
                for j in range(U):
                    t = i * U + j
                    wait(dve, sem("s_placed"), t - 3)
                    lane = lane_f[:, bass.ds(t, 1)]
                    v.tensor_scalar(in_lane[:, j % 4, :], iota[:, 0:P], lane, None, ALU.is_equal).then_inc(sem("s_in_lane"), 1)
                    v.tensor_scalar(of_tile[j % 4][:, :], iota[:, :], tile_f[:, bass.ds(t, 1)], None, ALU.is_equal)
                    for value, of in ((2, w_hi), (3, w_lo))[1 - j % 2:]:
                        ins = v.tensor_scalar(of_lane[j % 4][:, value, :], iota[:, 0:P], lane,
                                              of[:, bass.ds(t, 1)].bitcast(F32), ALU.is_equal, ALU.mult)
                    ins.then_inc(sem("s_onehots"), 1)

            turns(dve, ETURNS, onehots0)
            dve.wait_ge(sem("s_placed"), ET)
            step(v.tensor_copy(slots0[:, :, 2], bank[2][:, 0:ST]))
            v.tensor_copy(slots0[:, :, 0], bank[0][:, 0:ST]).then_inc(sem("s_slots0"), 1)
            v.tensor_scalar(slots0[:, :, 1], bank[1][:, 0:ST], -1.0, None, ALU.add).then_inc(sem("s_slots0"), 1)
            v.tensor_tensor(slots0[:, :, 2], slots0[:, :, 2], bank[3][:, 0:ST], ALU.add).then_inc(sem("s_slots0"), 1)
            step(v.memset(acc[:, 0:NT * D], 0.0))

            def bin_registers(table_of, i):
                _, r = nc.values_load_multi_w_load_instructions(
                    table_of[0:1, bass.ds(i * 8, 8)], engines=[mybir.EngineType.DVE], min_val=0, max_val=NT - 1)
                return r

            def sums(L, oh, slot, col, table_of):
                def onehot(i, jj):
                    at_t = ahead(i, jj, U, TURNS)
                    if at_t is None:
                        return
                    turn, j, T = at_t
                    h, k = divmod(j, H8)
                    dve.wait_ge(sem(f"L{L}_slot"), turn * 2 + h + 1)
                    wait(dve, sem(f"L{L}_seg"), T - H8 + 1)
                    if L == 0:
                        ins = v.tensor_scalar(oh[:, k, :], iota[:, 0:P], slot[:, h, k, 1:2], slot[:, h, k, 2:3],
                                              ALU.is_equal, ALU.mult)
                    else:
                        ins = v.tensor_scalar(oh[:, k, :], iota[:, 0:P], slot[:, h, k, col:col + 1], None, ALU.is_equal)
                    ins.then_inc(sem(f"L{L}_oh"), 1)

                for T in range(4):
                    onehot(0, T)

                def body(i):
                    regs = bin_registers(table_of, i)
                    for j in range(U):
                        T = i * U + j
                        onehot(i, j + 4)
                        if j % 2:
                            dve.wait_ge(sem(f"L{L}_seg"), T + 1)
                            G = i * 8 + j // 2
                            b = j // 2 % 2
                            wait(dve, sem(f"L{L}_acc"), G)
                            at = acc_n[:, bass.ds(regs[j // 2], 1), :]
                            if L == 3:
                                d = deg[:, bass.ds(regs[j // 2], 1)]
                                v.tensor_tensor(d, d, bank[2 + b][:, 0:1], ALU.add)
                            v.tensor_tensor(at, at, bank[b][:, :], ALU.add).then_inc(sem(f"L{L}_acc"), 1)

                turns(dve, TURNS, body)

            sums(0, oh0, slot0, 1, bin_s)
            dve.wait_ge(sem("L0_acc"), NG)

            def norm(L, n, s, z, out):
                v.bn_stats(stats[:, s, :], z).then_inc(sem(f"L{L}_bs"), 1)
                dve.wait_ge(sem(f"L{L}_bs"), n + 1)
                gate(dve, "dve")
                v.bn_aggr(mv[:, s, :], stats[:, s, :]).then_inc(sem(f"L{L}_mv"), 1)
                dve.wait_ge(sem(f"L{L}_std"), n + 1)
                v.reciprocal(rstd[:, s:s + 1], std[:, s:s + 1]).then_inc(sem(f"L{L}_rs"), 1)
                dve.wait_ge(sem(f"L{L}_rs"), n + 1)
                dve.wait_ge(sem(f"L{L}_mv"), n + 1)
                return v.tensor_scalar(out, z, mv[:, s, 0:1], rstd[:, s:s + 1], ALU.subtract, ALU.mult)

            dve.wait_ge(sem("s_x"), 16)
            dve.wait_ge(sem("s_we"), 16 * 5)

            def nodes0(i):
                for s in range(2):
                    n = i * 2 + s
                    z, x, y = dense0[:, s, :], x_res[:, bass.ds(n, 1), :], dense0[:, 2 + s, :]
                    v.tensor_tensor(z, acc_n[:, bass.ds(n, 1), :], x, ALU.add).then_inc(sem("L0_z"), 1)
                    dve.wait_ge(sem("L0_z"), n + 1)
                    norm(0, n, s, z, x).then_inc(sem("L0_x"), 1)
                    dve.wait_ge(sem("L0_x"), n + 1)
                    wait(dve, sem(f"L0_st{s}"), i * 16)
                    v.tensor_tensor(y, x, be[:, :], ALU.add).then_inc(sem("L0_y"), 1)

            turns(dve, NT // 2, nodes0)

            step(v.memset(acc[:, 0:NT * D], 0.0))
            v.tensor_copy(we_hi[:, :], we_f[:, :]).then_inc(sem("s_wsplit"), 1)
            dve.wait_ge(sem("s_wsplit"), 1)
            v.tensor_tensor(we_lo[:, :], we_f[:, :], we_hi[:, :], ALU.subtract).then_inc(sem("s_wsplit"), 1)
            step(v.tensor_scalar(eps1[:, :], eps1[:, :], 1.0, None, ALU.add))

            def low1(i, hh):
                at_h = ahead(i, hh, 2, TURNS)
                if at_h is None:
                    return
                turn, h, H = at_h
                dve.wait_ge(sem("L1_high"), H + 1)
                wait(dve, sem("L1_tr"), (H - 1) * 2)
                for q in range(2):
                    at = slice(4 * q, 4 * q + 4)
                    v.tensor_tensor(parts[h][:, at, EA:2 * EA], chunk[:, h, at, 0:EA], parts[h][:, at, 0:EA], ALU.subtract)\
                        .then_inc(sem("L1_part"), 1)

            def add1(i, jj):
                at_t = ahead(i, jj, U, TURNS)
                if at_t is None:
                    return
                turn, j, T = at_t
                h, k = divmod(j, H8)
                dve.wait_ge(sem("L1_small"), turn * 2 + h + 1)
                wait(dve, sem("L1_seg"), T - H8 + 1)
                v.tensor_scalar(oh1[:, k, :], iota[:, 0:P], small[:, bass.ds(T, 1), C_LOC], None, ALU.is_equal)\
                    .then_inc(sem("L1_oh"), 1)
                dve.wait_ge(sem("L1_mm"), T + 1)
                dve.wait_ge(sem(f"gath{k}"), G_ALL + turn * 32 + 16 * h + 16)
                wait(dve, sem("L1_seg"), T - 3)
                v.tensor_tensor(msg[j % 4][:, :], bank[j % 4][:, :], gath[k][:, :], ALU.add).then_inc(sem("L1_add"), 1)

            low1(0, 0)
            low1(0, 1)
            for T in range(3):
                add1(0, T)

            def edges1(i):
                regs = bin_registers(bin_d, i)
                for j in range(U):
                    T = i * U + j
                    if j % H8 == 5:
                        low1(i, j // H8 + 2)
                    add1(i, j + 3)
                    if j % 2:
                        dve.wait_ge(sem("L1_seg"), T + 1)
                        wait(dve, sem("L1_acc"), i * 8 + j // 2)
                        at = acc_n[:, bass.ds(regs[j // 2], 1), :]
                        v.tensor_tensor(at, at, bank[4 + j // 2 % 2][:, :], ALU.add).then_inc(sem("L1_acc"), 1)

            turns(dve, TURNS, edges1)

            dve.wait_ge(sem("L1_acc"), NG)

            def own1(i):
                for s in range(2):
                    n = i * 2 + s
                    wait(dve, sem("L1_ntr"), n - 1)
                    v.scalar_tensor_tensor(gath[s][:, :], x_res[:, bass.ds(n, 1), :], eps1[:, 0:1], acc_n[:, bass.ds(n, 1), :],
                                           ALU.mult, ALU.add).then_inc(sem("L1_hs"), 1)

            turns(dve, NT // 2, own1)

            def batch(count_of, src, nf, evs):
                def body(c):
                    for f in range(nf):
                        dve.wait_ge(sem(evs), c * nf + f + 1)
                        v.bn_stats(bst[:, f, bass.ds(c, 1), :], src[:, f, bass.ds(c * 512, 512)]).then_inc(sem(f"L1_bst{nf}"), 1)

                turns(dve, 4, body)
                dve.wait_ge(sem(f"L1_bst{nf}"), 4 * nf)
                for f in range(nf):
                    ins = v.bn_aggr(bmv[:, f, :], bst[:, f, :, :].rearrange("p c s -> p (c s)"))
                ins.then_inc(sem("L1_bmv"), 1)
                dve.wait_ge(sem("L1_bstd"), count_of)
                g, be = (g1, be1) if nf == 8 else (g2, be2)
                sc, sh, tm = bscale[:, 0:nf], bshift[:, 0:nf], btmp[:, 0:nf]
                step(v.reciprocal(tm, bstd[:, 0:nf]))
                step(v.tensor_tensor(sc, tm, g, ALU.mult))
                step(v.tensor_tensor(tm, bmv[:, 0:nf, 0], sc, ALU.mult))
                v.tensor_tensor(sh, be, tm, ALU.subtract).then_inc(sem("L1_bn"), 1)

            batch(1, aT, 8, "L1_ev1")
            batch(2, hT, 4, "L1_ev2")

            def back1(i):
                for s in range(2):
                    n = i * 2 + s
                    at = x_res[:, bass.ds(n, 1), :]
                    dve.wait_ge(sem("L1_btr"), n + 1)
                    v.tensor_tensor(at, at, bank[s][:, :], ALU.add).then_inc(sem("L1_z"), 1)
                    dve.wait_ge(sem("L1_z"), n + 1)
                    v.bn_stats(nst[:, bass.ds(n, 1), :], x_res[:, bass.ds(n, 1), :]).then_inc(sem("L1_nst"), 1)

            turns(dve, NT // 2, back1)
            dve.wait_ge(sem("L1_nst"), NT)
            for n in range(NT):
                ins = v.bn_aggr(nmv[:, n, :], nst[:, n, :])
            ins.then_inc(sem("L1_mv"), 1)
            dve.wait_ge(sem("L1_std"), 1)
            step(v.reciprocal(nstd[:, :], nstd[:, :]))

            def norm1(i):
                for s in range(2):
                    n = i * 2 + s
                    wait(dve, sem("L1_utr"), n - 1)
                    wait(dve, sem("L1_x"), n - 1)
                    v.tensor_scalar(gath[4 + s][:, :], x_res[:, bass.ds(n, 1), :], nmv[:, bass.ds(n, 1), 0:1],
                                    nstd[:, bass.ds(n, 1)], ALU.subtract, ALU.mult).then_inc(sem("L1_xn"), 1)

            turns(dve, NT // 2, norm1)

            dve.wait_ge(sem("s_az"), 1)
            dve.wait_ge(sem("L1_x"), NT)

            def onehot2(i, jj):
                at_t = ahead(i, jj, U, TURNS)
                if at_t is None:
                    return
                turn, j, T = at_t
                h, k = divmod(j, H8)
                dve.wait_ge(sem("L2_slot"), turn * 2 + h + 1)
                wait(dve, sem("L2_seg"), T - 3)
                v.tensor_scalar(oh2[:, j % 4, 4, :], iota[:, 0:P], slot2[:, h, k, C_LOC:C_LOC + 1], None, ALU.is_equal)\
                    .then_inc(sem("L2_oh"), 1)

            def products2(i, jj):
                at_t = ahead(i, jj, U, TURNS)
                if at_t is None:
                    return
                turn, j, T = at_t
                h, k = divmod(j, H8)
                w, s, q, t, y = bank[4 + j % 2], gath[k], prod[j % 4], dot[j % 2], slot2[:, h, k, :]
                dve.wait_ge(sem("L2_dot"), T + 1)
                wait(dve, sem("L2_seg"), T - 3)
                v.scalar_tensor_tensor(t[:, :], s[:, 2 * P:3 * P], y[:, C_Y + 2:C_Y + 3], t[:, :], ALU.mult, ALU.add)\
                    .then_inc(sem("L2_t"), 1)
                dve.wait_ge(sem("L2_w"), T + 1)
                v.tensor_tensor(q[:, 0:2, :], w[:, 0:2 * P].rearrange("p (a c) -> p a c", a=2), expand(s[:, 0:P], 1, 2), ALU.mult)
                dve.wait_ge(sem("L2_t"), T * 2 + 1)
                v.scalar_tensor_tensor(t[:, :], s[:, 3 * P:4 * P], y[:, C_Y + 3:C_Y + 4], t[:, :], ALU.mult, ALU.add)\
                    .then_inc(sem("L2_t"), 1)
                v.tensor_tensor(q[:, 2:5, :], expand(w[:, 2 * P:3 * P], 1, 3),
                                s[:, P:4 * P].rearrange("p (m c) -> p m c", m=3), ALU.mult)
                dve.wait_ge(sem("L2_t"), T * 2 + 2)
                v.scalar_tensor_tensor(q[:, 5, :], t[:, :], 3.0 ** -0.5, w[:, 3 * P:4 * P], ALU.mult, ALU.mult)\
                    .then_inc(sem("L2_prod"), 1)

            for T in range(3):
                onehot2(0, T)
            products2(0, 0)

            def edges2(i):
                regs = bin_registers(bin_d, i)
                for j in range(U):
                    T = i * U + j
                    products2(i, j + 1)
                    if j % 2:
                        b = j // 2 % 2
                        dve.wait_ge(sem("L2_seg"), T + 1)
                        wait(dve, sem("L2_acc"), i * 8 + j // 2)
                        for part in range(2):
                            at = acc2[:, bass.ds(regs[j // 2], 1), D * part:D * part + D]
                            ins = v.tensor_tensor(at, at, bank[2 * part + b][:, :], ALU.add)
                        ins.then_inc(sem("L2_acc"), 1)
                    onehot2(i, j + 3)

            turns(dve, TURNS, edges2)

            def nodes2(i):
                for s in range(2):
                    n = i * 2 + s
                    z, x = dz[s], x_res[:, bass.ds(n, 1), :].rearrange("p o d -> p (o d)")
                    dve.wait_ge(sem("L2_mm"), n + 1)
                    v.scalar_tensor_tensor(z[:, 0:P], bank[4 + s][:, 0:P], C_OUT, x[:, 0:P], ALU.mult, ALU.add)
                    v.scalar_tensor_tensor(z[:, P:D].rearrange("p (u m) -> p u m", m=3),
                                           bank[4 + s][:, P:D].rearrange("p (m u) -> p u m", m=3), C_OUT,
                                           x[:, P:D].rearrange("p (u m) -> p u m", m=3), ALU.mult, ALU.add).then_inc(sem("L2_nz"), 1)
                    dve.wait_ge(sem("L2_nz"), n + 1)
                    norm(2, n, s, z[:, :], x_res[:, bass.ds(n, 1), :]).then_inc(sem("L2_x"), 1)

            turns(dve, NT // 2, nodes2)

            dve.wait_ge(sem("s_az"), 2)
            dve.wait_ge(sem("s_ones"), 4)
            sums(3, oh3, slot3, C_LOC, bin_d)
            dve.wait_ge(sem("L3_acc"), NG)
            step(v.tensor_scalar(deg[:, :], deg[:, :], 1.0, None, ALU.max))
            step(v.reciprocal(rdeg[:, :], deg[:, :]))

            def mean3(i, ss):
                at_n = ahead(i, ss, 2, NT // 2)
                if at_n is None:
                    return
                _, s, n = at_n
                wait(dve, sem("L3_ntr"), n - 1)
                v.tensor_scalar(dn[s][:, 4:8, :], acc_n[:, bass.ds(n, 1), :].rearrange("p o (k c) -> p (o k) c", k=4),
                                rdeg[:, bass.ds(n, 1)], None, ALU.mult).then_inc(sem("L3_hs"), 1)

            mean3(0, 0)
            mean3(0, 1)
            dve.wait_ge(sem("s_w3"), 64)

            def nodes3(i):
                for s in range(2):
                    n = i * 2 + s
                    z, y = dz[s][:, :], dy[s][:, :]
                    mean3(i, s + 2)
                    dve.wait_ge(sem("L3_mm"), n + 1)
                    v.tensor_tensor(z, bank[4 + s][:, :], bias3, ALU.add).then_inc(sem("L3_z"), 1)
                    dve.wait_ge(sem("L3_z"), n + 1)
                    norm(3, n * 2, 0, z, z).then_inc(sem("L3_n"), 1)
                    dve.wait_ge(sem("L3_n"), n * 4 + 1)
                    v.tensor_tensor(z, z, gamma3, ALU.mult).then_inc(sem("L3_n"), 1)
                    dve.wait_ge(sem("L3_n"), n * 4 + 2)
                    v.tensor_tensor(z, z, beta3, ALU.add).then_inc(sem("L3_n"), 1)
                    dve.wait_ge(sem("L3_n"), n * 4 + 3)
                    v.tensor_tensor(z, z, x_res[:, bass.ds(n, 1), :], ALU.add).then_inc(sem("L3_n"), 1)
                    dve.wait_ge(sem("L3_n"), n * 4 + 4)
                    wait(dve, sem(f"L3_st{s}"), i * 16)
                    norm(3, n * 2 + 1, 1, z, y).then_inc(sem("L3_y"), 1)

            turns(dve, NT // 2, nodes3)


_INS = ["src", "dst", "x", "edge_attr_4", "edge_attr_64", "edge_attr_8", "edge_weight", "L1_gnn_W_e",
        "L1_gnn_W1", "L1_gnn_W2", "L2_gnn_W_up0", "L2_gnn_W_up1", "L2_gnn_W_mlp1", "L2_gnn_W_mlp2", "L2_gnn_W_mlp3",
        "L2_gnn_W_mlp4", "L2_gnn_W_out0", "L2_gnn_W_out1"]


def kernel(**inputs):
    import numpy as np
    import concourse.bacc as bacc
    from concourse.bass_utils import run_bass_kernel_spmd

    arrays = {name: np.ascontiguousarray(inputs[name]) for name in _INS}
    arrays["w0"] = np.ascontiguousarray(np.asarray(inputs["L0_gnn_weight"]).T)
    arrays["w3"] = np.ascontiguousarray(np.concatenate(
        [np.asarray(inputs["L3_gnn_W_self"]).T, np.asarray(inputs["L3_gnn_W_neigh"]).T]))
    columns = [np.asarray(inputs[f"L1_gnn_{k}"]).reshape(-1, P).T for k in ("b1", "g1", "beta1", "b2", "g2", "beta2")]
    arrays["bn"] = np.ascontiguousarray(np.concatenate(columns, axis=1))
    arrays["eps"] = np.ascontiguousarray(np.broadcast_to(np.asarray(inputs["L1_gnn_eps"]), (P, 1)))
    arrays["be"] = np.ascontiguousarray(np.broadcast_to(np.asarray(inputs["L1_gnn_b_e"]), (P, D)))
    for k in ("bias", "gamma", "beta"):
        arrays[k] = np.ascontiguousarray(np.broadcast_to(np.asarray(inputs[f"L3_gnn_{k}"]), (P, D)))

    nc = bacc.Bacc("TRN2", target_bir_lowering=False, num_devices=1)
    aps = {name: nc.dram_tensor(f"in_{name}", v.shape, mybir.dt.from_np(v.dtype), kind="ExternalInput").ap()
           for name, v in arrays.items()}
    aps["out"] = nc.dram_tensor("out", (N, D), F32, kind="ExternalOutput").ap()
    build(nc, aps)
    r = run_bass_kernel_spmd(nc, [{f"in_{name}": v for name, v in arrays.items()}], core_ids=[0])
    return r.results[0]["out"]
```

```python
from contextlib import ExitStack

import concourse.bass as bass
from concourse import mybir

F32 = mybir.dt.float32
I32 = mybir.dt.int32
F32R = mybir.dt.float32r
ALU = mybir.AluOpType
ACT = mybir.ActivationFunctionType
AX = mybir.AxisListType

P = 128
N = 2048
D = 512
E = 32768
NT = N // P
ET = E // P
GROUP = 2 * P
NG = E // GROUP + NT
ST = NG * GROUP // P
U = 16
H8 = 8
PADS = ST - ET
TURNS = ST // U
ETURNS = ET // U
G_ALL = 16 * ST // H8
EA, EF, NY = 64, 8, 4
NORMS = {0: 0, 2: NT, 3: 2 * NT}
SMALL = 16
C_EF, C_Y, C_SRC, C_LOC = 0, EF, EF + NY, EF + NY + 1
ROW = EA + SMALL
LN_EPS = 1e-5
SILU_2MOM = 1.679177


def wait(eng, sem, value):
    if isinstance(value, int) and value <= 0:
        return
    eng.wait_ge(sem, value)


def turns(eng, n, body, first=1, last=1):
    for i in range(first):
        body(i)
    with eng.Fori(first, n - last) as i:
        body(i)
    for i in range(n - last, n):
        body(i)


def ahead(turn, k, per, end):
    turn_k = turn + k // per if k // per else turn
    if isinstance(turn_k, int) and turn_k >= end:
        return None
    return turn_k, k % per, turn * per + k


def expand(ap, axis, n):
    shape = list(ap.shape)
    return ap.unsqueeze(axis).broadcast_to(shape[:axis] + [n] + shape[axis:])


class Chain:

    def __init__(self, eng, sem):
        self.eng, self.sem, self.n = eng, sem, 0

    def __call__(self, ins):
        ins.then_inc(self.sem, 1)
        self.n += 1
        self.eng.wait_ge(self.sem, self.n)


def build(nc, a):
    ctx = ExitStack()
    with ctx:
        def sb(name, shape, dt=F32, at=ctx):
            return at.enter_context(nc.sbuf_tensor(name, shape, dt))

        sems = {}

        def sem(name):
            if name not in sems:
                sems[name] = ctx.enter_context(nc.semaphore(name))
            return sems[name]

        def gate(eng):
            eng.sem_inc(sem("gates"), 1)

        slots_d = nc.dram_tensor("slots_by_dst", [P * ST, ROW], F32, kind="Internal").ap()
        table = [nc.dram_tensor(f"nodes_{k}", [N, D], F32, kind="Internal").ap() for k in (1, 2, 3)]
        proj0 = nc.dram_tensor("projected_0", [N, D], F32, kind="Internal").ap()
        slots_d_v = slots_d.rearrange("(p t) c -> p t c", p=P)

        x_res = sb("x_res", [P, NT, D])
        acc = sb("acc", [P, NT * 2 * D])
        small = sb("small", [P, ST, SMALL])
        gath = [sb(f"gath{k}", [P, D]) for k in range(H8)]
        wbuf = sb("wbuf", [P, 8192])
        we_hi = sb("we_hi", [P, D], F32R)
        we_lo = sb("we_lo", [P, D], F32R)
        be = sb("be", [P, D])
        wup = sb("wup", [P, 2, P])
        ident = sb("ident", [P, P])
        iota = sb("iota", [P, ST])
        bin_s = sb("bin_s", [P, NG // 4], I32)
        bin_d = sb("bin_d", [P, NG // 4], I32)
        idx = sb("idx", [P, 2, H8], I32)
        stats = sb("stats", [P, 4, 6])
        mv = sb("mv", [P, 4, 2])
        std = sb("std", [P, 4])
        rstd = sb("rstd", [P, 4])
        eps_ln = sb("eps_ln", [P, 1])
        rdeg = sb("rdeg", [P, NT])
        ones2 = sb("ones2", [P, 2])
        eps1 = sb("eps1", [P, 1])
        bn_in = sb("bn_in", [P, 36])
        bank = [ctx.enter_context(nc.psum_tensor(f"bank{k}", [P, 512], F32)) for k in range(8)]

        edge_small = acc[:, 12288:16384].rearrange("p (t c) -> p t c", c=SMALL)
        is_bin = acc[:, 0:4096].rearrange("p (b t) -> p b t", b=NT)
        count = acc[:, 4096:8192].rearrange("p (b t) -> p b t", b=NT)
        slots0 = acc[:, 8192:8192 + 4 * ST].rearrange("p (t c) -> p t c", c=4)
        pad_in = acc[:, 11264:11264 + PADS * NT].rearrange("p (t b) -> p t b", b=NT)
        acc_n = acc[:, 0:NT * D].rearrange("p (n d) -> p n d", d=D)

        s0 = ExitStack()
        key = [sb(f"key{k}", [P, ET], I32, s0) for k in range(2)]
        hi_i = sb("hi_i", [P, ET], I32, s0)
        lo_i = sb("lo_i", [P, ET], I32, s0)
        hi_f = sb("hi_f", [P, ET], F32, s0)
        rank = sb("rank", [P, ET], F32, s0)
        row = sb("row", [P, ET], I32, s0)
        w_in = sb("w_in", [P, ET], F32, s0)
        tile_f = sb("tile_f", [P, ET], F32, s0)
        lane_f = sb("lane_f", [P, ET], F32, s0)
        dst_f = sb("dst_f", [P, ET], F32, s0)
        loc_f = sb("loc_f", [P, ET], F32, s0)
        w_hi = sb("w_hi", [P, ET], F32R, s0)
        w_lo = sb("w_lo", [P, ET], F32, s0)
        tri = sb("tri", [P, P], F32, s0)
        ones = sb("ones", [P, P], F32, s0)
        pad_d = sb("pad_d", [P, ROW], F32, s0)
        pad_n = sb("pad_n", [P, PADS], F32, s0)
        pad_row = sb("pad_row", [P, PADS], I32, s0)
        pad_f = sb("pad_f", [P, PADS], F32, s0)
        pad_lane = sb("pad_lane", [P, PADS], I32, s0)
        held = sb("held", [P, NT], F32, s0)
        pads_from = sb("pads_from", [P, NT], F32, s0)
        before = sb("before", [P, NT], F32, s0)
        rcount = sb("rcount", [P, NT], F32, s0)
        tot_i = sb("tot_i", [P, NT], I32, s0)
        grp_i = sb("grp_i", [P, NT], I32, s0)
        grp = sb("grp", [P, NT], F32, s0)
        gend = sb("gend", [P, NT], F32, s0)
        off = sb("off", [P, NT], F32, s0)
        gsum = sb("gsum", [P, NG], F32, s0)
        packed = sb("packed", [P, NG // 4], F32, s0)
        stage_d = sb("stage_d", [P, 2, H8, ROW], F32, s0)
        drow = sb("drow", [P, 2, H8], I32, s0)
        slot0 = sb("slot0", [P, 2, H8, 4], F32, s0)
        of_tile = [sb(f"of_tile{k}", [P, ST], F32R, s0) for k in range(4)]
        of_lane = [sb(f"of_lane{k}", [P, 4, P], F32R, s0) for k in range(4)]
        s0.close()
        small_flat = small[:, :, :].rearrange("p t c -> p (t c)")
        dense0 = small_flat[:, 0:6 * D].rearrange("p (b d) -> p b d", b=6)
        oh0 = small_flat[:, 6 * D:6 * D + H8 * P].rearrange("p (k n) -> p k n", k=H8)
        in_lane = small_flat[:, 6 * D + H8 * P:6 * D + H8 * P + 4 * P].rearrange("p (k n) -> p k n", k=4)
        ef_in = dense0[:, 0:4, :].rearrange("p a (t c) -> p (a t) c", c=EF)
        y_in = dense0[:, 4:6, :].rearrange("p a (t c) -> p (a t) c", c=NY)
        gcmp = acc[:, 8192:8192 + NG * NT].rearrange("p (g b) -> p g b", b=NT)

        s1 = ExitStack()
        chunk = acc[:, 12288:12288 + 2 * H8 * ROW].rearrange("p (h t c) -> p h t c", h=2, t=H8)
        parts = [sb(f"parts{k}", [P, H8, 2 * EA], F32R, s1) for k in range(2)]
        rowT = [sb(f"rowT{k}", [P, 4 * P], F32R, s1) for k in range(4)]
        msg = [sb(f"msg{k}", [P, D], F32, s1) for k in range(4)]
        oh1 = sb("oh1", [P, H8, P], F32, s1)
        msg_hi = sb("msg_hi", [P, D], F32R, s1)
        msg_lo = sb("msg_lo", [P, D], F32R, s1)
        oh1_r = [sb(f"oh1_r{k}", [P, P], F32R, s1) for k in range(2)]
        s1.close()
        s1d = ExitStack()
        hT = sb("hT", [P, 4, N], F32, s1d)
        bst = sb("bst", [P, 8, 4, 6], F32, s1d)
        bmv = sb("bmv", [P, 8, 2], F32, s1d)
        bstd = sb("bstd", [P, 8], F32, s1d)
        bscale = sb("bscale", [P, 8], F32, s1d)
        bshift = sb("bshift", [P, 8], F32, s1d)
        btmp = sb("btmp", [P, 8], F32, s1d)
        nst = sb("nst", [P, NT, 6], F32, s1d)
        nmv = sb("nmv", [P, NT, 2], F32, s1d)
        nstd = sb("nstd", [P, NT], F32, s1d)
        s1d.close()
        aT = acc[:, :].rearrange("p (f n) -> p f n", f=8)
        s2 = ExitStack()
        slot2 = sb("slot2", [P, 2, H8, SMALL], F32, s2)
        ef_in2 = sb("ef_in2", [P, H8, SMALL], F32, s2)
        efT = sb("efT", [P, P], F32, s2)
        hid = [wbuf[:, 2048 + D * k:2048 + D * (k + 1)] for k in range(2)]
        last = wbuf[:, 3072:3072 + D]
        last_hi = sb("last_hi", [P, 4 * P], F32R, s2)
        last_lo = sb("last_lo", [P, 4 * P], F32R, s2)
        last_parts = [[sb(f"last_parts{h}{e}", [P, 4 * P], F32R, s2) for e in range(2)] for h in range(2)]
        prod = [sb(f"prod{k}", [P, 6, P], F32, s2) for k in range(4)]
        dot = [sb(f"dot{k}", [P, P], F32, s2) for k in range(2)]
        oh2 = wbuf[:, 4096:4096 + H8 * P].rearrange("p (k n) -> p k n", k=H8)
        scaled = [sb(f"scaled{k}", [P, 4, P], F32, s2) for k in range(4)]
        s2.close()
        s2d = ExitStack()
        dn = [sb(f"dn{k}", [P, 8, P], F32, s2d) for k in range(2)]
        dnT = [sb(f"dnT{k}", [P, 8, P], F32, s2d) for k in range(2)]
        dz = [wbuf[:, 5632 + D * k:5632 + D * (k + 1)] for k in range(2)]
        dy = [be[:, :], wbuf[:, 6656:6656 + D]]
        slot3 = sb("slot3", [P, 2, H8, SMALL], F32, s2d)
        oh3 = wbuf[:, 7168:8192].rearrange("p (k n) -> p k n", k=H8)
        seen = sb("seen", [P, NT, 2 * P], F32, s2d)
        s2d.close()
        iota_b = iota[:, 0:NT]
        b1, g1, be1 = (bn_in[:, 8 * k:8 * k + 8] for k in range(3))
        b2, g2, be2 = (bn_in[:, 24 + 4 * k:28 + 4 * k] for k in range(3))

        w0 = wbuf[:, 0:2048].rearrange("p (k n) -> p k n", k=4)
        w1 = wbuf[:, 0:4096].rearrange("p (k n) -> p k n", k=4)
        w2 = wbuf[:, 4096:8192].rearrange("p (k n) -> p k n", k=8)
        we_f = wbuf[:, 2048:2560]
        m1 = wbuf[:, 0:512].rearrange("p (j n) -> p j n", j=4)
        m2 = wbuf[:, 512:640]
        m3 = wbuf[:, 640:768]
        m4 = wbuf[:, 768:1280]
        wo = wbuf[:, 1280:1792].rearrange("p (k n) -> p k n", k=4)
        w3 = wbuf[:, 0:4096].rearrange("p (k n) -> p k n", k=8)
        bias3, gamma3, beta3 = (wbuf[:, 4096 + D * k:4096 + D * (k + 1)] for k in range(3))

        own = acc[:, NT * D:2 * NT * D].rearrange("p (n d) -> p n d", d=D)
        acc2 = acc[:, :].rearrange("p (n d) -> p n d", d=2 * D)
        C1, C2 = 1.0 / EF ** 0.5, SILU_2MOM / 8.0
        C_OUT = C2 / (16.0 * 10.0)

        block = ctx.enter_context(nc.Block())

        @block.sync
        def _(sp):
            def load(dst, src, name):
                sp.dma_start(dst, src).then_inc(sem(name), 16)

            for k, name in ((0, "src"), (1, "dst")):
                load(key[k][:, :], a[name].rearrange("(p t) -> p t", p=P), f"s_key{k}")
            load(ef_in, a["edge_attr_8"].rearrange("(p t) c -> p t c", p=P), "s_attr")
            load(y_in, a["edge_attr_4"].rearrange("(p t) c -> p t c", p=P), "s_attr")
            load(w_in[:, :], a["edge_weight"].rearrange("(p t) -> p t", p=P), "s_w")
            load(x_res[:, :, :], a["x"].rearrange("(n p) d -> p n d", p=P), "s_x")
            load(w0, a["w0"].rearrange("(k p) n -> p k n", p=P), "s_w0")
            for k in range(2):
                load(we_f[EA * k:EA * k + EA, :], a["L1_gnn_W_e"], "s_we")
            load(be[:, :], a["be"], "s_we")
            load(bn_in[:, :], a["bn"], "s_we")
            load(eps1[:, :], a["eps"], "s_we")
            for k in range(2):
                load(wup[:, k, :], a[f"L2_gnn_W_up{k}"], "s_wup")

            sp.wait_ge(sem("s_rows"), 1)

            def stage_dst(i):
                for h in range(2):
                    t0 = i * U + h * H8
                    wait(sp, sem(f"s_scat_d{h}"), i * (16 * H8))
                    gate(sp)
                    s = sem(f"s_stage_d{h}")
                    sp.dma_start(stage_d[:, h, :, 0:EA],
                                 a["edge_attr_64"].rearrange("(p t) c -> p t c", p=P)[:, bass.ds(t0, H8), :]).then_inc(s, 16)
                    sp.dma_start(stage_d[:, h, :, EA:ROW], edge_small[:, bass.ds(t0, H8), :]).then_inc(s, 16)
                    sp.dma_start(drow[:, h], row[:, bass.ds(t0, H8)]).then_inc(s, 16)

            turns(sp, ETURNS, stage_dst)

            sp.wait_ge(sem("L0_mm"), NT)
            sp.wait_ge(sem("s_wsplit"), 2)
            load(w1, a["L1_gnn_W1"].rearrange("(k p) n -> p k n", p=P), "s_w1")
            load(w2, a["L1_gnn_W2"].rearrange("(k p) n -> p k n", p=P), "s_w1")

            sp.wait_ge(sem("s_pads"), 16 * PADS)
            for h in range(2):
                sp.wait_ge(sem(f"s_scat_d{h}"), 16 * H8 * ETURNS)

            def chunks(i):
                for h in range(2):
                    H = i * 2 + h
                    wait(sp, sem("L1_part"), (H - 1) * 2)
                    gate(sp)
                    wait(sp, sem("L1_idx"), H - 1)
                    gate(sp)
                    sp.dma_start(chunk[:, h], slots_d_v[:, bass.ds(H * H8, H8), :]).then_inc(sem(f"L1_chunk{h}"), 16)

            turns(sp, TURNS, chunks)

            sp.wait_ge(sem("L1_h2"), 16)
            sp.wait_ge(sem("s_wz"), 1)
            for k in range(H8):
                j, e = divmod(k, 2)
                load(m1[16 * k + C_EF:16 * k + C_EF + EF, j, 64 * e:64 * e + 64], a["L2_gnn_W_mlp1"], "s_w2")
            for e in range(2):
                load(m2[64 * e:64 * e + 64, 64 * e:64 * e + 64], a["L2_gnn_W_mlp2"], "s_w2")
                load(m3[64 * e:64 * e + 64, 64 * e:64 * e + 64], a["L2_gnn_W_mlp3"], "s_w2")
                for q, to in ((1, 0), (0, 1), (2, 2), (3, 3)):
                    load(m4[64 * e:64 * e + 64, P * to:P * to + P], a["L2_gnn_W_mlp4"][:, P * q:P * q + P], "s_w4")
            for k in range(2):
                load(wo[:, 2 * k:2 * k + 2, :], a[f"L2_gnn_W_out{k}"].rearrange("(k p) n -> p k n", p=P), "s_w2")

            def up(i):
                for s in range(2):
                    n = i * 2 + s
                    sp.wait_ge(sem("L1_ub"), n + 1)
                    gate(sp)
                    sp.dma_start(table[1][bass.ds(n * P, P), :], gath[s][:, :]).then_inc(sem(f"L1_st{s}"), 16)

            turns(sp, NT // 2, up)

            def stack2(i):
                for h in range(2):
                    H = i * 2 + h
                    sp.wait_ge(sem("L2_low"), H + 1)
                    gate(sp)
                    wait(sp, sem("L2_w"), (H - 1) * H8)
                    gate(sp)
                    for e in range(2):
                        for r, part in enumerate((last_hi, last_lo)):
                            sp.dma_start(last_parts[h][e][64 * r:64 * r + 64, :].bitcast(F32),
                                         part[64 * e:64 * e + 64, :].bitcast(F32))\
                                .then_inc(sem(f"L2_stack{h}"), 16)

            turns(sp, TURNS, stack2)

            def nodes3(i):
                for s in range(2):
                    n = i * 2 + s
                    sp.wait_ge(sem("L2_x"), n + 1)
                    gate(sp)
                    sp.dma_start(table[2][bass.ds(n * P, P), :], x_res[:, bass.ds(n, 1), :]).then_inc(sem("L2_st"), 16)

            turns(sp, NT // 2, nodes3)
            sp.wait_ge(sem("L2_mm"), NT)
            load(w3, a["w3"].rearrange("(k p) n -> p k n", p=P), "s_w3")
            for k, name in enumerate(("bias", "gamma", "beta")):
                load((bias3, gamma3, beta3)[k], a[name], "s_w3")

            def store(i):
                for s in range(2):
                    n = i * 2 + s
                    sp.wait_ge(sem("L3_y"), n + 1)
                    gate(sp)
                    sp.dma_start(a["out"][bass.ds(n * P, P), :], dy[s]).then_inc(sem(f"L3_st{s}"), 16)

            turns(sp, NT // 2, store)
            for s in range(2):
                sp.wait_ge(sem(f"L3_st{s}"), 16 * (NT // 2))

        @block.gpsimd
        def _(pool):
            pool.memset(pad_d[:, :], 0.0).then_inc(sem("s_pad0"), 1)
            pool.iota(iota[:, :], [[1, ST]], 0, 0, True).then_inc(sem("s_iota"), 1)
            pool.iota(pad_n[:, :], [[1, PADS]], 0, PADS, True).then_inc(sem("s_iota"), 1)
            pool.wait_ge(sem("s_pad0"), 1)
            pool.memset(pad_d[:, EA + C_LOC:EA + C_LOC + 1], -1.0).then_inc(sem("s_pad"), 1)
            pool.memset(edge_small[:, :, :], 0.0).then_inc(sem("s_pad"), 1)
            pool.memset(ident[:, :], 0.0).then_inc(sem("s_id"), 1)
            pool.memset(tri[:, :], 0.0).then_inc(sem("s_id"), 1)
            pool.memset(ones[:, :], 1.0).then_inc(sem("s_ones"), 1)
            pool.memset(ones2[:, :], 1.0).then_inc(sem("s_ones"), 1)
            pool.memset(eps_ln[:, :], LN_EPS).then_inc(sem("s_ones"), 1)
            pool.wait_ge(sem("s_id"), 2)
            pool.affine_select(out=ident[:, :], in_=ident[:, :], compare_op=ALU.not_equal, fill=1.0, base=0,
                               pattern=[[-1, P]], channel_multiplier=1).then_inc(sem("s_id"), 1)
            pool.affine_select(out=tri[:, :], in_=tri[:, :], compare_op=ALU.is_ge, fill=1.0, base=0,
                               pattern=[[-1, P]], channel_multiplier=1).then_inc(sem("s_id"), 1)

            def scatter(i):
                for h in range(2):
                    pool.wait_ge(sem(f"s_stage_d{h}"), i * 48 + 48)
                    gate(pool)
                    for k in range(H8):
                        pool.indirect_dma_start(slots_d, bass.IndirectOffsetOnAxis(ap=drow[:, h, k:k + 1], axis=0),
                                                stage_d[:, h, k, :], None).then_inc(sem(f"s_scat_d{h}"), 16)

            def gather(L, source, ready, total, free):
                def body(i):
                    for j in range(U):
                        h, k = divmod(j, H8)
                        T = i * U + j
                        pool.wait_ge(sem(f"L{L}_idx"), i * 2 + h + 1)
                        wait(pool, sem(f"L{L}_{free}"), T - H8 + 1)
                        gate(pool)
                        pool.wait_ge(sem(ready), total)
                        pool.indirect_dma_start(gath[k][:, :], None, source,
                                                bass.IndirectOffsetOnAxis(ap=idx[:, h, k:k + 1], axis=0))\
                            .then_inc(sem(f"gath{k}"), 16)

                turns(pool, TURNS, body)

            pool.wait_ge(sem("s_pad"), 2)
            for k in range(PADS):
                pool.wait_ge(sem("s_rows"), 1)
                pool.indirect_dma_start(slots_d, bass.IndirectOffsetOnAxis(ap=pad_row[:, k:k + 1], axis=0),
                                        pad_d[:, :], None).then_inc(sem("s_pads"), 16)
            turns(pool, ETURNS, scatter)
            pool.wait_ge(sem("L0_pst0"), 16 * (NT // 2))
            gather(0, proj0, "L0_pst1", 16 * (NT // 2), "seg")
            pool.wait_ge(sem("L0_z"), NT)
            pool.memset(acc[:, 0:NT * D], 0.0).then_inc(sem("s_az"), 1)
            pool.wait_ge(sem("L0_st0"), 16 * (NT // 2))
            gather(1, table[0], "L0_st1", 16 * (NT // 2), "add")
            pool.wait_ge(sem("L1_h2"), 16)
            pool.memset(wbuf[:, 0:768], 0.0).then_inc(sem("s_wz"), 1)
            pool.memset(acc[:, :], 0.0).then_inc(sem("s_az"), 1)
            pool.wait_ge(sem("L1_st0"), 16 * (NT // 2))
            gather(2, table[1], "L1_st1", 16 * (NT // 2), "prod")
            pool.wait_ge(sem("L2_hs"), 1)
            pool.memset(seen[:, :, :], 0.0).then_inc(sem("s_az"), 1)
            pool.wait_ge(sem("L2_hs"), NT)
            pool.memset(acc[:, 0:NT * D], 0.0).then_inc(sem("s_az"), 1)
            gather(3, table[2], "L2_st", 16 * NT, "seg")

        @block.scalar
        def _(act):
            act.wait_ge(sem("s_attr"), 32)
            act.wait_ge(sem("s_pad"), 2)
            nc.scalar.activation(edge_small[:, :, C_EF:C_EF + EF], ef_in, ACT.Copy).then_inc(sem("s_small"), 1)
            nc.scalar.activation(edge_small[:, :, C_Y:C_Y + NY], y_in, ACT.Copy).then_inc(sem("s_small"), 1)
            act.wait_ge(sem("s_key0"), 16)
            nc.scalar.activation(edge_small[:, :, C_SRC], key[0][:, :], ACT.Copy).then_inc(sem("s_small"), 1)
            act.wait_ge(sem("s_key1"), 16)
            nc.scalar.activation(dst_f[:, :], key[1][:, :], ACT.Copy).then_inc(sem("s_vals"), 1)
            act.wait_ge(sem("s_w"), 16)
            nc.scalar.activation(w_hi[:, :], w_in[:, :], ACT.Copy).then_inc(sem("s_vals"), 1)

            act.wait_ge(sem("s_small"), 3)
            act.wait_ge(sem("s_x"), 16)

            def copy0(i, ss):
                at_n = ahead(i, ss, 2, NT // 2)
                if at_n is None:
                    return
                _, s, n = at_n
                wait(act, sem("L0_tr"), n - 1)
                nc.scalar.activation(dense0[:, s, :], x_res[:, bass.ds(n, 1), :], ACT.Copy).then_inc(sem("L0_hs"), 1)

            def turned0(i, ss):
                at_n = ahead(i, ss, 2, NT // 2)
                if at_n is None:
                    return
                _, s, n = at_n
                act.wait_ge(sem("L0_tr"), n + 1)
                wait(act, sem("L0_mm"), n - 1)
                nc.scalar.activation(dense0[:, 2 + s, :], bank[6 + s][:, :], ACT.Copy).then_inc(sem("L0_hT"), 1)

            copy0(0, 0)
            copy0(0, 1)
            turned0(0, 0)

            def project0(i):
                for s in range(2):
                    n = i * 2 + s
                    copy0(i, s + 2)
                    turned0(i, s + 1)
                    act.wait_ge(sem("L0_mm"), n + 1)
                    wait(act, sem(f"L0_pst{s}"), i * 16)
                    nc.scalar.activation(dense0[:, 4 + s, :], bank[4 + s][:, :], ACT.Copy).then_inc(sem("L0_pr"), 1)
                    act.wait_ge(sem("L0_pr"), n + 1)
                    act.dma_start(proj0[bass.ds(n * P, P), :], dense0[:, 4 + s, :]).then_inc(sem(f"L0_pst{s}"), 16)

            turns(act, NT // 2, project0)

            act.wait_ge(sem("s_loc1"), 1)

            def scale0(i):
                for j in range(U):
                    t = i * U + j
                    act.wait_ge(sem("s_in_lane"), t + 1)
                    wait(act, sem("s_placed"), t - 3)
                    for value, of in enumerate((dst_f, loc_f, w_hi)[:3 - j % 2]):
                        ins = nc.scalar.activation(of_lane[j % 4][:, value, :], in_lane[:, j % 4, :], ACT.Copy,
                                                   scale=of[:, bass.ds(t, 1)].bitcast(F32))
                    ins.then_inc(sem("s_scaled"), 1)

            turns(act, ETURNS, scale0)

            act.wait_ge(sem("s_slots0"), 3)

            def idx0(i):
                for h in range(2):
                    H = i * 2 + h
                    wait(act, sem("L0_seg"), (H - 1) * H8)
                    wait(act, sem("L0_oh"), (H - 1) * H8)
                    nc.scalar.activation(slot0[:, h], slots0[:, bass.ds(H * H8, H8), :], ACT.Copy)
                    nc.scalar.activation(idx[:, h], slots0[:, bass.ds(H * H8, H8), 0], ACT.Copy).then_inc(sem("L0_idx"), 1)

            turns(act, TURNS, idx0)

            def root(L, n, s):
                act.wait_ge(sem("norm_mv"), NORMS[L] + n + 1)
                nc.scalar.activation(std[:, s:s + 1], mv[:, s, 1:2], ACT.Sqrt, bias=eps_ln[:, :]).then_inc(sem("norm_std"), 1)

            def nodes0(i):
                for s in range(2):
                    n = i * 2 + s
                    root(0, n, s)
                    act.wait_ge(sem("L0_y"), n + 1)
                    act.dma_start(table[0][bass.ds(n * P, P), :], dense0[:, 2 + s, :]).then_inc(sem(f"L0_st{s}"), 16)

            turns(act, NT // 2, nodes0)

            def small1(i, hh):
                at_h = ahead(i, hh, 2, TURNS)
                if at_h is None:
                    return
                turn, h, H = at_h
                act.wait_ge(sem(f"L1_chunk{h}"), turn * 16 + 16)
                wait(act, sem("L1_add"), (H - 1) * H8)
                nc.scalar.activation(small[:, bass.ds(H * H8, H8), :], chunk[:, h, :, EA:ROW], ACT.Copy)
                nc.scalar.activation(idx[:, h], chunk[:, h, :, EA + C_SRC], ACT.Copy).then_inc(sem("L1_idx"), 1)

            def turned1(i, qq):
                at_q = ahead(i, qq, 4, TURNS)
                if at_q is None:
                    return
                turn, q, Q = at_q
                act.wait_ge(sem("L1_tr"), Q + 1)
                wait(act, sem("L1_mm"), (Q - 3) * 4)
                nc.scalar.activation(rowT[q][:, :], bank[6 + q % 2][:, :], ACT.Copy).then_inc(sem("L1_rowT"), 1)

            def relu1(i, jj):
                at_t = ahead(i, jj, U, TURNS)
                if at_t is None:
                    return
                turn, j, T = at_t
                k = j % 4
                act.wait_ge(sem("L1_add"), T + 1)
                if k == 3:
                    wait(act, sem("L1_seg"), T - 3)
                nc.scalar.activation(msg_hi[:, :] if k == 3 else msg[k][:, :], msg[k][:, :], ACT.Relu).then_inc(sem("L1_relu"), 1)

            def high1(i, hh):
                at_h = ahead(i, hh, 2, TURNS)
                if at_h is None:
                    return
                turn, h, H = at_h
                act.wait_ge(sem(f"L1_chunk{h}"), turn * 16 + 16)
                wait(act, sem("L1_tr"), (H - 1) * 2)
                nc.scalar.activation(parts[h][:, :, 0:EA], chunk[:, h, :, 0:EA], ACT.Copy).then_inc(sem("L1_high"), 1)

            for s in range(2):
                act.wait_ge(sem(f"L0_st{s}"), 16 * (NT // 2))
            high1(0, 0)
            small1(0, 0)
            high1(0, 1)
            turned1(0, 0)
            turned1(0, 1)
            for T in range(3):
                relu1(0, T)

            def edges1(i):
                for j in range(U):
                    if j % H8 == 0:
                        small1(i, j // H8 + 1)
                    if j % H8 == 4:
                        high1(i, j // H8 + 2)
                    if j % 4 == 0:
                        turned1(i, j // 4 + 2)
                    relu1(i, j + 3)

            turns(act, TURNS, edges1)

            def turned1n(i):
                for s in range(2):
                    n = i * 2 + s
                    act.wait_ge(sem("L1_ntr"), n + 1)
                    nc.scalar.activation(hT[:, :, bass.ds(n * P, P)],
                                         bank[s][:, :].rearrange("p (k n) -> p k n", k=4), ACT.Copy).then_inc(sem("L1_hT"), 1)

            turns(act, NT // 2, turned1n)

            def evac1(c):
                for f in range(8):
                    F = c * 8 + f
                    act.wait_ge(sem("L1_h1"), F + 1)
                    nc.scalar.activation(aT[:, f, bass.ds(c * 512, 512)], bank[2 + f % 4][:, :], ACT.Identity,
                                         bias=b1[:, f:f + 1]).then_inc(sem("L1_ev1"), 1)

            turns(act, 4, evac1)

            act.wait_ge(sem("L1_bmv"), 1)
            nc.scalar.activation(bstd[:, :], bmv[:, :, 1], ACT.Sqrt, bias=eps_ln[:, :]).then_inc(sem("L1_bstd"), 1)
            act.wait_ge(sem("L1_bn"), 1)

            def silu1(c):
                if isinstance(c, int) and c >= 4:
                    return
                for f in range(8):
                    at = aT[:, f, bass.ds(c * 512, 512)]
                    nc.scalar.activation(at, at, ACT.Silu, bias=bshift[:, f:f + 1], scale=bscale[:, f:f + 1])\
                        .then_inc(sem("L1_silu"), 1)

            silu1(0)

            def second1(c):
                silu1(c + 1)
                for g in range(4):
                    act.wait_ge(sem("L1_h2"), c * 4 + g + 1)
                    nc.scalar.activation(hT[:, g, bass.ds(c * 512, 512)], bank[2 + g][:, :], ACT.Identity,
                                         bias=b2[:, g:g + 1]).then_inc(sem("L1_ev2"), 1)

            turns(act, 4, second1)

            act.wait_ge(sem("L1_bmv"), 2)
            nc.scalar.activation(bstd[:, 0:4], bmv[:, 0:4, 1], ACT.Sqrt, bias=eps_ln[:, :]).then_inc(sem("L1_bstd"), 1)
            act.wait_ge(sem("L1_bn"), 2)

            def act1(i):
                for s in range(2):
                    n = i * 2 + s
                    wait(act, sem("L1_btr"), n - 1)
                    for g in range(4):
                        ins = nc.scalar.activation(gath[2 + s][:, P * g:P * g + P], hT[:, g, bass.ds(n * P, P)], ACT.Silu,
                                                   bias=bshift[:, g:g + 1], scale=bscale[:, g:g + 1])
                    ins.then_inc(sem("L1_sT"), 1)

            turns(act, NT // 2, act1)

            act.wait_ge(sem("L1_mv"), 1)
            nc.scalar.activation(nstd[:, :], nmv[:, :, 1], ACT.Sqrt, bias=eps_ln[:, :]).then_inc(sem("L1_std"), 1)

            def keep1(i, ss):
                at_n = ahead(i, ss, 2, NT // 2)
                if at_n is None:
                    return
                _, s, n = at_n
                act.wait_ge(sem("L1_utr"), n + 1)
                wait(act, sem("L1_umm"), n - 1)
                nc.scalar.activation(gath[6 + s][:, :], bank[2 + s][:, :], ACT.Copy).then_inc(sem("L1_uT"), 1)

            keep1(0, 0)

            def up1(i):
                for s in range(2):
                    n = i * 2 + s
                    keep1(i, s + 1)
                    act.wait_ge(sem("L1_umm"), n + 1)
                    wait(act, sem(f"L1_st{s}"), i * 16)
                    nc.scalar.activation(gath[s][:, :], bank[4 + s][:, :], ACT.Copy, scale=P ** -0.5).then_inc(sem("L1_ub"), 1)

            turns(act, NT // 2, up1)

            def slots2(i, hh):
                at_h = ahead(i, hh, 2, TURNS)
                if at_h is None:
                    return
                turn, h, H = at_h
                wait(act, sem("L2_prod"), (H - 1) * H8)
                gate(act)
                nc.scalar.activation(slot2[:, h], small[:, bass.ds(H * H8, H8), :], ACT.Copy)
                nc.scalar.activation(idx[:, h], small[:, bass.ds(H * H8, H8), C_SRC], ACT.Copy).then_inc(sem("L2_idx"), 1)

            def attributes2(i, hh):
                at_h = ahead(i, hh, 2, TURNS)
                if at_h is None:
                    return
                turn, h, H = at_h
                wait(act, sem("L2_tr"), H)
                gate(act)
                nc.scalar.activation(ef_in2[:, :, :], small[:, bass.ds(H * H8, H8), :], ACT.Copy).then_inc(sem("L2_ef"), 1)

            def turned2(i, hh):
                at_h = ahead(i, hh, 2, TURNS)
                if at_h is None:
                    return
                turn, h, H = at_h
                act.wait_ge(sem("L2_tr"), H + 1)
                wait(act, sem("L2_z"), H * 3 - 2)
                nc.scalar.activation(efT[:, :], bank[7][:, 0:P], ACT.Copy).then_inc(sem("L2_efT"), 1)

            def hidden2(i, hh, k):
                at_h = ahead(i, hh, 2, TURNS)
                if at_h is None:
                    return
                turn, h, H = at_h
                act.wait_ge(sem("L2_z"), H * 3 + k + 1)
                if k == 2:
                    wait(act, sem("L2_low"), H)
                nc.scalar.activation((hid[0], hid[1], last)[k], bank[6][:, :], ACT.Silu, scale=C1 if k == 0 else C2)\
                    .then_inc(sem("L2_h"), 1)
                if k == 2:
                    wait(act, sem(f"L2_stack{1 - h}"), (turn + h) * 64)
                    act.wait_ge(sem("L2_h"), H * 3 + 3)
                    nc.scalar.activation(last_hi[:, :], last, ACT.Copy).then_inc(sem("L2_high"), 1)

            def scaled2(i, jj):
                at_t = ahead(i, jj, U, TURNS)
                if at_t is None:
                    return
                turn, j, T = at_t
                h, k = divmod(j, H8)
                y = slot2[:, h, k, C_Y:C_Y + NY]
                act.wait_ge(sem(f"gath{k}"), 2 * G_ALL + turn * 32 + 16 * h + 16)
                wait(act, sem("L2_prod"), T - 1)
                nc.scalar.activation(dot[j % 2][:, :], gath[k][:, P:2 * P], ACT.Copy, scale=y[:, 1:2]).then_inc(sem("L2_dot"), 1)
                act.wait_ge(sem("L2_oh"), T + 1)
                wait(act, sem("L2_seg"), T - 3)
                for m in range(4):
                    nc.scalar.activation(scaled[j % 4][:, m, :], oh2[:, k, :], ACT.Copy, scale=y[:, m:m + 1])\
                        .then_inc(sem("L2_ohy"), 1)

            attributes2(0, 0)
            slots2(0, 0)
            turned2(0, 0)
            for k in range(3):
                hidden2(0, 0, k)
            attributes2(0, 1)
            turned2(0, 1)
            hidden2(0, 1, 0)
            hidden2(0, 1, 1)
            for T in range(3):
                scaled2(0, T)

            def edges2(i):
                for j in range(U):
                    if j % H8 == 0:
                        slots2(i, j // H8 + 1)
                    if j % H8 == 1:
                        attributes2(i, j // H8 + 2)
                        hidden2(i, j // H8 + 1, 2)
                    if j % H8 == 3:
                        turned2(i, j // H8 + 2)
                    if j % H8 in (5, 7):
                        hidden2(i, j // H8 + 2, j % H8 // 2 - 2)
                    scaled2(i, j + 3)

            turns(act, TURNS, edges2)

            def copy2(i, ss):
                at_n = ahead(i, ss, 2, NT // 2)
                if at_n is None:
                    return
                _, s, n = at_n
                act.wait_ge(sem("L2_acc"), NG)
                wait(act, sem("L2_ntr"), n - 1)
                nc.scalar.activation(dn[s][:, :, :], acc2[:, bass.ds(n, 1), :], ACT.Copy).then_inc(sem("L2_hs"), 1)

            def turned2n(i, ss):
                at_n = ahead(i, ss, 2, NT // 2)
                if at_n is None:
                    return
                _, s, n = at_n
                act.wait_ge(sem("L2_ntr"), n + 1)
                wait(act, sem("L2_mm"), n - 1)
                for b in range(2):
                    nc.scalar.activation(dnT[s][:, 4 * b:4 * b + 4, :], bank[2 * s + b][:, :], ACT.Copy).then_inc(sem("L2_nT"), 1)

            copy2(0, 0)
            copy2(0, 1)
            turned2n(0, 0)
            copy2(0, 2)
            turned2n(0, 1)

            def nodes2(i):
                for s in range(2):
                    n = i * 2 + s
                    copy2(i, s + 3)
                    turned2n(i, s + 2)
                    root(2, n, s)

            turns(act, NT // 2, nodes2, last=2)

            def idx3(i, hh):
                at_h = ahead(i, hh, 2, TURNS)
                if at_h is None:
                    return
                _, h, H = at_h
                wait(act, sem("L3_seg"), (H - 1) * H8)
                wait(act, sem("L3_oh"), (H - 1) * H8)
                nc.scalar.activation(slot3[:, h], small[:, bass.ds(H * H8, H8), :], ACT.Copy)
                nc.scalar.activation(idx[:, h], small[:, bass.ds(H * H8, H8), C_SRC], ACT.Copy).then_inc(sem("L3_idx"), 1)

            idx3(0, 0)

            def edges3(i):
                own = not (isinstance(i, int) and i in (0, TURNS - 1))
                n = i - 1
                if own:
                    wait(act, sem("L3_xtr"), n)
                    gate(act)
                    nc.scalar.activation(dn[0][:, 0:4, :], x_res[:, bass.ds(n, 1), :], ACT.Copy).then_inc(sem("L3_xs"), 1)
                idx3(i, 1)
                if own:
                    act.wait_ge(sem("L3_xtr"), n + 1)
                    nc.scalar.activation(dnT[0][:, 0:4, :], bank[6][:, :], ACT.Copy).then_inc(sem("L3_xT"), 1)
                idx3(i, 2)

            turns(act, TURNS, edges3, first=2)

            def copy3(i, ss):
                at_n = ahead(i, ss, 2, NT // 2)
                if at_n is None:
                    return
                _, s, n = at_n
                act.wait_ge(sem("L3_acc"), NG)
                wait(act, sem("L3_ntr"), n - 1)
                nc.scalar.activation(dn[s][:, 4:8, :], acc_n[:, bass.ds(n, 1), :], ACT.Copy).then_inc(sem("L3_hs"), 1)

            def turned3(i, ss):
                at_n = ahead(i, ss, 2, NT // 2)
                if at_n is None:
                    return
                _, s, n = at_n
                act.wait_ge(sem("L3_ntr"), n + 1)
                wait(act, sem("L3_mm"), n - 1)
                nc.scalar.activation(dnT[s][:, 4:8, :], bank[2 * s][:, :], ACT.Copy).then_inc(sem("L3_nT"), 1)

            copy3(0, 0)
            copy3(0, 1)
            turned3(0, 0)
            copy3(0, 2)
            turned3(0, 1)
            root(3, 0, 0)

            def nodes3(i):
                for s in range(2):
                    n = i * 2 + s
                    last = isinstance(n, int) and n == NT - 1
                    copy3(i, s + 3)
                    turned3(i, s + 2)
                    if not last:
                        root(3, n * 2 + 1, 1 - s)
                    root(3, n * 2 + (1 if last else 2), 2 + s)

            turns(act, NT // 2, nodes3, last=2)

        @block.tensor
        def _(pe):
            pe.wait_ge(sem("s_id"), 4)
            pe.wait_ge(sem("s_ones"), 3)
            def counts(k):
                pe.wait_ge(sem("s_rcount"), k + 1)
                nc.tensor.matmul(bank[0][:, 0:NT], tri[:, :], rcount[:, :], start=True, stop=True)
                nc.tensor.matmul(bank[1][:, 0:NT], ones[:, :], rcount[:, :], start=True, stop=True).then_inc(sem("s_counts"), 1)

            counts(0)

            def turn0(i, ss):
                at_n = ahead(i, ss, 2, NT // 2)
                if at_n is None:
                    return
                _, s, n = at_n
                pe.wait_ge(sem("L0_hs"), n + 1)
                wait(pe, sem("L0_hT"), n - 1)
                for k in range(4):
                    ins = nc.tensor.transpose(bank[6 + s][:, P * k:P * k + P], dense0[:, s, P * k:P * k + P], ident[:, :])
                ins.then_inc(sem("L0_tr"), 1)

            pe.wait_ge(sem("s_w0"), 16)
            turn0(0, 0)

            def nodes0(i):
                for s in range(2):
                    n = i * 2 + s
                    turn0(i, s + 1)
                    pe.wait_ge(sem("L0_hT"), n + 1)
                    wait(pe, sem("L0_pr"), n - 1)
                    for k in range(4):
                        ins = nc.tensor.matmul(bank[4 + s][:, :], dense0[:, 2 + s, P * k:P * k + P], w0[:, k, :],
                                               start=k == 0, stop=k == 3)
                    ins.then_inc(sem("L0_mm"), 1)

            nodes0(0)
            with pe.Fori(1, NT // 4) as i:
                nodes0(i)
            counts(1)
            with pe.Fori(NT // 4, NT // 2 - 1) as i:
                nodes0(i)
            nodes0(NT // 2 - 1)

            def place0(i):
                for j in range(U):
                    t = i * U + j
                    pe.wait_ge(sem("s_onehots"), t + 1)
                    pe.wait_ge(sem("s_scaled"), t + 1)
                    for value in range(4):
                        ins = nc.tensor.matmul(bank[value][:, 0:ST], of_lane[j % 4][:, value, :], of_tile[j % 4][:, :],
                                               start=isinstance(i, int) and i == 0 and j == 0,
                                               stop=isinstance(i, int) and i == ETURNS - 1 and j == U - 1)
                    ins.then_inc(sem("s_placed"), 1)

            turns(pe, ETURNS, place0)
            pe.wait_ge(sem("s_slots0"), 3)

            def sums(L, oh, aside=None):
                def body(i):
                    for j in range(U):
                        h, k = divmod(j, H8)
                        T = i * U + j
                        if aside is not None:
                            aside(i, j)
                        pe.wait_ge(sem(f"L{L}_oh"), T + 1)
                        pe.wait_ge(sem(f"gath{k}"), L * G_ALL + i * 32 + 16 * h + 16)
                        if j % 2 == 0:
                            wait(pe, sem(f"L{L}_acc"), i * 8 + j // 2 - 3)
                        nc.tensor.matmul(bank[j // 2 % 4][:, :], oh[:, k, :], gath[k][:, :], start=j % 2 == 0, stop=j % 2 == 1)\
                            .then_inc(sem(f"L{L}_seg"), 1)

                turns(pe, TURNS, body, first=2 if L == 3 else 1)

            sums(0, oh0)
            pe.wait_ge(sem("L0_acc"), NG)

            pe.wait_ge(sem("s_wsplit"), 2)

            def turn1(i, qq):
                at_q = ahead(i, qq, 4, TURNS)
                if at_q is None:
                    return
                turn, q, Q = at_q
                h = q // 2
                pe.wait_ge(sem("L1_part"), (turn * 2 + h) * 2 + 2)
                wait(pe, sem("L1_rowT"), Q - 1)
                for k in range(4):
                    ins = nc.tensor.transpose(bank[6 + q % 2][:, P * k:P * k + P],
                                              parts[h][:, 4 * (q % 2) + k, :].bitcast(F32), ident[:, :])
                ins.then_inc(sem("L1_tr"), 1)

            def mm1(i, jj):
                at_t = ahead(i, jj, U, TURNS)
                if at_t is None:
                    return
                turn, j, T = at_t
                q, k = divmod(j, 4)
                pe.wait_ge(sem("L1_rowT"), turn * 4 + q + 1)
                wait(pe, sem("L1_add"), T - 3)
                rows = rowT[q][:, P * k:P * k + P]
                nc.tensor.matmul(bank[j % 4][:, :], rows, we_hi[:, :], start=True, stop=False)
                nc.tensor.matmul(bank[j % 4][:, :], rows, we_lo[:, :], start=False, stop=True)\
                    .then_inc(sem("L1_mm"), 1)

            turn1(0, 0)
            turn1(0, 1)
            for T in range(5):
                mm1(0, T)

            def edges1(i):
                for j in range(U):
                    T = i * U + j
                    if j % 4 == 0:
                        turn1(i, j // 4 + 2)
                    mm1(i, j + 5)
                    pe.wait_ge(sem("L1_oh"), T + 1)
                    pe.wait_ge(sem("L1_relu"), T + 1)
                    if j % 2 == 0:
                        wait(pe, sem("L1_acc"), i * 8 + j // 2 - 1)
                    if j % 4 == 3:
                        pe.wait_ge(sem("L1_rest"), i * 4 + j // 4 + 1)
                        ends = oh1_r[j % H8 // 4][:, :]
                        nc.tensor.matmul(bank[4 + j // 2 % 2][:, :], ends, msg_hi[:, :], start=False, stop=False)
                        nc.tensor.matmul(bank[4 + j // 2 % 2][:, :], ends, msg_lo[:, :], start=False, stop=True)\
                            .then_inc(sem("L1_seg"), 1)
                    else:
                        nc.tensor.matmul(bank[4 + j // 2 % 2][:, :], oh1[:, j % H8, :], msg[j % 4][:, :],
                                         start=j % 2 == 0, stop=j % 2 == 1).then_inc(sem("L1_seg"), 1)

            turns(pe, TURNS, edges1)

            def turn1n(i):
                for s in range(2):
                    n = i * 2 + s
                    pe.wait_ge(sem("L1_hs"), n + 1)
                    wait(pe, sem("L1_hT"), n - 1)
                    for k in range(4):
                        ins = nc.tensor.transpose(bank[s][:, P * k:P * k + P], gath[s][:, P * k:P * k + P], ident[:, :])
                    ins.then_inc(sem("L1_ntr"), 1)

            turns(pe, NT // 2, turn1n)
            pe.wait_ge(sem("s_w1"), 32)
            pe.wait_ge(sem("L1_hT"), NT)
            pe.wait_ge(sem("L1_acc"), NG)

            def first1(c):
                for f in range(8):
                    wait(pe, sem("L1_ev1"), c * 8 + f - 3)
                    for k in range(4):
                        ins = nc.tensor.matmul(bank[2 + f % 4][:, :], w1[:, k, P * f:P * f + P], hT[:, k, bass.ds(c * 512, 512)],
                                               start=k == 0, stop=k == 3)
                    ins.then_inc(sem("L1_h1"), 1)

            turns(pe, 4, first1)
            pe.wait_ge(sem("L1_ev1"), 32)

            def second1(c):
                for g in range(4):
                    wait(pe, sem("L1_ev2"), c * 4 + g - 3)
                    for f in range(8):
                        if g == 0:
                            pe.wait_ge(sem("L1_silu"), c * 8 + f + 1)
                        ins = nc.tensor.matmul(bank[2 + g][:, :], w2[:, f, P * g:P * g + P], aT[:, f, bass.ds(c * 512, 512)],
                                               start=f == 0, stop=f == 7)
                    ins.then_inc(sem("L1_h2"), 1)

            turns(pe, 4, second1)

            def back1(i):
                for s in range(2):
                    n = i * 2 + s
                    pe.wait_ge(sem("L1_sT"), n + 1)
                    wait(pe, sem("L1_z"), n - 1)
                    for g in range(4):
                        ins = nc.tensor.transpose(bank[s][:, P * g:P * g + P], gath[2 + s][:, P * g:P * g + P], ident[:, :])
                    ins.then_inc(sem("L1_btr"), 1)

            turns(pe, NT // 2, back1)

            def uturn(i, ss):
                at_n = ahead(i, ss, 2, NT // 2)
                if at_n is None:
                    return
                _, s, n = at_n
                pe.wait_ge(sem("L1_xn"), n + 1)
                wait(pe, sem("L1_uT"), n - 1)
                nc.tensor.transpose(bank[2 + s][:, 0:P], gath[4 + s][:, 0:P], ident[:, :])
                for m in range(3):
                    ins = nc.tensor.transpose(bank[2 + s][:, P * m + P:P * m + 2 * P],
                                              gath[4 + s][:, P:D].rearrange("p (u m) -> p m u", m=3)[:, m, :], ident[:, :])
                ins.then_inc(sem("L1_utr"), 1)

            pe.wait_ge(sem("s_wup"), 32)
            pe.wait_ge(sem("L1_ev2"), 16)
            uturn(0, 0)

            def up1(i):
                for s in range(2):
                    n = i * 2 + s
                    uturn(i, s + 1)
                    pe.wait_ge(sem("L1_uT"), n + 1)
                    wait(pe, sem("L1_ub"), n - 1)
                    for m in range(4):
                        ins = nc.tensor.matmul(bank[4 + s][:, P * m:P * m + P], gath[6 + s][:, P * m:P * m + P],
                                               wup[:, min(m, 1), :], start=True, stop=True)
                    ins.then_inc(sem("L1_umm"), 1)

            turns(pe, NT // 2, up1)

            pe.wait_ge(sem("s_w2"), 16 * (8 + 4 + 2))
            pe.wait_ge(sem("s_wsplit"), 4)
            pe.wait_ge(sem("L1_ub"), NT)

            def turn2(i, hh):
                at_h = ahead(i, hh, 2, TURNS)
                if at_h is None:
                    return
                turn, h, H = at_h
                pe.wait_ge(sem("L2_ef"), H + 1)
                wait(pe, sem("L2_efT"), H)
                nc.tensor.transpose(bank[7][:, 0:P], ef_in2[:, :, :].rearrange("p t c -> p (t c)"), ident[:, :]).then_inc(sem("L2_tr"), 1)

            def layer2(i, hh, k):
                at_h = ahead(i, hh, 2, TURNS)
                if at_h is None:
                    return
                turn, h, H = at_h
                wait(pe, sem("L2_h"), H * 3 + k)
                if k == 0:
                    pe.wait_ge(sem("L2_efT"), H + 1)
                    for j in range(4):
                        ins = nc.tensor.matmul(bank[6][:, P * j:P * j + P], m1[:, j, :], efT[:, :], start=True, stop=True)
                else:
                    ins = nc.tensor.matmul(bank[6][:, :], (m2, m3)[k - 1], hid[k - 1], start=True, stop=True)
                ins.then_inc(sem("L2_z"), 1)

            def weights2(i, jj):
                at_t = ahead(i, jj, U, TURNS)
                if at_t is None:
                    return
                turn, j, T = at_t
                h, k = divmod(j, H8)
                pe.wait_ge(sem(f"L2_stack{h}"), turn * 64 + 64)
                wait(pe, sem("L2_prod"), T - 1)
                slots = last_parts[h][k % 2][:, P * (k // 2):P * (k // 2) + P]
                nc.tensor.matmul(bank[4 + j % 2][:, :], slots, we_hi[:, :], start=True, stop=False)
                nc.tensor.matmul(bank[4 + j % 2][:, :], slots, we_lo[:, :], start=False, stop=True).then_inc(sem("L2_w"), 1)

            turn2(0, 0)
            for k in range(3):
                layer2(0, 0, k)
            turn2(0, 1)
            layer2(0, 1, 0)
            layer2(0, 1, 1)
            weights2(0, 0)
            weights2(0, 1)

            def edges2(i):
                for j in range(U):
                    T = i * U + j
                    if j % H8 == 0:
                        layer2(i, j // H8 + 1, 2)
                    if j % H8 == 2:
                        turn2(i, j // H8 + 2)
                    if j % H8 in (4, 6):
                        layer2(i, j // H8 + 2, j % H8 // 2 - 2)
                    weights2(i, j + 2)
                    pe.wait_ge(sem("L2_ohy"), T * 4 + 4)
                    pe.wait_ge(sem("L2_prod"), T + 1)
                    if j % 2 == 0:
                        wait(pe, sem("L2_acc"), i * 8 + j // 2 - 1)
                    first, last, b = j % 2 == 0, j % 2 == 1, j // 2 % 2
                    q, o = prod[j % 4], scaled[j % 4]
                    nc.tensor.matmul(bank[b][:, :], o[:, 0, :], q[:, 1:5, :], start=first, stop=last)
                    for m in range(3):
                        nc.tensor.matmul(bank[2 + b][:, P * m:P * m + P], o[:, 1 + m, :], q[:, 0, :],
                                         start=first and m == 0, stop=False, skip_group_check=True)
                    nc.tensor.matmul(bank[2 + b][:, 3 * P:4 * P], oh2[:, j % H8, :], q[:, 5, :], start=False, stop=last,
                                     skip_group_check=True).then_inc(sem("L2_seg"), 1)

            turns(pe, TURNS, edges2)

            def turn2n(L, i, ss):
                at_n = ahead(i, ss, 2, NT // 2)
                if at_n is None:
                    return
                _, s, n = at_n
                pe.wait_ge(sem(f"L{L}_hs"), n + 1)
                wait(pe, sem(f"L{L}_nT"), (n - 1) * (2 if L == 2 else 1))
                for k in (range(8) if L == 2 else range(4, 8)):
                    at = bank[2 * s + (k // 4 if L == 2 else 0)]
                    ins = nc.tensor.transpose(at[:, P * (k % 4):P * (k % 4) + P], dn[s][:, k, :], ident[:, :])
                ins.then_inc(sem(f"L{L}_ntr"), 1)

            pe.wait_ge(sem("L2_acc"), NG)
            turn2n(2, 0, 0)
            turn2n(2, 0, 1)

            def nodes2(i):
                for s in range(2):
                    n = i * 2 + s
                    pe.wait_ge(sem("L2_nT"), n * 2 + 2)
                    wait(pe, sem("L2_nz"), n - 1)
                    for m, (k0, k1) in enumerate(((0, 7), (4, 1), (5, 2), (6, 3))):
                        for r, k in enumerate((k0, k1)):
                            ins = nc.tensor.matmul(bank[4 + s][:, P * m:P * m + P], dnT[s][:, k, :], wo[:, 2 * min(m, 1) + r, :],
                                                   start=r == 0, stop=r == 1)
                    ins.then_inc(sem("L2_mm"), 1)
                    turn2n(2, i, s + 2)

            turns(pe, NT // 2, nodes2)

            pe.wait_ge(sem("L2_nz"), NT)

            def own3(i, j):
                if isinstance(i, int) and i in (0, TURNS - 1):
                    return
                n = i - 1
                if j < 4:
                    k = j
                    if k == 0:
                        pe.wait_ge(sem("L3_xs"), n + 1)
                    ins = nc.tensor.transpose(bank[6][:, P * k:P * k + P], dn[0][:, k, :], ident[:, :])
                    if k == 3:
                        ins.then_inc(sem("L3_xtr"), 1)
                if j in (5, 8, 11, 14):
                    k = (j - 5) // 3
                    if k == 0:
                        pe.wait_ge(sem("s_w3"), 64)
                        pe.wait_ge(sem("L3_xT"), n + 1)
                        wait(pe, sem("L3_kept"), n * 2)
                    ins = nc.tensor.matmul(bank[7][:, :], dnT[0][:, k, :], w3[:, k, :], start=k == 0, stop=k == 3)
                    if k == 3:
                        ins.then_inc(sem("L3_own"), 1)

            sums(3, oh3, own3)
            pe.wait_ge(sem("L3_acc"), NG)
            for n in range(NT):
                for half in range(2):
                    ins = nc.tensor.matmul(bank[6][:, 2 * n:2 * n + 2], seen[:, n, P * half:P * half + P], ones2[:, :],
                                           start=half == 0, stop=half == 1)
            ins.then_inc(sem("L3_deg"), 1)
            turn2n(3, 0, 0)
            turn2n(3, 0, 1)

            def nodes3(i):
                for s in range(2):
                    n = i * 2 + s
                    pe.wait_ge(sem("L3_nT"), n + 1)
                    wait(pe, sem("L3_z"), n - 1)
                    for k in range(4, 8):
                        ins = nc.tensor.matmul(bank[4 + s][:, :], dnT[s][:, k, :], w3[:, k, :], start=k == 4, stop=k == 7)
                    ins.then_inc(sem("L3_mm"), 1)
                    turn2n(3, i, s + 2)

            turns(pe, NT // 2, nodes3)

        @block.vector
        def _(dve):
            v = nc.vector
            step = Chain(dve, sem("s_step"))

            def bins(turn, k, loc, bin_of):
                dve.wait_ge(sem(f"s_key{k}"), 16)
                step(v.tensor_scalar(hi_i[:, :], key[k][:, :], 7, None, ALU.arith_shift_right))
                step(v.tensor_scalar(lo_i[:, :], key[k][:, :], P - 1, None, ALU.bitwise_and))
                step(v.tensor_copy(hi_f[:, :], hi_i[:, :]))
                dve.wait_ge(sem("s_pad"), 2)
                step(v.tensor_copy(loc, lo_i[:, :]))
                dve.wait_ge(sem("s_iota"), 1)
                step(v.tensor_tensor(is_bin, expand(hi_f[:, :], 1, NT), expand(iota_b, 2, ET), ALU.is_equal))
                flat = is_bin.rearrange("p b t -> p (b t)")
                step(v.tensor_tensor_scan(count.rearrange("p b t -> p (b t)"), flat, flat, 0.0, ALU.add, ALU.bypass))
                step(v.memset(before[:, :], 0.0))
                step(v.tensor_copy(before[:, 1:NT], count[:, 0:NT - 1, ET - 1]))
                v.tensor_tensor(rcount[:, :], count[:, :, ET - 1], before[:, :], ALU.subtract).then_inc(sem("s_rcount"), 1)
                dve.wait_ge(sem("s_counts"), turn + 1)
                step(v.tensor_scalar(tot_i[:, :], bank[1][:, 0:NT], float(GROUP - 1), None, ALU.add))
                step(v.tensor_scalar(grp_i[:, :], tot_i[:, :], 8, None, ALU.arith_shift_right))
                step(v.tensor_copy(grp[:, :], grp_i[:, :]))
                step(v.tensor_tensor_scan(gend[:, :], grp[:, :], grp[:, :], 0.0, ALU.add, ALU.bypass))
                step(v.tensor_tensor(off[:, :], gend[:, :], grp[:, :], ALU.subtract))
                step(v.scalar_tensor_tensor(off[:, :], off[:, :], float(GROUP), bank[0][:, 0:NT], ALU.mult, ALU.add))
                step(v.scalar_tensor_tensor(off[:, :], off[:, :], -1.0, before[:, :], ALU.add, ALU.subtract))
                step(v.tensor_tensor(count, count, expand(off[:, :], 2, ET), ALU.add))
                step(v.tensor_tensor(is_bin, count, is_bin, ALU.mult))
                step(v.tensor_reduce(rank[:, :], is_bin.rearrange("p b t -> p t b"), AX.X, ALU.add))
                step(v.tensor_copy(hi_i[:, :], rank[:, :]))
                step(v.tensor_scalar(lo_i[:, :], hi_i[:, :], P - 1, None, ALU.bitwise_and))
                step(v.tensor_scalar(hi_i[:, :], hi_i[:, :], 7, None, ALU.arith_shift_right))
                if turn == 0:
                    step(v.scalar_tensor_tensor(row[:, :], lo_i[:, :], float(ST), hi_i[:, :], ALU.mult, ALU.add))
                    step(v.tensor_copy(held[:, :], bank[1][:, 0:NT]))
                    step(v.tensor_tensor_scan(pads_from[:, :], held[:, :], held[:, :], 0.0, ALU.add, ALU.bypass))
                    step(v.tensor_tensor(pads_from[:, :], held[:, :], pads_from[:, :], ALU.subtract))
                    step(v.tensor_tensor(off[:, :], gend[:, :], grp[:, :], ALU.subtract))
                    step(v.scalar_tensor_tensor(pads_from[:, :], off[:, :], float(GROUP), pads_from[:, :], ALU.mult, ALU.add))
                    dve.wait_ge(sem("s_iota"), 2)
                    step(v.tensor_tensor(pad_in[:, :, :], expand(pad_n[:, :], 2, NT), expand(pads_from[:, :], 1, PADS), ALU.is_ge))
                    step(v.tensor_tensor(pad_in[:, :, :], pad_in[:, :, :], expand(held[:, :], 1, PADS), ALU.mult))
                    step(v.tensor_reduce(pad_f[:, :], pad_in[:, :, :], AX.X, ALU.add))
                    step(v.tensor_tensor(pad_row[:, :], pad_f[:, :], pad_n[:, :], ALU.add))
                    step(v.tensor_scalar(pad_lane[:, :], pad_row[:, :], P - 1, None, ALU.bitwise_and))
                    step(v.tensor_scalar(pad_row[:, :], pad_row[:, :], 7, None, ALU.arith_shift_right))
                    step(v.scalar_tensor_tensor(pad_row[:, :], pad_lane[:, :], float(ST), pad_row[:, :], ALU.mult, ALU.add))
                    dve.wait_ge(sem("s_small"), 3)
                    v.memset(before[:, :], 0.0).then_inc(sem("s_rows"), 1)
                else:
                    step(v.tensor_copy(tile_f[:, :], hi_i[:, :]))
                    step(v.tensor_copy(lane_f[:, :], lo_i[:, :]))
                step(v.tensor_tensor(gcmp, expand(gend[:, :], 1, NG), expand(iota[:, 0:NG], 2, NT), ALU.is_le))
                step(v.tensor_reduce(gsum[:, :], gcmp, AX.X, ALU.add))
                step(v.tensor_scalar(gsum[:, :], gsum[:, :], float(NT - 1), None, ALU.min))
                four = gsum[:, :].rearrange("p (w g) -> p w g", g=4)
                step(v.scalar_tensor_tensor(packed[:, :], four[:, :, 3], float(NT), four[:, :, 2], ALU.mult, ALU.add))
                step(v.scalar_tensor_tensor(packed[:, :], packed[:, :], float(NT), four[:, :, 1], ALU.mult, ALU.add))
                step(v.scalar_tensor_tensor(bin_of[:, :], packed[:, :], float(NT), four[:, :, 0], ALU.mult, ALU.add))

            bins(0, 1, edge_small[:, :, C_LOC], bin_d)
            dve.wait_ge(sem("s_rows"), 1)
            bins(1, 0, loc_f[:, :], bin_s)

            dve.wait_ge(sem("s_vals"), 2)
            v.tensor_scalar(loc_f[:, :], loc_f[:, :], 1.0, None, ALU.add).then_inc(sem("s_loc1"), 1)
            step(v.tensor_tensor(w_lo[:, :], w_in[:, :], w_hi[:, :], ALU.subtract))

            def onehots0(i):
                for j in range(U):
                    t = i * U + j
                    wait(dve, sem("s_placed"), t - 3)
                    lane = lane_f[:, bass.ds(t, 1)]
                    v.tensor_scalar(in_lane[:, j % 4, :], iota[:, 0:P], lane, None, ALU.is_equal).then_inc(sem("s_in_lane"), 1)
                    v.tensor_scalar(of_tile[j % 4][:, :], iota[:, :], tile_f[:, bass.ds(t, 1)], None, ALU.is_equal)
                    for value, of in ((2, w_hi), (3, w_lo))[1 - j % 2:]:
                        ins = v.tensor_scalar(of_lane[j % 4][:, value, :], iota[:, 0:P], lane,
                                              of[:, bass.ds(t, 1)].bitcast(F32), ALU.is_equal, ALU.mult)
                    ins.then_inc(sem("s_onehots"), 1)

            turns(dve, ETURNS, onehots0)
            dve.wait_ge(sem("s_we"), 16 * 5)
            v.tensor_copy(we_hi[:, :], we_f[:, :]).then_inc(sem("s_wsplit"), 1)
            dve.wait_ge(sem("s_wsplit"), 1)
            v.tensor_tensor(we_lo[:, :], we_f[:, :], we_hi[:, :], ALU.subtract).then_inc(sem("s_wsplit"), 1)
            dve.wait_ge(sem("s_placed"), ET)
            step(v.tensor_copy(slots0[:, :, 2], bank[2][:, 0:ST]))
            v.tensor_copy(slots0[:, :, 0], bank[0][:, 0:ST]).then_inc(sem("s_slots0"), 1)
            v.tensor_scalar(slots0[:, :, 1], bank[1][:, 0:ST], -1.0, None, ALU.add).then_inc(sem("s_slots0"), 1)
            v.tensor_tensor(slots0[:, :, 2], slots0[:, :, 2], bank[3][:, 0:ST], ALU.add).then_inc(sem("s_slots0"), 1)
            step(v.memset(acc[:, 0:NT * D], 0.0))

            def bin_registers(table_of, i):
                _, r = nc.values_load_multi_w_load_instructions(
                    table_of[0:1, bass.ds(i * 2, 2)], engines=[mybir.EngineType.DVE], min_val=0, max_val=NT ** 4 - 1)
                return [(r[g // 4] >> (4 * (g % 4))) & (NT - 1) for g in range(8)]

            def sums(L, oh, slot, col, table_of, aside=None):
                def onehot(i, jj):
                    at_t = ahead(i, jj, U, TURNS)
                    if at_t is None:
                        return
                    turn, j, T = at_t
                    h, k = divmod(j, H8)
                    dve.wait_ge(sem(f"L{L}_idx"), turn * 2 + h + 1)
                    wait(dve, sem(f"L{L}_seg"), T - H8 + 1)
                    if L == 0:
                        ins = v.tensor_scalar(oh[:, k, :], iota[:, 0:P], slot[:, h, k, 1:2], slot[:, h, k, 2:3],
                                              ALU.is_equal, ALU.mult)
                    else:
                        ins = v.tensor_scalar(oh[:, k, :], iota[:, 0:P], slot[:, h, k, col:col + 1], None, ALU.is_equal)
                    ins.then_inc(sem(f"L{L}_oh"), 1)

                for T in range(4):
                    onehot(0, T)

                def body(i):
                    regs = bin_registers(table_of, i)
                    for j in range(U):
                        T, k = i * U + j, j % H8
                        onehot(i, j + 4)
                        if aside is not None:
                            aside(i, j)
                        if j % 2:
                            dve.wait_ge(sem(f"L{L}_seg"), T + 1)
                            wait(dve, sem(f"L{L}_acc"), i * 8 + j // 2)
                            at = acc_n[:, bass.ds(regs[j // 2], 1), :]
                            if L == 3:
                                ends = seen[:, bass.ds(regs[j // 2], 1), :]
                                v.tensor_tensor(ends, ends, oh[:, k - 1:k + 1, :].rearrange("p a n -> p (a n)"), ALU.add)
                            v.tensor_tensor(at, at, bank[j // 2 % 4][:, :], ALU.add).then_inc(sem(f"L{L}_acc"), 1)

                turns(dve, TURNS, body)

            sums(0, oh0, slot0, 1, bin_s)
            dve.wait_ge(sem("L0_acc"), NG)

            def moments(L, n, s, z):
                v.bn_stats(stats[:, s, :], z).then_inc(sem("norm_bs"), 1)
                dve.wait_ge(sem("norm_bs"), NORMS[L] + n + 1)
                gate(dve)
                v.bn_aggr(mv[:, s, :], stats[:, s, :]).then_inc(sem("norm_mv"), 1)

            def inverse(L, n, s):
                dve.wait_ge(sem("norm_std"), NORMS[L] + n + 1)
                v.reciprocal(rstd[:, s:s + 1], std[:, s:s + 1]).then_inc(sem("norm_rs"), 1)
                dve.wait_ge(sem("norm_rs"), NORMS[L] + n + 1)
                dve.wait_ge(sem("norm_mv"), NORMS[L] + n + 1)

            def norm(L, n, s, z, out):
                inverse(L, n, s)
                return v.tensor_scalar(out, z, mv[:, s, 0:1], rstd[:, s:s + 1], ALU.subtract, ALU.mult)

            dve.wait_ge(sem("s_x"), 16)
            dve.wait_ge(sem("s_we"), 16 * 5)

            def sum0(i, ss):
                at_n = ahead(i, ss, 2, NT // 2)
                if at_n is None:
                    return
                _, s, n = at_n
                z = dense0[:, s, :]
                v.tensor_tensor(z, acc_n[:, bass.ds(n, 1), :], x_res[:, bass.ds(n, 1), :], ALU.add).then_inc(sem("L0_z"), 1)
                dve.wait_ge(sem("L0_z"), n + 1)
                moments(0, n, s, z)

            sum0(0, 0)

            def nodes0(i):
                for s in range(2):
                    n = i * 2 + s
                    z, x, y = dense0[:, s, :], x_res[:, bass.ds(n, 1), :], dense0[:, 2 + s, :]
                    sum0(i, s + 1)
                    norm(0, n, s, z, x).then_inc(sem("L0_x"), 1)
                    dve.wait_ge(sem("L0_x"), n + 1)
                    wait(dve, sem(f"L0_st{s}"), i * 16)
                    v.tensor_tensor(y, x, be[:, :], ALU.add).then_inc(sem("L0_y"), 1)

            turns(dve, NT // 2, nodes0)

            step(v.tensor_scalar(eps1[:, :], eps1[:, :], 1.0, None, ALU.add))

            def low1(i, hh):
                at_h = ahead(i, hh, 2, TURNS)
                if at_h is None:
                    return
                turn, h, H = at_h
                dve.wait_ge(sem("L1_high"), H + 1)
                wait(dve, sem("L1_tr"), (H - 1) * 2)
                for q in range(2):
                    at = slice(4 * q, 4 * q + 4)
                    v.tensor_tensor(parts[h][:, at, EA:2 * EA], chunk[:, h, at, 0:EA], parts[h][:, at, 0:EA], ALU.subtract)\
                        .then_inc(sem("L1_part"), 1)

            def add1(i, jj):
                at_t = ahead(i, jj, U, TURNS)
                if at_t is None:
                    return
                turn, j, T = at_t
                h, k = divmod(j, H8)
                dve.wait_ge(sem("L1_idx"), turn * 2 + h + 1)
                wait(dve, sem("L1_seg"), T - H8 + 1)
                v.tensor_scalar(oh1_r[k // 4][:, :] if k % 4 == 3 else oh1[:, k, :], iota[:, 0:P], small[:, bass.ds(T, 1), C_LOC], None, ALU.is_equal)\
                    .then_inc(sem("L1_oh"), 1)
                dve.wait_ge(sem("L1_mm"), T + 1)
                dve.wait_ge(sem(f"gath{k}"), G_ALL + turn * 32 + 16 * h + 16)
                wait(dve, sem("L1_seg"), T - 3)
                v.tensor_tensor(msg[j % 4][:, :], bank[j % 4][:, :], gath[k][:, :], ALU.add).then_inc(sem("L1_add"), 1)

            dve.wait_ge(sem("s_az"), 1)
            def rest1(i, jj):
                at_t = ahead(i, jj, U, TURNS)
                if at_t is None or at_t[1] % 4 != 3:
                    return
                T = at_t[2]
                dve.wait_ge(sem("L1_relu"), T + 1)
                wait(dve, sem("L1_seg"), T - 3)
                v.scalar_tensor_tensor(msg_lo[:, :], msg[3][:, :], 0.0, msg_hi[:, :], ALU.max, ALU.subtract)\
                    .then_inc(sem("L1_rest"), 1)

            low1(0, 0)
            low1(0, 1)
            for T in range(3):
                add1(0, T)

            def edges1(i):
                regs = bin_registers(bin_d, i)
                for j in range(U):
                    T = i * U + j
                    if j % H8 == 5:
                        low1(i, j // H8 + 2)
                    add1(i, j + 3)
                    rest1(i, j + 2)
                    if j % 2:
                        dve.wait_ge(sem("L1_seg"), T + 1)
                        wait(dve, sem("L1_acc"), i * 8 + j // 2)
                        at = acc_n[:, bass.ds(regs[j // 2], 1), :]
                        v.tensor_tensor(at, at, bank[4 + j // 2 % 2][:, :], ALU.add).then_inc(sem("L1_acc"), 1)

            turns(dve, TURNS, edges1)

            dve.wait_ge(sem("L1_acc"), NG)

            def own1(i):
                for s in range(2):
                    n = i * 2 + s
                    wait(dve, sem("L1_ntr"), n - 1)
                    v.scalar_tensor_tensor(gath[s][:, :], x_res[:, bass.ds(n, 1), :], eps1[:, 0:1], acc_n[:, bass.ds(n, 1), :],
                                           ALU.mult, ALU.add).then_inc(sem("L1_hs"), 1)

            turns(dve, NT // 2, own1)

            def batch(which, src, nf, evs):
                def body(c):
                    for f in range(nf):
                        dve.wait_ge(sem(evs), c * nf + f + 1)
                        v.bn_stats(bst[:, f, bass.ds(c, 1), :], src[:, f, bass.ds(c * 512, 512)]).then_inc(sem(f"L1_bst{nf}"), 1)

                turns(dve, 4, body)
                dve.wait_ge(sem(f"L1_bst{nf}"), 4 * nf)
                for f in range(nf):
                    ins = v.bn_aggr(bmv[:, f, :], bst[:, f, :, :].rearrange("p c s -> p (c s)"))
                ins.then_inc(sem("L1_bmv"), 1)
                dve.wait_ge(sem("L1_bstd"), which)
                g, be = (g1, be1) if nf == 8 else (g2, be2)
                sc, sh, tm = bscale[:, 0:nf], bshift[:, 0:nf], btmp[:, 0:nf]
                step(v.reciprocal(tm, bstd[:, 0:nf]))
                step(v.tensor_tensor(sc, tm, g, ALU.mult))
                step(v.tensor_tensor(tm, bmv[:, 0:nf, 0], sc, ALU.mult))
                v.tensor_tensor(sh, be, tm, ALU.subtract).then_inc(sem("L1_bn"), 1)

            batch(1, aT, 8, "L1_ev1")
            batch(2, hT, 4, "L1_ev2")

            def back1(i):
                for s in range(2):
                    n = i * 2 + s
                    at = x_res[:, bass.ds(n, 1), :]
                    dve.wait_ge(sem("L1_btr"), n + 1)
                    v.tensor_tensor(at, at, bank[s][:, :], ALU.add).then_inc(sem("L1_z"), 1)
                    dve.wait_ge(sem("L1_z"), n + 1)
                    v.bn_stats(nst[:, bass.ds(n, 1), :], x_res[:, bass.ds(n, 1), :]).then_inc(sem("L1_nst"), 1)

            turns(dve, NT // 2, back1)
            dve.wait_ge(sem("L1_nst"), NT)
            for n in range(NT):
                ins = v.bn_aggr(nmv[:, n, :], nst[:, n, :])
            ins.then_inc(sem("L1_mv"), 1)
            dve.wait_ge(sem("L1_std"), 1)
            step(v.reciprocal(nstd[:, :], nstd[:, :]))

            def norm1(i):
                for s in range(2):
                    n = i * 2 + s
                    wait(dve, sem("L1_utr"), n - 1)
                    v.tensor_scalar(gath[4 + s][:, :], x_res[:, bass.ds(n, 1), :], nmv[:, bass.ds(n, 1), 0:1],
                                    nstd[:, bass.ds(n, 1)], ALU.subtract, ALU.mult).then_inc(sem("L1_xn"), 1)
                    dve.wait_ge(sem("L1_xn"), n + 1)
                    v.tensor_scalar(x_res[:, bass.ds(n, 1), :], x_res[:, bass.ds(n, 1), :], nmv[:, bass.ds(n, 1), 0:1],
                                    nstd[:, bass.ds(n, 1)], ALU.subtract, ALU.mult).then_inc(sem("L1_x"), 1)

            turns(dve, NT // 2, norm1)

            dve.wait_ge(sem("s_az"), 2)
            dve.wait_ge(sem("L1_x"), NT)

            def onehot2(i, jj):
                at_t = ahead(i, jj, U, TURNS)
                if at_t is None:
                    return
                turn, j, T = at_t
                h, k = divmod(j, H8)
                dve.wait_ge(sem("L2_idx"), turn * 2 + h + 1)
                wait(dve, sem("L2_seg"), T - H8 + 1)
                v.tensor_scalar(oh2[:, k, :], iota[:, 0:P], slot2[:, h, k, C_LOC:C_LOC + 1], None, ALU.is_equal)\
                    .then_inc(sem("L2_oh"), 1)

            def products2(i, jj):
                at_t = ahead(i, jj, U, TURNS)
                if at_t is None:
                    return
                turn, j, T = at_t
                h, k = divmod(j, H8)
                w, s, q, t, y = bank[4 + j % 2], gath[k], prod[j % 4], dot[j % 2], slot2[:, h, k, :]
                dve.wait_ge(sem("L2_dot"), T + 1)
                wait(dve, sem("L2_seg"), T - 3)
                v.scalar_tensor_tensor(t[:, :], s[:, 2 * P:3 * P], y[:, C_Y + 2:C_Y + 3], t[:, :], ALU.mult, ALU.add)\
                    .then_inc(sem("L2_t"), 1)
                dve.wait_ge(sem("L2_w"), T + 1)
                v.tensor_tensor(q[:, 0:2, :], w[:, 0:2 * P].rearrange("p (a c) -> p a c", a=2), expand(s[:, 0:P], 1, 2), ALU.mult)
                dve.wait_ge(sem("L2_t"), T * 2 + 1)
                v.scalar_tensor_tensor(t[:, :], s[:, 3 * P:4 * P], y[:, C_Y + 3:C_Y + 4], t[:, :], ALU.mult, ALU.add)\
                    .then_inc(sem("L2_t"), 1)
                v.tensor_tensor(q[:, 2:5, :], expand(w[:, 2 * P:3 * P], 1, 3),
                                s[:, P:4 * P].rearrange("p (m c) -> p m c", m=3), ALU.mult)
                dve.wait_ge(sem("L2_t"), T * 2 + 2)
                v.scalar_tensor_tensor(q[:, 5, :], t[:, :], 3.0 ** -0.5, w[:, 3 * P:4 * P], ALU.mult, ALU.mult)\
                    .then_inc(sem("L2_prod"), 1)

            def low2(i, hh):
                at_h = ahead(i, hh, 2, TURNS)
                if at_h is None:
                    return
                H = at_h[2]
                dve.wait_ge(sem("L2_high"), H + 1)
                v.tensor_tensor(last_lo[:, :], last, last_hi[:, :], ALU.subtract).then_inc(sem("L2_low"), 1)

            dve.wait_ge(sem("s_w4"), 16 * 8)
            v.tensor_copy(we_hi[:, :], m4).then_inc(sem("s_wsplit"), 1)
            dve.wait_ge(sem("s_wsplit"), 3)
            v.tensor_tensor(we_lo[:, :], m4, we_hi[:, :], ALU.subtract).then_inc(sem("s_wsplit"), 1)
            for T in range(5):
                onehot2(0, T)
            low2(0, 0)
            products2(0, 0)
            products2(0, 1)

            def edges2(i):
                regs = bin_registers(bin_d, i)
                for j in range(U):
                    T = i * U + j
                    if j % H8 == 2:
                        low2(i, j // H8 + 1)
                    products2(i, j + 2)
                    if j % 2:
                        b = j // 2 % 2
                        dve.wait_ge(sem("L2_seg"), T + 1)
                        wait(dve, sem("L2_acc"), i * 8 + j // 2)
                        for part in range(2):
                            at = acc2[:, bass.ds(regs[j // 2], 1), D * part:D * part + D]
                            ins = v.tensor_tensor(at, at, bank[2 * part + b][:, :], ALU.add)
                        ins.then_inc(sem("L2_acc"), 1)
                    onehot2(i, j + 5)

            turns(dve, TURNS, edges2)

            def sum2(i, ss):
                at_n = ahead(i, ss, 2, NT // 2)
                if at_n is None:
                    return
                _, s, n = at_n
                z, x = dz[s], x_res[:, bass.ds(n, 1), :].rearrange("p o d -> p (o d)")
                wait(dve, sem("L2_x"), n - 1)
                dve.wait_ge(sem("L2_mm"), n + 1)
                v.scalar_tensor_tensor(z[:, 0:P], bank[4 + s][:, 0:P], C_OUT, x[:, 0:P], ALU.mult, ALU.add)
                v.scalar_tensor_tensor(z[:, P:D].rearrange("p (u m) -> p u m", m=3),
                                       bank[4 + s][:, P:D].rearrange("p (m u) -> p u m", m=3), C_OUT,
                                       x[:, P:D].rearrange("p (u m) -> p u m", m=3), ALU.mult, ALU.add).then_inc(sem("L2_nz"), 1)
                dve.wait_ge(sem("L2_nz"), n + 1)
                moments(2, n, s, z)

            sum2(0, 0)

            def nodes2(i):
                for s in range(2):
                    n = i * 2 + s
                    sum2(i, s + 1)
                    norm(2, n, s, dz[s], x_res[:, bass.ds(n, 1), :]).then_inc(sem("L2_x"), 1)

            turns(dve, NT // 2, nodes2)

            dve.wait_ge(sem("s_az"), 4)
            dve.wait_ge(sem("s_w3"), 64)

            def own3(i, j):
                if j != 15 or isinstance(i, int) and i in (0, TURNS - 1):
                    return
                n = i - 1
                x = x_res[:, bass.ds(n, 1), :]
                dve.wait_ge(sem("L3_own"), n + 1)
                v.tensor_tensor(own[:, bass.ds(n, 1), :], bank[7][:, :], bias3, ALU.add).then_inc(sem("L3_kept"), 1)
                dve.wait_ge(sem("L2_st"), 16 * NT)
                v.tensor_tensor(x, x, beta3, ALU.add).then_inc(sem("L3_kept"), 1)

            sums(3, oh3, slot3, C_LOC, bin_d, own3)
            dve.wait_ge(sem("L3_acc"), NG)
            dve.wait_ge(sem("L3_deg"), 1)
            degree = bank[6][:, 0:NT * 2].rearrange("p (n two) -> p n two", two=2)[:, :, 0]
            step(v.tensor_scalar(rdeg[:, :], degree, 1.0, None, ALU.max))
            step(v.reciprocal(rdeg[:, :], rdeg[:, :]))
            dve.wait_ge(sem("L3_kept"), NT * 2)

            def sum3(i, ss):
                at_n = ahead(i, ss, 2, NT // 2)
                if at_n is None:
                    return
                _, s, n = at_n
                wait(dve, sem("L3_n"), (n - 1) * 2)
                dve.wait_ge(sem("L3_mm"), n + 1)
                v.scalar_tensor_tensor(dz[s], bank[4 + s][:, :], rdeg[:, bass.ds(n, 1)], own[:, bass.ds(n, 1), :],
                                       ALU.mult, ALU.add).then_inc(sem("L3_z"), 1)
                dve.wait_ge(sem("L3_z"), n + 1)
                moments(3, n * 2 - (0 if isinstance(n, int) and n == 0 else 1), s, dz[s])

            def out3(n, s, last):
                wait(dve, sem(f"L3_st{s}"), (n - s) * 8)
                norm(3, n * 2 + (1 if last else 2), 2 + s, gath[s][:, :], dy[s]).then_inc(sem("L3_y"), 1)

            sum3(0, 0)

            def nodes3(i):
                for s in range(2):
                    n = i * 2 + s
                    z, r = dz[s], gath[s][:, :]
                    sum3(i, s + 1)
                    inverse(3, n * 2 - (0 if isinstance(n, int) and n == 0 else 1), s)
                    v.scalar_tensor_tensor(z, z, mv[:, s, 0:1], gamma3, ALU.subtract, ALU.mult).then_inc(sem("L3_n"), 1)
                    dve.wait_ge(sem("L3_n"), n * 2 + 1)
                    v.scalar_tensor_tensor(r, z, rstd[:, s:s + 1], x_res[:, bass.ds(n, 1), :], ALU.mult, ALU.add)\
                        .then_inc(sem("L3_n"), 1)
                    dve.wait_ge(sem("L3_n"), n * 2 + 2)
                    last = isinstance(n, int) and n == NT - 1
                    moments(3, n * 2 + (1 if last else 2), 2 + s, r)
                    if not (isinstance(n, int) and n == 0):
                        out3(n - 1, 1 - s, False)

            turns(dve, NT // 2, nodes3, first=2)
            out3(NT - 1, 1, True)


_INS = ["src", "dst", "x", "edge_attr_4", "edge_attr_64", "edge_attr_8", "edge_weight", "L1_gnn_W_e",
        "L1_gnn_W1", "L1_gnn_W2", "L2_gnn_W_up0", "L2_gnn_W_up1", "L2_gnn_W_mlp1", "L2_gnn_W_mlp2", "L2_gnn_W_mlp3",
        "L2_gnn_W_mlp4", "L2_gnn_W_out0", "L2_gnn_W_out1"]


def kernel(**inputs):
    import numpy as np
    import concourse.bacc as bacc
    from concourse.bass_utils import run_bass_kernel_spmd

    arrays = {name: np.ascontiguousarray(inputs[name]) for name in _INS}
    arrays["w0"] = np.ascontiguousarray(np.asarray(inputs["L0_gnn_weight"]).T)
    arrays["w3"] = np.ascontiguousarray(np.concatenate(
        [np.asarray(inputs["L3_gnn_W_self"]).T, np.asarray(inputs["L3_gnn_W_neigh"]).T]))
    columns = [np.asarray(inputs[f"L1_gnn_{k}"]).reshape(-1, P).T for k in ("b1", "g1", "beta1", "b2", "g2", "beta2")]
    arrays["bn"] = np.ascontiguousarray(np.concatenate(columns, axis=1))
    arrays["eps"] = np.ascontiguousarray(np.broadcast_to(np.asarray(inputs["L1_gnn_eps"]), (P, 1)))
    arrays["be"] = np.ascontiguousarray(np.broadcast_to(np.asarray(inputs["L1_gnn_b_e"]), (P, D)))
    for k in ("bias", "gamma", "beta"):
        arrays[k] = np.ascontiguousarray(np.broadcast_to(np.asarray(inputs[f"L3_gnn_{k}"]), (P, D)))

    nc = bacc.Bacc("TRN2", target_bir_lowering=False, num_devices=1)
    aps = {name: nc.dram_tensor(f"in_{name}", v.shape, mybir.dt.from_np(v.dtype), kind="ExternalInput").ap()
           for name, v in arrays.items()}
    aps["out"] = nc.dram_tensor("out", (N, D), F32, kind="ExternalOutput").ap()
    build(nc, aps)
    r = run_bass_kernel_spmd(nc, [{f"in_{name}": v for name, v in arrays.items()}], core_ids=[0])
    return r.results[0]["out"]
```
